# Optimizing a Trainium2 kernel written in Bass

```python
import numpy as np
import jax
import jax.numpy as jnp

def _softmax(x, axis=-1):
    return jax.nn.softmax(x, axis=axis)

def _gelu(x):
    return jax.nn.gelu(x, approximate=True)

def _silu(x):
    return jax.nn.silu(x)

def _sigmoid(x):
    return jax.nn.sigmoid(x)

def _layernorm(x, axis=-1, eps=1e-05):
    m = jnp.mean(x, axis=axis, keepdims=True)
    v = jnp.var(x, axis=axis, keepdims=True)
    return (x - m) / jnp.sqrt(v + eps)

def _scatter_add(tgt, idx, src, axis=0):
    return tgt.at[idx].add(src)

def _segment_sum(src, seg, n):
    return jax.ops.segment_sum(src, seg, n)
kernel_name = 'mk_lm_tower_d2_tok_ids256_r4_b534eb'

def setup_inputs(seed: int=0):
    np.random.seed(seed)
    _w = jnp.asarray

    def _rec_inputs():
        import jax
        import jax.numpy as jnp
        _rk = jax.random.key(seed)
        x = jax.random.randint(jax.random.fold_in(_rk, 1), (16, 256), 0, 250, jnp.int32)
        itok_BS_0_63 = jax.random.randint(jax.random.fold_in(_rk, 21), (16, 256), 0, 64, jnp.int32)
        return (x, itok_BS_0_63)
    x, itok_BS_0_63 = _rec_inputs()

    def _L0_tok_setup():
        import jax, jax.numpy as jnp
        import numpy as np
        NUM_MOVES = 250
        MOVE_FEAT = 128
        ENTITY_SIZE = 64
        PP_TOKENS = 256
        PP_BINS = 32
        B, T = (64, 1024)

        def _pp_encoding_table():
            rng = PP_TOKENS
            values = np.arange(PP_TOKENS)
            bins = np.arange(PP_BINS)
            arr = (bins[None] < np.floor(PP_BINS * values / rng)[:, None]).astype(np.float64)
            extra = values % (rng / PP_BINS) / (rng / PP_BINS)
            extra = 2 * extra - 1
            extra_mask = (bins[None] <= np.floor(PP_BINS * values / rng)[:, None]) - arr
            arr = arr + extra_mask * extra[:, None]
            arr = np.where(arr <= 0, -1.0, arr)
            return jnp.asarray(arr, dtype=jnp.float32)
        key = jax.random.key(seed)
        k1, k2, k3, k4 = jax.random.split(key, 4)
        tokens = jax.random.randint(k1, (B, T), 0, NUM_MOVES, dtype=jnp.int32)
        pp_used = jax.random.randint(k2, (B, T), 0, 64, dtype=jnp.int32)
        pp_max = jax.random.randint(k3, (B, T), 0, 64, dtype=jnp.int32)
        move_table = jax.random.normal(k4, (NUM_MOVES, MOVE_FEAT), dtype=jnp.float32)
        pp_table = _pp_encoding_table()
        kw, kb = jax.random.split(jax.random.fold_in(key, 7))
        lin_in = MOVE_FEAT + PP_BINS
        W = jax.random.normal(kw, (ENTITY_SIZE, lin_in), dtype=jnp.float32) / np.sqrt(lin_in)
        b = jnp.zeros((ENTITY_SIZE,), dtype=jnp.float32)
        return {'tokens': tokens, 'pp_used': pp_used, 'pp_max': pp_max, 'move_table': move_table, 'pp_table': pp_table, 'W': W, 'b': b}
    _L0_tok_all = _L0_tok_setup()
    _L0_tok_in = {k: v for k, v in _L0_tok_all.items() if k in ('move_table', 'pp_table', 'W', 'b')}
    del _L0_tok_all

    def _L0_attn_setup():
        import jax, jax.numpy as jnp
        import numpy as np
        DIM = 64
        N_SCALES = 4
        PHASES_PER_SCALE = 16
        K_PHASES = N_SCALES * PHASES_PER_SCALE
        B, L = (2, 256)
        key = jax.random.key(seed)
        ks = jax.random.split(key, 16)
        s = 0.02
        d, k = (DIM, K_PHASES)
        return {'x': jax.random.normal(ks[0], (B, L, d), dtype=jnp.float32), 'Wk1': jax.random.normal(ks[1], (d, d), dtype=jnp.float32) * s, 'bk1': jnp.zeros((d,), jnp.float32), 'Wk2': jax.random.normal(ks[2], (d, k), dtype=jnp.float32) * s, 'bk2': jnp.zeros((k,), jnp.float32), 'Wq1': jax.random.normal(ks[3], (d, d), dtype=jnp.float32) * s, 'bq1': jnp.zeros((d,), jnp.float32), 'Wq2': jax.random.normal(ks[4], (d, k), dtype=jnp.float32) * s, 'bq2': jnp.zeros((k,), jnp.float32), 'Wv': jax.random.normal(ks[5], (d, d), dtype=jnp.float32) * s, 'bv': jnp.zeros((d,), jnp.float32), 'ln_w': jnp.ones((d,), jnp.float32), 'ln_b': jnp.zeros((d,), jnp.float32), 'Wo': jax.random.normal(ks[6], (d, d), dtype=jnp.float32) * s, 'bo': jnp.zeros((d,), jnp.float32)}
    _L0_attn_all = _L0_attn_setup()
    _L0_attn_in = {k: v for k, v in _L0_attn_all.items() if k in ('Wk1', 'bk1', 'Wk2', 'bk2', 'Wq1', 'bq1', 'Wq2', 'bq2', 'Wv', 'bv', 'ln_w', 'ln_b', 'Wo', 'bo')}
    del _L0_attn_all

    def _L0_ffn_setup():
        import jax, jax.numpy as jnp
        import numpy as np
        TOP_K = 2
        LN_EPS = 1e-05
        key = jax.random.key(seed)
        ks = jax.random.split(key, 8)
        B, S, D, E, H = (16, 256, 64, 8, 256)
        x = jax.random.normal(ks[0], (B, S, D), dtype=jnp.float32)
        Wr = jax.random.normal(ks[1], (D, E), dtype=jnp.float32) * 0.1
        br = jnp.zeros((E,), dtype=jnp.float32)
        ln_g = jnp.ones((E, D), dtype=jnp.float32)
        ln_b = jnp.zeros((E, D), dtype=jnp.float32)
        W1 = jax.random.normal(ks[2], (E, D, H), dtype=jnp.float32) * (1.0 / np.sqrt(D))
        b1 = jnp.zeros((E, H), dtype=jnp.float32)
        W2 = jax.random.normal(ks[3], (E, H, D), dtype=jnp.float32) * (1.0 / np.sqrt(H))
        b2 = jnp.zeros((E, D), dtype=jnp.float32)
        return {'x': x, 'Wr': Wr, 'br': br, 'ln_g': ln_g, 'ln_b': ln_b, 'W1': W1, 'b1': b1, 'W2': W2, 'b2': b2}
    _L0_ffn_all = _L0_ffn_setup()
    _L0_ffn_in = {k: v for k, v in _L0_ffn_all.items() if k in ('Wr', 'br', 'ln_g', 'ln_b', 'W1', 'b1', 'W2', 'b2')}
    del _L0_ffn_all

    def _L1_attn_setup():
        import jax, jax.numpy as jnp
        import numpy as np
        EMB, HEADS, DEPTH, SEQ, BATCH = (64, 8, 4, 2048, 4)
        DH = EMB // HEADS
        FF = 4 * EMB
        EPS = 1e-05

        def _layernorm(x, g, b):
            mu = x.mean(-1, keepdims=True)
            var = ((x - mu) ** 2).mean(-1, keepdims=True)
            return (x - mu) * jax.lax.rsqrt(var + EPS) * g + b

        def _linear_attn(x, Wq, Wk, Wv, Wo, bo):
            b, n, dm = x.shape
            split = lambda t: t.reshape(b, n, HEADS, DH).transpose(0, 2, 1, 3)
            scale = DH ** (-0.25)
            q = jax.nn.softmax(split(x @ Wq) * scale, axis=-1)
            k = jax.nn.softmax(split(x @ Wk) * scale, axis=-2)
            v = split(x @ Wv)
            context = jnp.einsum('bhnd,bhne->bhde', k, v)
            out = jnp.einsum('bhnd,bhde->bhne', q, context)
            out = out.transpose(0, 2, 1, 3).reshape(b, n, dm)
            return out @ Wo + bo

        def _forward(x, Wq, Wk, Wv, Wo, bo, ln1_g, ln1_b, W1, b1, W2, b2, ln2_g, ln2_b):
            for i in range(DEPTH):
                h = _layernorm(x, ln1_g[i], ln1_b[i])
                x = x + _linear_attn(h, Wq[i], Wk[i], Wv[i], Wo[i], bo[i])
                h = _layernorm(x, ln2_g[i], ln2_b[i])
                x = x + (jax.nn.gelu(h @ W1[i] + b1[i], approximate=False) @ W2[i] + b2[i])
            return x
        key = jax.random.key(seed)
        ks = jax.random.split(key, 8)
        w = lambda k, shape: jax.random.normal(k, shape, dtype=jnp.float32) * 0.02
        D = DEPTH
        return {'x': jax.random.normal(ks[0], (BATCH, SEQ, EMB), dtype=jnp.float32), 'Wq': w(ks[1], (D, EMB, EMB)), 'Wk': w(ks[2], (D, EMB, EMB)), 'Wv': w(ks[3], (D, EMB, EMB)), 'Wo': w(ks[4], (D, EMB, EMB)), 'bo': jnp.zeros((D, EMB), jnp.float32), 'ln1_g': jnp.ones((D, EMB), jnp.float32), 'ln1_b': jnp.zeros((D, EMB), jnp.float32), 'W1': w(ks[5], (D, EMB, FF)), 'b1': jnp.zeros((D, FF), jnp.float32), 'W2': w(ks[6], (D, FF, EMB)), 'b2': jnp.zeros((D, EMB), jnp.float32), 'ln2_g': jnp.ones((D, EMB), jnp.float32), 'ln2_b': jnp.zeros((D, EMB), jnp.float32)}
    _L1_attn_all = _L1_attn_setup()
    _L1_attn_in = {k: v for k, v in _L1_attn_all.items() if k in ('Wq', 'Wk', 'Wv', 'Wo', 'bo', 'ln1_g', 'ln1_b', 'W1', 'b1', 'W2', 'b2', 'ln2_g', 'ln2_b')}
    del _L1_attn_all

    def _L1_ffn_setup():
        import jax, jax.numpy as jnp
        import numpy as np
        B, S, D, H, E, K = (8, 2048, 64, 256, 8, 2)
        key = jax.random.key(seed)
        ks = jax.random.split(key, 7)
        s_in = 1.0 / np.sqrt(D)
        s_hid = 1.0 / np.sqrt(H)
        return {'x': jax.random.normal(ks[0], (B, S, D), dtype=jnp.float32), 'Wg': jax.random.uniform(ks[1], (E, D), jnp.float32, -s_in, s_in), 'bg': jax.random.uniform(ks[2], (E,), jnp.float32, -s_in, s_in), 'W1': jax.random.uniform(ks[3], (E, H, D), jnp.float32, -s_in, s_in), 'b1': jax.random.uniform(ks[4], (E, H), jnp.float32, -s_in, s_in), 'W2': jax.random.uniform(ks[5], (E, D, H), jnp.float32, -s_hid, s_hid), 'b2': jax.random.uniform(ks[6], (E, D), jnp.float32, -s_hid, s_hid)}
    _L1_ffn_all = _L1_ffn_setup()
    _L1_ffn_in = {k: v for k, v in _L1_ffn_all.items() if k in ('Wg', 'bg', 'W1', 'b1', 'W2', 'b2')}
    del _L1_ffn_all
    return {'x': x, 'itok_BS_0_63': itok_BS_0_63, 'L0_tok_move_table': _L0_tok_in['move_table'], 'L0_tok_pp_table': _L0_tok_in['pp_table'], 'L0_tok_W': _L0_tok_in['W'], 'L0_tok_b': _L0_tok_in['b'], 'L0_attn_Wk1': _L0_attn_in['Wk1'], 'L0_attn_bk1': _L0_attn_in['bk1'], 'L0_attn_Wk2': _L0_attn_in['Wk2'], 'L0_attn_bk2': _L0_attn_in['bk2'], 'L0_attn_Wq1': _L0_attn_in['Wq1'], 'L0_attn_bq1': _L0_attn_in['bq1'], 'L0_attn_Wq2': _L0_attn_in['Wq2'], 'L0_attn_bq2': _L0_attn_in['bq2'], 'L0_attn_Wv': _L0_attn_in['Wv'], 'L0_attn_bv': _L0_attn_in['bv'], 'L0_attn_ln_w': _L0_attn_in['ln_w'], 'L0_attn_ln_b': _L0_attn_in['ln_b'], 'L0_attn_Wo': _L0_attn_in['Wo'], 'L0_attn_bo': _L0_attn_in['bo'], 'L0_ffn_Wr': _L0_ffn_in['Wr'], 'L0_ffn_br': _L0_ffn_in['br'], 'L0_ffn_ln_g': _L0_ffn_in['ln_g'], 'L0_ffn_ln_b': _L0_ffn_in['ln_b'], 'L0_ffn_W1': _L0_ffn_in['W1'], 'L0_ffn_b1': _L0_ffn_in['b1'], 'L0_ffn_W2': _L0_ffn_in['W2'], 'L0_ffn_b2': _L0_ffn_in['b2'], 'L1_attn_Wq': _L1_attn_in['Wq'], 'L1_attn_Wk': _L1_attn_in['Wk'], 'L1_attn_Wv': _L1_attn_in['Wv'], 'L1_attn_Wo': _L1_attn_in['Wo'], 'L1_attn_bo': _L1_attn_in['bo'], 'L1_attn_ln1_g': _L1_attn_in['ln1_g'], 'L1_attn_ln1_b': _L1_attn_in['ln1_b'], 'L1_attn_W1': _L1_attn_in['W1'], 'L1_attn_b1': _L1_attn_in['b1'], 'L1_attn_W2': _L1_attn_in['W2'], 'L1_attn_b2': _L1_attn_in['b2'], 'L1_attn_ln2_g': _L1_attn_in['ln2_g'], 'L1_attn_ln2_b': _L1_attn_in['ln2_b'], 'L1_ffn_Wg': _L1_ffn_in['Wg'], 'L1_ffn_bg': _L1_ffn_in['bg'], 'L1_ffn_W1': _L1_ffn_in['W1'], 'L1_ffn_b1': _L1_ffn_in['b1'], 'L1_ffn_W2': _L1_ffn_in['W2'], 'L1_ffn_b2': _L1_ffn_in['b2']}

def reference(x, itok_BS_0_63, L0_tok_move_table, L0_tok_pp_table, L0_tok_W, L0_tok_b, L0_attn_Wk1, L0_attn_bk1, L0_attn_Wk2, L0_attn_bk2, L0_attn_Wq1, L0_attn_bq1, L0_attn_Wq2, L0_attn_bq2, L0_attn_Wv, L0_attn_bv, L0_attn_ln_w, L0_attn_ln_b, L0_attn_Wo, L0_attn_bo, L0_ffn_Wr, L0_ffn_br, L0_ffn_ln_g, L0_ffn_ln_b, L0_ffn_W1, L0_ffn_b1, L0_ffn_W2, L0_ffn_b2, L1_attn_Wq, L1_attn_Wk, L1_attn_Wv, L1_attn_Wo, L1_attn_bo, L1_attn_ln1_g, L1_attn_ln1_b, L1_attn_W1, L1_attn_b1, L1_attn_W2, L1_attn_b2, L1_attn_ln2_g, L1_attn_ln2_b, L1_ffn_Wg, L1_ffn_bg, L1_ffn_W1, L1_ffn_b1, L1_ffn_W2, L1_ffn_b2):
    import jax
    import jax.numpy as jnp

    def _L0_tok_ref(tokens, pp_used, pp_max, move_table, pp_table, W, b):
        import jax, jax.numpy as jnp
        import numpy as np
        NUM_MOVES = 250
        MOVE_FEAT = 128
        ENTITY_SIZE = 64
        PP_TOKENS = 256
        PP_BINS = 32
        B, T = (64, 1024)

        def _pp_encoding_table():
            rng = PP_TOKENS
            values = np.arange(PP_TOKENS)
            bins = np.arange(PP_BINS)
            arr = (bins[None] < np.floor(PP_BINS * values / rng)[:, None]).astype(np.float64)
            extra = values % (rng / PP_BINS) / (rng / PP_BINS)
            extra = 2 * extra - 1
            extra_mask = (bins[None] <= np.floor(PP_BINS * values / rng)[:, None]) - arr
            arr = arr + extra_mask * extra[:, None]
            arr = np.where(arr <= 0, -1.0, arr)
            return jnp.asarray(arr, dtype=jnp.float32)
        pp_max_f = jnp.maximum(pp_max, 1).astype(jnp.float32)
        ratio = jnp.minimum(pp_used.astype(jnp.float32) / pp_max_f, 1.0)
        pp_ratio_token = jnp.floor(31.0 * (1.0 - ratio)).astype(jnp.int32)
        enc = jax.nn.relu(move_table[tokens])
        pp_enc = pp_table[pp_ratio_token]
        x = jnp.concatenate((enc, pp_enc), axis=-1)
        return jnp.einsum('btf,ef->bte', x, W) + b

    def _L0_attn_ref(x, Wk1, bk1, Wk2, bk2, Wq1, bq1, Wq2, bq2, Wv, bv, ln_w, ln_b, Wo, bo):
        import jax, jax.numpy as jnp
        import numpy as np
        DIM = 64
        N_SCALES = 4
        PHASES_PER_SCALE = 16
        K_PHASES = N_SCALES * PHASES_PER_SCALE
        B, L = (2, 256)
        Bb, Ll, D = x.shape
        K = K_PHASES
        freq = jnp.repeat(2.0 ** jnp.arange(N_SCALES, dtype=jnp.float32), PHASES_PER_SCALE)

        def encode(W1, b1, W2, b2):
            h = jax.nn.gelu(x @ W1 + b1, approximate=False)
            return jnp.tanh(h @ W2 + b2)
        key_phase = encode(Wk1, bk1, Wk2, bk2) * freq * jnp.pi
        query_phase = encode(Wq1, bq1, Wq2, bq2) * freq * jnp.pi
        key_phasor = jnp.cos(key_phase) + 1j * jnp.sin(key_phase)
        query_conj = jnp.cos(query_phase) - 1j * jnp.sin(query_phase)
        V = (x @ Wv + bv).astype(jnp.complex64)
        bound = key_phasor[..., None] * V[:, :, None, :]
        memory = jnp.cumsum(bound, axis=1)
        retrieved = jnp.real(jnp.sum(memory * query_conj[..., None], axis=2))
        positions = jnp.arange(1, Ll + 1, dtype=jnp.float32)
        retrieved = retrieved / jnp.sqrt(positions * K)[None, :, None]
        mu = jnp.mean(retrieved, axis=-1, keepdims=True)
        var = jnp.var(retrieved, axis=-1, keepdims=True)
        normed = (retrieved - mu) / jnp.sqrt(var + 1e-05) * ln_w + ln_b
        return x + normed @ Wo + bo

    def _L0_ffn_ref(x, Wr, br, ln_g, ln_b, W1, b1, W2, b2):
        import jax, jax.numpy as jnp
        import numpy as np
        TOP_K = 2
        LN_EPS = 1e-05
        B, S, D = x.shape
        N = B * S
        xt = x.reshape(N, D)
        logits = xt @ Wr + br
        probs = jax.nn.softmax(logits, axis=-1)
        top_p, top_idx = jax.lax.top_k(probs, TOP_K)
        weights = top_p / top_p.sum(axis=-1, keepdims=True)
        mu = xt.mean(axis=-1, keepdims=True)
        var = ((xt - mu) ** 2).mean(axis=-1, keepdims=True)
        xn = (xt - mu) * jax.lax.rsqrt(var + LN_EPS)
        xe = xn[None, :, :] * ln_g[:, None, :] + ln_b[:, None, :]
        h = jax.nn.gelu(jnp.einsum('end,edh->enh', xe, W1) + b1[:, None, :], approximate=False)
        y = jnp.einsum('enh,ehd->end', h, W2) + b2[:, None, :]
        y_tok = jnp.transpose(y, (1, 0, 2))
        sel = jnp.take_along_axis(y_tok, top_idx[:, :, None], axis=1)
        out = (weights[:, :, None] * sel).sum(axis=1)
        return out.reshape(B, S, D)

    def _L1_attn_ref(x, Wq, Wk, Wv, Wo, bo, ln1_g, ln1_b, W1, b1, W2, b2, ln2_g, ln2_b):
        import jax, jax.numpy as jnp
        import numpy as np
        EMB, HEADS, DEPTH, SEQ, BATCH = (64, 8, 4, 2048, 4)
        DH = EMB // HEADS
        FF = 4 * EMB
        EPS = 1e-05

        def _layernorm(x, g, b):
            mu = x.mean(-1, keepdims=True)
            var = ((x - mu) ** 2).mean(-1, keepdims=True)
            return (x - mu) * jax.lax.rsqrt(var + EPS) * g + b

        def _linear_attn(x, Wq, Wk, Wv, Wo, bo):
            b, n, dm = x.shape
            split = lambda t: t.reshape(b, n, HEADS, DH).transpose(0, 2, 1, 3)
            scale = DH ** (-0.25)
            q = jax.nn.softmax(split(x @ Wq) * scale, axis=-1)
            k = jax.nn.softmax(split(x @ Wk) * scale, axis=-2)
            v = split(x @ Wv)
            context = jnp.einsum('bhnd,bhne->bhde', k, v)
            out = jnp.einsum('bhnd,bhde->bhne', q, context)
            out = out.transpose(0, 2, 1, 3).reshape(b, n, dm)
            return out @ Wo + bo

        def _forward(x, Wq, Wk, Wv, Wo, bo, ln1_g, ln1_b, W1, b1, W2, b2, ln2_g, ln2_b):
            for i in range(DEPTH):
                h = _layernorm(x, ln1_g[i], ln1_b[i])
                x = x + _linear_attn(h, Wq[i], Wk[i], Wv[i], Wo[i], bo[i])
                h = _layernorm(x, ln2_g[i], ln2_b[i])
                x = x + (jax.nn.gelu(h @ W1[i] + b1[i], approximate=False) @ W2[i] + b2[i])
            return x
        return _forward(x, Wq, Wk, Wv, Wo, bo, ln1_g, ln1_b, W1, b1, W2, b2, ln2_g, ln2_b)

    def _L1_ffn_ref(x, Wg, bg, W1, b1, W2, b2):
        import jax, jax.numpy as jnp
        import numpy as np
        B, S, D, H, E, K = (8, 2048, 64, 256, 8, 2)
        gate_scores = jnp.einsum('bsd,ed->bse', x, Wg) + bg
        topk_scores, topk_idx = jax.lax.top_k(gate_scores, K)
        topk_probs = jax.nn.softmax(topk_scores, axis=-1)
        combine = jnp.sum(topk_probs[..., None] * jax.nn.one_hot(topk_idx, E, dtype=x.dtype), axis=-2)
        out = jnp.zeros_like(x)
        for e in range(E):
            h = jax.nn.relu(jnp.einsum('bsd,hd->bsh', x, W1[e]) + b1[e])
            y = jnp.einsum('bsh,dh->bsd', h, W2[e]) + b2[e]
            out = out + combine[..., e:e + 1] * y
        return out
    h = _L0_tok_ref(x, itok_BS_0_63, itok_BS_0_63, L0_tok_move_table, L0_tok_pp_table, L0_tok_W, L0_tok_b)
    h = h + _L0_attn_ref(_layernorm(h, axis=-1), L0_attn_Wk1, L0_attn_bk1, L0_attn_Wk2, L0_attn_bk2, L0_attn_Wq1, L0_attn_bq1, L0_attn_Wq2, L0_attn_bq2, L0_attn_Wv, L0_attn_bv, L0_attn_ln_w, L0_attn_ln_b, L0_attn_Wo, L0_attn_bo)
    h = h + _L0_ffn_ref(_layernorm(h, axis=-1), L0_ffn_Wr, L0_ffn_br, L0_ffn_ln_g, L0_ffn_ln_b, L0_ffn_W1, L0_ffn_b1, L0_ffn_W2, L0_ffn_b2)
    h = h + _L1_attn_ref(_layernorm(h, axis=-1), L1_attn_Wq, L1_attn_Wk, L1_attn_Wv, L1_attn_Wo, L1_attn_bo, L1_attn_ln1_g, L1_attn_ln1_b, L1_attn_W1, L1_attn_b1, L1_attn_W2, L1_attn_b2, L1_attn_ln2_g, L1_attn_ln2_b)
    h = h + _L1_ffn_ref(_layernorm(h, axis=-1), L1_ffn_Wg, L1_ffn_bg, L1_ffn_W1, L1_ffn_b1, L1_ffn_W2, L1_ffn_b2)
    return h

_drawn_inputs = setup_inputs


def setup_inputs(seed=0):
    import zlib

    import numpy as np

    out = dict(_drawn_inputs(seed))
    spreads = {'L0_tok_b': (0.0, 0.1),
     'L0_attn_bk1': (0.0, 0.8),
     'L0_attn_bk2': (0.0, 0.8),
     'L0_attn_bq1': (0.0, 0.8),
     'L0_attn_bq2': (0.0, 0.8),
     'L0_attn_bv': (0.0, 0.1),
     'L0_attn_ln_w': (1.0, 0.6),
     'L0_attn_ln_b': (0.0, 0.472),
     'L0_attn_bo': (0.0, 0.1),
     'L0_ffn_br': (0.0, 0.1),
     'L0_ffn_ln_g': (1.0, 0.2),
     'L0_ffn_ln_b': (0.0, 0.318),
     'L0_ffn_b1': (0.0, 0.31),
     'L0_ffn_b2': (0.0, 0.1),
     'L1_attn_bo': (0.0, 0.1),
     'L1_attn_ln1_g': (1.0, 0.6),
     'L1_attn_ln1_b': (0.0, 0.8),
     'L1_attn_b1': (0.0, 0.55),
     'L1_attn_b2': (0.0, 0.1),
     'L1_attn_ln2_g': (1.0, 0.6),
     'L1_attn_ln2_b': (0.0, 0.8)}
    factors = {'L0_attn_Wk1': 8.0,
     'L0_attn_Wk2': 8.0,
     'L0_attn_Wq1': 8.0,
     'L0_attn_Wq2': 8.0,
     'L1_attn_Wq': 34.084,
     'L1_attn_Wk': 26.23,
     'L1_attn_Wv': 3.353,
     'L1_attn_Wo': 3.33,
     'L1_attn_W1': 3.061,
     'L1_ffn_bg': 3.557,
     'L1_ffn_b1': 7.825,
     'L1_ffn_b2': 6.255}
    for name, (base, spread) in spreads.items():
        noise = np.random.default_rng([zlib.crc32(name.encode()), seed]).standard_normal(out[name].shape)
        drawn = base * np.exp(spread * noise) if base else spread * noise
        out[name] = jnp.asarray(drawn.astype(out[name].dtype))
    for name, factor in factors.items():
        out[name] = (out[name] * factor).astype(out[name].dtype)
    return out
```

```python
from contextlib import ExitStack

import concourse.bass as bass
from concourse import mybir

ALU = mybir.AluOpType
ACT = mybir.ActivationFunctionType
F32 = mybir.dt.float32
BF16 = mybir.dt.bfloat16
I32 = mybir.dt.int32
AX_X = mybir.AxisListType.X

P = 128
D = 64
S = 256
B = 16
G = 4
U = 2
GC = 512
UC = 1024
UT = 16
E = 8
HID = 256
LAYERS = 4
HEADS = 8
DH = 8
EPS = 1e-5
PHASES = 64
MAGIC = 0x5F3759DF
ROUND = float(3 * 2 ** 22)
TWO_PI = 6.283185
NEWTON = 3



class PsumPlan:

    def __init__(self):
        self.count = [0] * 8
        self.at = {}
        self.body = None

    def add(self, key, bank):
        if self.body is None:
            self.at[key] = (bank, self.count[bank], 0)
            self.count[bank] += 1
        else:
            self.body.append((key, bank))

    def loop(self):
        self.body = []

    def end(self, trips):
        per = [sum(b == bank for _, b in self.body) for bank in range(8)]
        seen = list(self.count)
        for key, bank in self.body:
            self.at[key] = (bank, seen[bank], per[bank])
            seen[bank] += 1
        self.count = [c + trips * p for c, p in zip(self.count, per)]
        self.body = None


def plan_psum():
    plan = PsumPlan()
    for n in range(3):
        plan.add(("table", n), 2 + n)
    for g in range(G):
        plan.add(("embed", g), g % 2)

    def transposes(t, groups=range(G)):
        for g in groups:
            plan.add(("xt", t, g), 6 + g % 2)

    transposes(0)
    for g in range(G):
        for h in range(2):
            plan.add(("enc1", g, h), h)
        for kind in range(2):
            for h in range(2):
                plan.add(("enc2", g, kind, h), 2 + 2 * kind + h)
    for g in range(G):
        plan.add(("v0", g), g % 2)
        for h in range(2):
            for jb in range(2):
                plan.add(("score", g, h, jb), 2 + 2 * h + jb)
        plan.add(("ret", g), 6 + g % 2)
    transposes(1)
    for g in range(G):
        plan.add(("o0", g), g % 2)

    def moe(m):
        transposes(2 if m == 0 else 12)
        for g in range(G):
            plan.add(("gate", m, g), 4 + g % 2)
        if m == 0:
            transposes(3)
        plan.loop()
        for s in range(2):
            for g in range(G):
                for hc in range(2):
                    for h in range(2):
                        plan.add(("up", m, s, g, hc, h), 2 * hc + h)
                plan.add(("down", m, s, g), 4 + g % 2)
        plan.end(E // 2)

    moe(0)
    plan.loop()
    transposes("attn")
    for g in range(G):
        plan.add(("q", g), g % 2)
        plan.add(("k", g), 2 + g % 2)
    for what, g in (("v", 0), ("v", 1), ("v", 2), ("qt", 0), ("v", 3), ("qt", 1), ("qt", 2), ("qt", 3)):
        plan.add((what, g), 4)
    for g in range(G):
        plan.add(("kt", g), 5)
        plan.add(("ctx", g), 6)
        plan.add(("m", g), 6)
        plan.add(("o", g), 7)
    transposes("ffn")
    for g in range(G):
        for hc in range(2):
            for h in range(2):
                plan.add(("fup", g, hc, h), 2 * hc + h)
        plan.add(("fdown", g), 4 + g % 2)
    plan.end(LAYERS)
    moe(1)
    return plan.at


class Chain:

    def __init__(self, eng, sem):
        self.eng, self.sem, self.n, self.i, self.per = eng, sem, 0, None, 0

    def __call__(self, ins):
        ins.then_inc(self.sem, 1)
        self.n += 1
        return ins

    def settle(self):
        self.eng.wait_ge(self.sem, self.n if self.i is None else self.n + self.i * self.per)

    def enter(self, i, per):
        self.i, self.per, self.start = i, per, self.n

    def leave(self, trips):
        assert self.n - self.start == self.per, (self.n - self.start, self.per)
        self.n = self.start + trips * self.per
        self.i = None


def lm_tower(nc, a, out):
    use = plan_psum()
    ctx = ExitStack()
    with ctx:
        def sb(name, shape, dt=F32):
            return ctx.enter_context(nc.sbuf_tensor(name, shape, dt))

        def sem(name):
            return ctx.enter_context(nc.semaphore(name))

        ctx.enter_context(nc.allow_non_contiguous_dma("small vectors and weights, once"))

        bank = [ctx.enter_context(nc.psum_tensor(f"bank{b}", [P, GC], F32)) for b in range(8)]
        Hs = sb("Hs", [P, G * GC])
        Xs = sb("Xs", [P, G * GC])
        Xn = sb("Xn", [P, G * GC])
        Cen = sb("Cen", [P, G * GC])
        Sq = sb("Sq", [P, G * GC])
        XT = sb("XT", [P, G * GC])
        stat = sb("stat", [P, U, 6, UT])
        Ph = sb("Ph", [P, G, 4 * GC])
        tok_i = Ph[:, 0:2, :].rearrange("p a b -> p (a b)").bitcast(I32)
        pp_i = Ph[:, 2:4, :].rearrange("p a b -> p (a b)").bitcast(I32)
        onehot = sb("onehot", [P, 2, 3, UC], BF16)
        ppstep = sb("ppstep", [16, 2, UC])
        Gk = sb("Gk", [P, 2, 2, GC])
        Turn = sb("Turn", [P, 4 * GC])
        Sc = sb("Sc", [P, 2, 4, 384])
        Vt = sb("Vt", [P, G, GC])
        Hd = sb("Hd", [P, 2, 2, 2, GC])
        Xe = Ph[:, 3, 0:UC].rearrange("p (n c) -> p n c", n=2)
        Tmp = sb("Tmp", [P, GC])
        Wgt = sb("Wgt", [P, GC])
        Qe = Ph[:, 0, :].rearrange("p (n c) -> p n c", n=G)
        Ke = Ph[:, 1, :].rearrange("p (n c) -> p n c", n=G)
        Kt = Ph[:, 2, 0:UC].rearrange("p (n c) -> p n c", n=2)
        Qf = Ph[:, 2, UC:2 * UC].rearrange("p (n c) -> p n c", n=2)
        Cm = sb("Cm", [P, 2, 2, P])
        Mm = sb("Mm", [P, 2, 2, P])
        small = sb("small", [P, G, 3, D])
        ksm = sb("ksm", [P, G, 4, 2])
        route = sb("route", [P, 8, UT * E])
        rt = sb("rt", [P, 8, UT])
        comb = sb("comb", [P, G, E, E])
        ident = sb("ident", [P, P])
        headmask = sb("headmask", [P, P])
        causal = sb("causal", [P, 384])
        iota_i = sb("iota_i", [P, 1], I32)
        iota_f = sb("iota_f", [P, 4])
        epos_i = sb("epos_i", [P, UT], I32)
        epos = sb("epos", [P, UT])
        prio_i = sb("prio_i", [P, UT * E], I32)
        prio = sb("prio", [P, UT * E])
        turn = sb("turn", [P, 8])
        mtT = sb("mtT", [P, 250])
        tokW = sb("tokW", [P, D])
        ppW = sb("ppW", [32, D])
        ppT = sb("ppT", [32, S])
        ppR = sb("ppR", [32, 10])
        tokb = sb("tokb", [16, D])
        tf = sb("tf", [P, 3, D])
        tabs = sb("tabs", [P, 3, 3, D], BF16)
        w_enc1 = sb("w_enc1", [P, P])
        w_enc2 = sb("w_enc2", [P, P])
        bd0 = sb("bd0", [P, 2, P])
        v_b1 = sb("v_b1", [P, 1])
        v_b2 = sb("v_b2", [P, 2])
        v_ln0 = sb("v_ln0", [P, 2])
        rows0 = sb("rows0", [P, 2, D])
        bdg = sb("bdg", [P, 2, 2 * E])
        rowg = sb("rowg", [P, 2, E])
        rowb2 = sb("rowb2", [P, 2, E, D])
        PK = 256 + 128 + 4
        pack = sb("pack", [P, 2, PK])
        bd1 = sb("bd1", [P, 4, P])
        ff = sb("ff", [P, 256 + 128])
        lvecs = sb("lvecs", [P, LAYERS, 6])
        lvec = sb("lvec", [P, 6])
        lrow = sb("lrow", [P, 2, D])
        rows1 = sb("rows1", [P, LAYERS, 2, D])

        psum_full = [sem(f"psum_full{b}") for b in range(8)]
        psum_free = [sem(f"psum_free{b}") for b in range(8)]
        tok_in = [sem(f"tok_in{g}") for g in range(G)]
        tab_in, enc_in, vec_in, l1_in = sem("tab_in"), sem("enc_in"), sem("vec_in"), sem("l1_in")
        attn_w_in, ff_w_in = sem("attn_w_in"), sem("ff_w_in")
        pack_in = [[sem(f"pack_in{m}{s}") for s in range(2)] for m in range(2)]
        out_done = sem("out_done")
        zeros_ready, consts_ready, ident_ready = sem("zeros_ready"), sem("consts_ready"), sem("ident_ready")
        pool_step, dve_step, act_step = sem("pool_step"), sem("dve_step"), sem("act_step")
        tables_ready, onehot_ready = sem("tables_ready"), sem("onehot_ready")
        tab_lhs_ready = sem("tab_lhs_ready")
        cen_ready, sq_ready, xn_ready = sem("cen_ready"), sem("sq_ready"), sem("xn_ready")
        frac_ready, cs_ready, hx_ready = sem("frac_ready"), sem("cs_ready"), sem("hx_ready")
        gap_ready, tanh_ready = sem("gap_ready"), sem("tanh_ready")
        xe_ready = sem("xe_ready")
        acc_done = sem("acc_done")
        bias_added = sem("bias_added")
        negm_ready = sem("negm_ready")
        qe_ready, qn_ready = sem("qe_ready"), sem("qn_ready")

        block = ctx.enter_context(nc.Block())

        def full(eng, key, i=0):
            b, n, per = use[key]
            eng.wait_ge(psum_full[b], n + 1 + i * per if per else n + 1)

        def bank_free(key, i=0):
            b, n, per = use[key]
            if n or per:
                nc.tensor.wait_ge(psum_free[b], n + i * per if per else n)
            return bank[b]

        def made(ins, key):
            ins.then_inc(psum_full[use[key][0]], 1)

        def read(ins, key):
            ins.then_inc(psum_free[use[key][0]], 1)

        def ps(key):
            return bank[use[key][0]]

        def ln_no(k, u):
            return 2 * k + u + 1

        def gsl(t, g):
            return t[:, g * GC:(g + 1) * GC]

        def usl(t, u):
            return t[:, u * UC:(u + 1) * UC].rearrange("p (t d) -> p t d", d=D)

        def tiles(t, g):
            return gsl(t, g).rearrange("p (t d) -> p t d", d=D)

        def row(ap, n=E):
            return ap.unsqueeze(1).broadcast_to([P, n, D])

        def wide(ap, n, d=D):
            return ap.unsqueeze(2).broadcast_to([P, n, d])

        @block.sync
        def _(sp):
            sp.dma_start(mtT[:, :], a["move_tableT"]).then_inc(tab_in, 16)
            sp.dma_start(tokW[:, :], a["tok_WT"][0:P, :]).then_inc(tab_in, 16)
            sp.dma_start(ppW[:, :], a["tok_WT"][P:P + 32, :]).then_inc(tab_in, 16)
            sp.dma_start(ppT[:, :], a["pp_tableT"]).then_inc(tab_in, 16)
            sp.dma_start(tokb[0:10, :], a["tok_b"].partition_broadcast(10)).then_inc(tab_in, 16)
            for g in range(G):
                sl = slice(g * UC, (g + 1) * UC)
                sp.dma_start(tok_i[:, sl], a["x"][sl].partition_broadcast(P)).then_inc(tok_in[g], 16)
                sp.dma_start(pp_i[0:10, sl], a["itok"][sl].partition_broadcast(10)).then_inc(tok_in[g], 16)
            def packs(m):
                for s in range(2):
                    if m == 1:
                        full(sp, ("down", 0, s, G - 1), E // 2 - 1)
                    w = PK if m == 0 else PK - 2
                    sp.dma_start(pack[:, s, 0:w], a[f"pack{m}"][s]).then_inc(pack_in[m][s], 16)
                with sp.Fori(0, E // 2 - 1) as i:
                    for s in range(2):
                        full(sp, ("down", m, s, G - 1), i)
                        src = a[f"pack{m}"][bass.ds(2 * i + 2 + s, 1)].rearrange("e p c -> (e p) c")
                        sp.dma_start(pack[:, s, 0:w], src).then_inc(pack_in[m][s], 16)

            def ff_weights(src_ff, src_w2):
                for h in range(2):
                    sp.dma_start(ff[h * D:(h + 1) * D, 0:HID], src_ff).then_inc(ff_w_in, 16)
                sp.dma_start(ff[:, HID:HID + P].rearrange("p (c d) -> p c d", c=2),
                             src_w2.rearrange("(c p) d -> p c d", c=2)).then_inc(ff_w_in, 16)

            def attn_weights(src):
                for h in range(2):
                    sp.dma_start(bd1[h * D:(h + 1) * D, :, h * D:(h + 1) * D], src).then_inc(attn_w_in, 16)

            packs(0)
            attn_weights(a["l1_attn"][0].rearrange("d (w n) -> d w n", w=4))
            ff_weights(a["l1_W1"][0], a["l1_W2"][0])
            with sp.Fori(0, LAYERS - 1) as i:
                full(sp, ("m", G - 1), i)
                attn_weights(a["l1_attn"][bass.ds(i + 1, 1)].rearrange("l d (w n) -> (l d) w n", w=4))
                full(sp, ("fdown", G - 1), i)
                ff_weights(a["l1_W1"][bass.ds(i + 1, 1)].rearrange("l d n -> (l d) n"),
                           a["l1_W2"][bass.ds(i + 1, 1)].rearrange("l d n -> (l d) n"))
            packs(1)
            for g in range(G):
                sp.wait_ge(acc_done, 2 * E * G - G + g + 1)
                for h in range(2):
                    for jb in range(2):
                        dst = out[4 * g + 2 * h + jb].rearrange("(j p) d -> p j d", p=P)
                        src = gsl(Hs, g).rearrange("p (b j k d) -> p b j k d", b=2, j=2, k=2)[:, jb, :, h, :]
                        sp.dma_start(dst, src).then_inc(out_done, 16)
            sp.wait_ge(out_done, 16 * B)

        @block.gpsimd
        def _(pool):
            step = Chain(pool, pool_step)
            gp = nc.gpsimd
            gp.memset(bd0[:, :, :], 0.0)
            gp.memset(bdg[:, :, :], 0.0)
            gp.memset(bd1[:, :, :], 0.0).then_inc(zeros_ready, 1)
            step(gp.iota(iota_i[:, :], [[0, 1]], base=0, channel_multiplier=1))
            step(gp.iota(epos_i[:, :], [[0, 4], [P, 2], [0, 2]], base=1, channel_multiplier=1))
            step(gp.iota(prio_i[:, :], [[0, UT], [-1, E]], base=E, channel_multiplier=0))
            step(gp.memset(ident[:, :], 0.0))
            step(gp.memset(headmask[:, :], 1.0))
            step(gp.memset(causal[:, :], 1.0))
            step.settle()
            gp.affine_select(out=ident[:, :], in_=ident[:, :], compare_op=ALU.not_equal, fill=1.0, base=0,
                             pattern=[[-1, P]], channel_multiplier=1).then_inc(ident_ready, 1)
            hm = headmask[:, :].rearrange("p (b c) -> p b c", c=DH)
            step(gp.affine_select(out=hm, in_=hm, compare_op=ALU.is_ge, fill=0.0, base=0,
                                  pattern=[[-DH, P // DH], [0, DH]], channel_multiplier=1))
            step.settle()
            step(gp.affine_select(out=hm, in_=hm, compare_op=ALU.is_ge, fill=0.0, base=DH - 1,
                                  pattern=[[DH, P // DH], [0, DH]], channel_multiplier=-1))
            for c in (0, 2):
                tri = causal[:, c * P:(c + 1) * P]
                step(gp.affine_select(out=tri, in_=tri, compare_op=ALU.is_ge, fill=0.0, base=0,
                                      pattern=[[1, P]], channel_multiplier=-1))
            step(gp.tensor_copy(iota_f[:, 0:1], iota_i[:, :]))
            step(gp.tensor_copy(epos[:, :], epos_i[:, :]))
            gp.tensor_copy(prio[:, :], prio_i[:, :]).then_inc(consts_ready, 1)

            pool.wait_ge(vec_in, VEC_DMAS * 16)
            for u in range(U):
                pool.wait_ge(xn_ready, ln_no(0, u))
                step(gp.tensor_tensor(usl(Hs, u), usl(Hs, u), usl(Xs, u), ALU.add))
                step.settle()
                gp.tensor_tensor(usl(Hs, u), usl(Hs, u), row(rows0[:, 1, :], UT), ALU.add).then_inc(hx_ready, 1)

            pool.wait_ge(l1_in, L1_DMAS * 16)
            with pool.Fori(0, LAYERS) as i:
                step.enter(i, 1)
                step(gp.tensor_copy(lrow[:, :, :].rearrange("p w d -> p (w d)"),
                                    rows1[:, bass.ds(i, 1), :, :].rearrange("p l w d -> p (l w d)")))
                step.settle()
                step.leave(LAYERS)
                for w in range(2):
                    for u in range(U):
                        pool.wait_ge(cen_ready, ln_no(5 + w, u) + 4 * i)
                        gp.tensor_tensor(usl(Xs, u), usl(Xs, u), row(lrow[:, w, :], UT), ALU.add).then_inc(bias_added, 1)
                pool.wait_ge(bias_added, 4 * i + 4)

        @block.scalar
        def _(act):
            ac = nc.scalar
            step = Chain(act, act_step)

            act.wait_ge(zeros_ready, 1)
            for h in range(2):
                hs = slice(h * D, (h + 1) * D)
                act.dma_start(w_enc1[hs, :], a["enc1"]).then_inc(enc_in, 16)
                act.dma_start(w_enc2[hs, :], a["enc2"][h]).then_inc(enc_in, 16)
                act.dma_start(bd0[hs, 0, hs], a["Wv"]).then_inc(enc_in, 16)
                act.dma_start(bd0[hs, 1, hs], a["Wo"]).then_inc(enc_in, 16)
                act.dma_start(bdg[hs, 0, h * E:(h + 1) * E], a["Wr"]).then_inc(enc_in, 16)
                act.dma_start(bdg[hs, 1, h * E:(h + 1) * E], a["WgT"]).then_inc(enc_in, 16)
                for n in range(2):
                    act.dma_start(v_b2[hs, n:n + 1], a["b_enc2"][n]).then_inc(vec_in, 16)
                    act.dma_start(v_ln0[hs, n:n + 1], a["ln0"][n]).then_inc(vec_in, 16)
                act.dma_start(v_b1[hs, :], a["b_enc1"][h]).then_inc(vec_in, 16)
            for n in range(2):
                act.dma_start(rows0[:, n, :], a["rows0"][n].partition_broadcast(P)).then_inc(vec_in, 16)
                act.dma_start(rowg[:, n, :], a["rowg"][n].partition_broadcast(P)).then_inc(vec_in, 16)
                act.dma_start(rowb2[:, n, :, :].rearrange("p e d -> p (e d)"),
                              a["rowb2"][n].partition_broadcast(P)).then_inc(vec_in, 16)
            for h in range(2):
                act.dma_start(lvecs[h * D:(h + 1) * D, :, 0:4], a["l1_ln"]).then_inc(l1_in, 16)
            act.dma_start(lvecs[:, :, 4:6], a["l1_b1"]).then_inc(l1_in, 16)
            act.dma_start(rows1[:, :, :, :].rearrange("p l w d -> p (l w d)"),
                          a["l1_rows"].partition_broadcast(P)).then_inc(l1_in, 16)

            def square(k, u, i=0):
                act.wait_ge(cen_ready, ln_no(k, u) + i)
                ac.activation(usl(Sq, u), usl(Cen, u), ACT.Square).then_inc(sq_ready, 1)

            def xt_out(t, g, i=0, scale=1.0, bias=0.0):
                full(act, ("xt", t, g), i)
                src = ps(("xt", t, g))
                if t in (0, 2, 3, 12):
                    read2 = ac.copy(gsl(XT, g), src[:, :])
                else:
                    read2 = ac.activation(gsl(XT, g), src[:, :], ACT.Identity, scale=scale, bias=bias)
                read2.then_inc(psum_free[use[("xt", t, g)][0]], 1)

            for g in range(G):
                full(act, ("embed", g))
                read(ac.copy(gsl(Hs, g), ps(("embed", g))[:, :]), ("embed", g))
            for u in range(U):
                square(0, u)
                for g in (2 * u, 2 * u + 1):
                    xt_out(0, g)
            act.wait_ge(vec_in, VEC_DMAS * 16)
            for g in range(G):
                for h in range(2):
                    full(act, ("enc1", g, h))
                    if g >= 2 and h == 0:
                        full(act, ("enc2", g - 2, 1, 1))
                    read(ac.activation(Gk[:, g % 2, h, :], ps(("enc1", g, h))[:, :], ACT.Gelu,
                                       bias=v_b1[:, 0:1]), ("enc1", g, h))
                for kind in range(2):
                    for h in range(2):
                        key = ("enc2", g, kind, h)
                        full(act, key)
                        n = 2 * kind + h
                        read(ac.activation(Ph[:, g, n * GC:(n + 1) * GC], ps(key)[:, :], ACT.Tanh,
                                           bias=v_b2[:, kind:kind + 1]), key)
            for g in range(G):
                act.wait_ge(frac_ready, g + 1)
                ac.activation(Ph[:, g, :], Ph[:, g, :], ACT.Sin, scale=TWO_PI).then_inc(cs_ready, 1)
                if g >= 1:
                    full(act, ("ret", g - 1))
                    read(ac.copy(gsl(Xn, g - 1), ps(("ret", g - 1))[:, :]), ("ret", g - 1))
            full(act, ("ret", G - 1))
            read(ac.copy(gsl(Xn, G - 1), ps(("ret", G - 1))[:, :]), ("ret", G - 1))
            for u in range(U):
                square(1, u)
                for g in (2 * u, 2 * u + 1):
                    xt_out(1, g, 0, v_ln0[:, 0:1], v_ln0[:, 1:2])

            def moe(m):
                k, t = (2, 2) if m == 0 else (13, 12)
                for u in range(U):
                    square(k, u)
                    for g in (2 * u, 2 * u + 1):
                        xt_out(t, g)
                for u in range(U):
                    if m == 0:
                        square(3, u)
                    act.wait_ge(gap_ready, 2 * m + u + 1)
                    ac.activation(rt[:, 6 + u, :], rt[:, 4 + u, :], ACT.Tanh, scale=0.5).then_inc(tanh_ready, 1)
                    if m == 0:
                        for g in (2 * u, 2 * u + 1):
                            xt_out(3, g)
                func = ACT.Gelu if m == 0 else ACT.Relu
                with act.Fori(0, E // 2) as i:
                    for s in range(2):
                        act.wait_ge(pack_in[m][s], 16 + 16 * i)
                        for g in range(G):
                            n = 4 * s + g
                            for hc in range(2):
                                for h in range(2):
                                    key = ("up", m, s, g, hc, h)
                                    full(act, key, i)
                                    ins = ac.activation(Hd[:, n % 2, hc, h, :], ps(key)[:, :], func,
                                                        bias=pack[:, s, 384 + hc:385 + hc])
                                    read(ins, key)

            moe(0)
            for u in range(U):
                square(4, u)
            act.wait_ge(l1_in, L1_DMAS * 16)
            scale = float(DH) ** -0.25
            with act.Fori(0, LAYERS) as i:
                step.enter(i, 1)
                step(ac.copy(lvec[:, :], lvecs[:, bass.ds(i, 1), :].rearrange("p l o -> p (l o)")))
                step.settle()
                step.leave(LAYERS)

                def vec(n):
                    return lvec[:, n:n + 1]

                def v_out(g):
                    full(act, ("v", g), i)
                    read(ac.copy(Vt[:, g, :], ps(("v", g))[:, :]), ("v", g))

                def kexp(g):
                    act.wait_ge(negm_ready, 4 * i + g + 1)
                    for jb in range(2):
                        c = slice(jb * S, (jb + 1) * S)
                        ins = ac.activation(Ke[:, g, c], ps(("k", g))[:, c], ACT.Exp, scale=scale,
                                            bias=ksm[:, g, 1, jb:jb + 1], accum_out=ksm[:, g, 2, jb:jb + 1])
                    read(ins, ("k", g))

                def qexp(g):
                    b, n, per = use[("q", g)]
                    act.wait_ge(psum_free[b], n + 1 + i * per)
                    ac.activation(Qe[:, g, :], Qe[:, g, :], ACT.Exp, scale=scale).then_inc(qe_ready, 1)

                def kt_out(g):
                    full(act, ("kt", g), i)
                    read(ac.copy(Kt[:, g % 2, :], ps(("kt", g))[:, :]), ("kt", g))

                def qt_out(g):
                    full(act, ("qt", g), i)
                    read(ac.copy(Qf[:, g % 2, :], ps(("qt", g))[:, :]), ("qt", g))

                square(5, 0, 4 * i)
                xt_out("attn", 0, i, vec(0), vec(1))
                xt_out("attn", 1, i, vec(0), vec(1))
                square(5, 1, 4 * i)
                v_out(0)
                v_out(1)
                xt_out("attn", 2, i, vec(0), vec(1))
                xt_out("attn", 3, i, vec(0), vec(1))
                kexp(0)
                qexp(0)
                kt_out(0)
                kexp(1)
                qexp(1)
                v_out(2)
                qt_out(0)
                kt_out(1)
                kexp(2)
                qexp(2)
                v_out(3)
                qt_out(1)
                kt_out(2)
                kexp(3)
                qexp(3)
                qt_out(2)
                kt_out(3)
                qt_out(3)

                def hidden(g):
                    for hc in range(2):
                        for h in range(2):
                            key = ("fup", g, hc, h)
                            full(act, key, i)
                            read(ac.activation(Hd[:, g % 2, hc, h, :], ps(key)[:, :], ACT.Gelu,
                                               bias=vec(4 + hc)), key)

                square(6, 0, 4 * i)
                xt_out("ffn", 0, i, vec(2), vec(3))
                xt_out("ffn", 1, i, vec(2), vec(3))
                square(6, 1, 4 * i)
                hidden(0)
                hidden(1)
                xt_out("ffn", 2, i, vec(2), vec(3))
                xt_out("ffn", 3, i, vec(2), vec(3))
                hidden(2)
                hidden(3)
                b, n, per = use[("fup", G - 1, 1, 1)]
                act.wait_ge(psum_free[b], n + 1 + i * per)
            moe(1)

        @block.vector
        def _(dve):
            step = Chain(dve, dve_step)
            ve = nc.vector

            dve.wait_ge(tab_in, 5 * 16)
            step(ve.tensor_scalar(mtT[:, :], mtT[:, :], 0.0, None, ALU.max))
            step(ve.tensor_copy(ppR[:, 0:9], ppT[:, 0:249:31]))
            ve.tensor_copy(ppR[:, 9:10], ppT[:, 255:256]).then_inc(tab_lhs_ready, 1)
            dve.wait_ge(consts_ready, 1)
            step(ve.tensor_scalar(iota_f[:, 1:2], iota_f[:, 0:1], 128.0, None, ALU.add))
            step(ve.tensor_scalar(iota_f[:, 2:3], iota_f[:, 0:1], -1.0, None, ALU.add))
            step(ve.tensor_scalar(turn[:, 1:2], iota_f[:, 0:1], 64.0, -64.0, ALU.is_ge, ALU.mult))
            step.settle()
            step(ve.tensor_tensor(turn[:, 2:3], iota_f[:, 0:1], turn[:, 1:2], ALU.add))
            step(ve.tensor_scalar(turn[:, 3:4], turn[:, 1:2], 1.0 / 256, 0.25, ALU.mult, ALU.add))
            step.settle()
            step(ve.tensor_scalar(turn[:, 4:5], turn[:, 2:3], 16.0, 0.5, ALU.is_ge, ALU.mult))
            step(ve.tensor_scalar(turn[:, 5:6], turn[:, 2:3], 32.0, None, ALU.is_ge))
            step(ve.tensor_scalar(turn[:, 6:7], turn[:, 2:3], 48.0, 2.0, ALU.is_ge, ALU.mult))
            step.settle()
            step(ve.tensor_tensor(turn[:, 7:8], turn[:, 4:5], turn[:, 5:6], ALU.add))
            step.settle()
            step(ve.scalar_tensor_tensor(turn[:, 0:1], turn[:, 6:7], 0.5, turn[:, 7:8], ALU.add, ALU.add))
            step(ve.tensor_scalar(epos[:, :], epos[:, :], EPS * PHASES, None, ALU.mult))
            for n, (rows, add) in enumerate(((P, None), (122, None), (10, tokb))):
                full(dve, ("table", n))
                src = ps(("table", n))[0:rows, 0:D]
                if add is None:
                    ins = ve.tensor_copy(tf[0:rows, 0, :], src)
                else:
                    ins = ve.tensor_tensor(tf[0:rows, 0, :], src, add[0:rows, :], ALU.add)
                read(ins, ("table", n))
                dve.wait_ge(psum_free[2 + n], 1)
                step(ve.tensor_copy(tabs[0:rows, n, 0, :], tf[0:rows, 0, :]))
                step.settle()
                step(ve.tensor_tensor(tf[0:rows, 1, :], tf[0:rows, 0, :], tabs[0:rows, n, 0, :], ALU.subtract))
                step.settle()
                step(ve.tensor_copy(tabs[0:rows, n, 1, :], tf[0:rows, 1, :]))
                step.settle()
                ins = ve.tensor_tensor(tabs[0:rows, n, 2, :], tf[0:rows, 1, :], tabs[0:rows, n, 1, :], ALU.subtract)
                if n < 2:
                    step(ins)
                    step.settle()
                else:
                    ins.then_inc(tables_ready, 1)

            def one_hot(g):
                dve.wait_ge(tok_in[g], 32)
                if g >= 2:
                    full(dve, ("embed", g - 2))
                sl = slice(g * UC, (g + 1) * UC)
                step(ve.tensor_scalar(onehot[:, g % 2, 0, :], tok_i[:, sl], iota_f[:, 0:1], None, ALU.is_equal))
                step(ve.tensor_scalar(onehot[0:122, g % 2, 1, :], tok_i[0:122, sl], iota_f[0:122, 1:2], None,
                                      ALU.is_equal))
                step(ve.tensor_scalar(ppstep[0:10, g % 2, :], pp_i[0:10, sl], 1.0, -1.0, ALU.min, ALU.mult))
                step.settle()
                ve.tensor_scalar(onehot[0:10, g % 2, 2, :], ppstep[0:10, g % 2, :], 8.0, iota_f[0:10, 2:3],
                                 ALU.min, ALU.is_equal).then_inc(onehot_ready, 1)

            def layernorm(k, u, src, dst, i=0, eps=EPS):
                st = stat[:, u]
                step(ve.tensor_reduce(st[:, 0, :], usl(src, u), AX_X, ALU.add))
                step.settle()
                step(ve.tensor_scalar(st[:, 1, :], st[:, 0, :], -1.0 / D, None, ALU.mult))
                step.settle()
                ve.tensor_tensor(usl(Cen, u), usl(src, u), wide(st[:, 1, :], UT), ALU.add).then_inc(cen_ready, 1)
                dve.wait_ge(sq_ready, ln_no(k, u) + i)
                step(ve.tensor_reduce(st[:, 2, :], usl(Sq, u), AX_X, ALU.add))
                step.settle()
                if eps is epos:
                    step(ve.scalar_tensor_tensor(st[:, 3, :], st[:, 2, :], 1.0 / D, epos[:, :], ALU.mult, ALU.add))
                else:
                    step(ve.tensor_scalar(st[:, 3, :], st[:, 2, :], 1.0 / D, eps, ALU.mult, ALU.add))
                step.settle()
                step(ve.tensor_scalar(st[:, 5, :].bitcast(I32), st[:, 3, :].bitcast(I32), 1, None,
                                      ALU.logical_shift_right))
                step.settle()
                step(ve.tensor_scalar(st[:, 4, :].bitcast(I32), st[:, 5, :].bitcast(I32), -1.0, float(MAGIC),
                                      ALU.mult, ALU.add))
                step.settle()
                for _ in range(NEWTON):
                    step(ve.tensor_tensor(st[:, 5, :], st[:, 4, :], st[:, 4, :], ALU.mult))
                    step.settle()
                    step(ve.scalar_tensor_tensor(st[:, 5, :], st[:, 5, :], -0.5, st[:, 3, :], ALU.mult, ALU.mult))
                    step.settle()
                    step(ve.scalar_tensor_tensor(st[:, 4, :], st[:, 5, :], 1.5, st[:, 4, :], ALU.add, ALU.mult))
                    step.settle()
                ve.tensor_tensor(usl(dst, u), usl(Cen, u), wide(st[:, 4, :], UT), ALU.mult).then_inc(xn_ready, 1)

            for g in range(G):
                one_hot(g)
            for u in range(U):
                dve.wait_ge(psum_free[0], u + 1)
                dve.wait_ge(psum_free[1], u + 1)
                layernorm(0, u, Hs, Xs)

            step.settle()
            for g in range(G):
                for n in range(4):
                    b, c, _ = use[("enc2", g, n // 2, n % 2)]
                    dve.wait_ge(psum_free[b], c + 1)
                step(ve.tensor_scalar(Ph[:, g, :], Ph[:, g, :], turn[:, 0:1], turn[:, 3:4], ALU.mult, ALU.add))
                step.settle()
                step(ve.tensor_scalar(Turn[:, :], Ph[:, g, :], ROUND, -ROUND, ALU.add, ALU.add))
                step.settle()
                ve.tensor_tensor(Ph[:, g, :], Ph[:, g, :], Turn[:, :], ALU.subtract).then_inc(frac_ready, 1)
                dve.wait_ge(frac_ready, g + 1)
            dve.wait_ge(vec_in, VEC_DMAS * 16)
            for g in range(G):
                full(dve, ("v0", g))
                read(ve.tensor_tensor(Vt[:, g, :].rearrange("p (t d) -> p t d", d=D),
                                      ps(("v0", g))[:, :].rearrange("p (t d) -> p t d", d=D),
                                      row(rows0[:, 0, :]), ALU.add), ("v0", g))
                for h in range(2):
                    for jb in range(2):
                        key = ("score", g, h, jb)
                        full(dve, key)
                        if g >= 2 and h == 0 and jb == 0:
                            full(dve, ("ret", g - 2))
                        read(ve.tensor_tensor(Sc[:, g % 2, 2 * h + jb, :], ps(key)[:, 0:384], causal[:, :],
                                              ALU.mult), key)
            for u in range(U):
                dve.wait_ge(psum_free[6], use[("ret", 2 * u)][1] + 1)
                dve.wait_ge(psum_free[7], use[("ret", 2 * u + 1)][1] + 1)
                layernorm(1, u, Xn, Xn, 0, epos)
            for g in range(G):
                full(dve, ("o0", g))
                dve.wait_ge(hx_ready, g // 2 + 1)
                read(ve.tensor_tensor(gsl(Hs, g), gsl(Hs, g), ps(("o0", g))[:, :], ALU.add), ("o0", g))

            def route_unit(m, u):
                lg, eq, f1, f2, t1, t2 = (route[:, n, :].rearrange("p (t e) -> p t e", e=E) for n in range(6))
                pr = prio[:, :].rearrange("p (t e) -> p t e", e=E)
                for g in (2 * u, 2 * u + 1):
                    full(dve, ("gate", m, g))
                    ins = ve.tensor_tensor(lg[:, (g % 2) * E:(g % 2 + 1) * E, :],
                                           ps(("gate", m, g))[:, 0:8 * E].rearrange("p (t e) -> p t e", e=E),
                                           rowg[:, m, :].unsqueeze(1).broadcast_to([P, E, E]), ALU.add)
                    read(ins, ("gate", m, g))
                    dve.wait_ge(psum_free[4 + g % 2], use[("gate", m, g)][1] + 1)

                def best(scores, top, first):
                    step(ve.tensor_reduce(top, scores, AX_X, ALU.max))
                    step.settle()
                    step(ve.tensor_tensor(eq, scores, wide(top, UT, E), ALU.is_equal))
                    step.settle()
                    step(ve.tensor_tensor(t1, eq, pr, ALU.mult))
                    step.settle()
                    step(ve.tensor_reduce(rt[:, 2, :], t1, AX_X, ALU.max))
                    step.settle()
                    step(ve.tensor_tensor(first, t1, wide(rt[:, 2, :], UT, E), ALU.is_equal))
                    step.settle()

                best(lg, rt[:, 0, :], f1)
                step(ve.scalar_tensor_tensor(route[:, 5, :], route[:, 2, :], -3.0e38, route[:, 0, :],
                                             ALU.mult, ALU.add))
                step.settle()
                best(t2, rt[:, 1, :], f2)
                ve.tensor_tensor(rt[:, 4 + u, :], rt[:, 0, :], rt[:, 1, :], ALU.subtract).then_inc(gap_ready, 1)
                dve.wait_ge(tanh_ready, 2 * m + u + 1)
                step(ve.tensor_scalar(rt[:, 2, :], rt[:, 6 + u, :], 0.5, 0.5, ALU.mult, ALU.add))
                step(ve.tensor_scalar(rt[:, 3, :], rt[:, 6 + u, :], -0.5, 0.5, ALU.mult, ALU.add))
                step.settle()
                step(ve.tensor_tensor(t1, f1, wide(rt[:, 2, :], UT, E), ALU.mult))
                step(ve.tensor_tensor(t2, f2, wide(rt[:, 3, :], UT, E), ALU.mult))
                step.settle()
                step(ve.tensor_tensor(comb[:, 2 * u:2 * u + 2, :, :].rearrange("p g t e -> p (g t) e"), t1, t2,
                                      ALU.add))
                step.settle()

            def own_affine(n, i):
                s, g = n % 8 // 4, n % 4
                if g == 0:
                    dve.wait_ge(pack_in[0][s], 16 + 16 * i)
                dve.wait_ge(psum_full[3], use[("up", 0, 0, 0, 1, 1)][1] + n % 8 - 1 + i * 8)
                ve.tensor_scalar(Xe[:, n % 2, :], gsl(XT, g), pack[:, s, 386:387], pack[:, s, 387:388],
                                 ALU.mult, ALU.add).then_inc(xe_ready, 1)

            def expert_pair(m, i, last):
                for n in range(8):
                    s, g = n // 4, n % 4
                    if m == 0 and not (last and n >= 6):
                        own_affine(n + 2, i + (n + 2) // 8)
                    key = ("down", m, s, g)
                    full(dve, key, i)
                    e = bass.ds(2 * i + s, 1)
                    b2 = rowb2[:, m, e, :].rearrange("p e d -> p (e d)")
                    w = comb[:, g, :, e].rearrange("p t e -> p (t e)")
                    tmp = Tmp[:, :].rearrange("p (t d) -> p t d", d=D)
                    wgt = Wgt[:, :].rearrange("p (t d) -> p t d", d=D)
                    read(ve.tensor_tensor(tmp, ps(key)[:, :].rearrange("p (t d) -> p t d", d=D), row(b2), ALU.add),
                         key)
                    dve.wait_ge(psum_free[use[key][0]], use[key][1] + 1 + i * use[key][2])
                    step(ve.tensor_tensor(wgt, tmp, wide(w, E), ALU.mult))
                    step.settle()
                    ve.tensor_tensor(gsl(Hs, g), gsl(Hs, g), Wgt[:, :], ALU.add).then_inc(acc_done, 1)
                    dve.wait_ge(acc_done, E * G * m + 8 * i + n + 1)

            def experts(m):
                if m == 0:
                    for g in (G - 2, G - 1):
                        b, c, _ = use[("xt", 3, g)]
                        dve.wait_ge(psum_free[b], c + 1)
                    own_affine(0, 0)
                    own_affine(1, 0)
                trips = E // 2 - 1
                with dve.Fori(0, trips) as i:
                    step.enter(i, 2 * G)
                    expert_pair(m, i, False)
                    step.leave(trips)
                expert_pair(m, trips, True)

            for u in range(U):
                dve.wait_ge(psum_free[0], use[("o0", 2 * u)][1] + 1)
                dve.wait_ge(psum_free[1], use[("o0", 2 * u + 1)][1] + 1)
                layernorm(2, u, Hs, Xs)
            for u in range(U):
                dve.wait_ge(xn_ready, ln_no(2, u))
                layernorm(3, u, Xs, Xn)
                route_unit(0, u)
            experts(0)

            for u in range(U):
                layernorm(4, u, Hs, Xs)
            dve.wait_ge(xn_ready, ln_no(4, 1))
            with dve.Fori(0, LAYERS) as i:
                step.enter(i, L1_STEPS)

                def keys_max(g):
                    full(dve, ("k", g), i)
                    step(ve.tensor_reduce(ksm[:, g, 0, :], ps(("k", g))[:, :].rearrange("p (b t) -> p b t", b=2),
                                          AX_X, ALU.max))
                    step.settle()
                    ve.tensor_scalar(ksm[:, g, 1, :], ksm[:, g, 0, :], -(float(DH) ** -0.25), None,
                                     ALU.mult).then_inc(negm_ready, 1)

                def queries_max(g):
                    full(dve, ("q", g), i)
                    q = ps(("q", g))[:, :].rearrange("p (n d) -> p n d", d=DH)
                    step(ve.tensor_reduce(small[:, g, 0, :], q, AX_X, ALU.max))
                    step.settle()
                    ins = ve.tensor_tensor(Qe[:, g, :].rearrange("p (n d) -> p n d", d=DH), q,
                                           wide(small[:, g, 0, :], D, DH), ALU.subtract)
                    read(ins, ("q", g))

                def queries_norm(g):
                    dve.wait_ge(qe_ready, 4 * i + g + 1)
                    q = Qe[:, g, :].rearrange("p (n d) -> p n d", d=DH)
                    step(ve.tensor_reduce(small[:, g, 1, :], q, AX_X, ALU.add))
                    step.settle()
                    step(ve.reciprocal(small[:, g, 2, :], small[:, g, 1, :]))
                    step.settle()
                    ve.tensor_tensor(q, q, wide(small[:, g, 2, :], D, DH), ALU.mult).then_inc(qn_ready, 1)

                def context_out(g):
                    full(dve, ("ctx", g), i)
                    ins = ve.tensor_tensor(Cm[:, g % 2, :, :], ps(("ctx", g))[:, 0:S].rearrange(
                        "p (b n) -> p b n", b=2), headmask[:, :].unsqueeze(1).broadcast_to([P, 2, P]), ALU.mult)
                    read(ins, ("ctx", g))

                def mix_out(g):
                    b, n, per = use[("k", g)]
                    dve.wait_ge(psum_free[b], n + 1 + i * per)
                    step(ve.reciprocal(ksm[:, g, 3, :], ksm[:, g, 2, :]))
                    step.settle()
                    full(dve, ("m", g), i)
                    for jb in range(2):
                        ins = ve.tensor_scalar(Mm[:, g % 2, jb, :], ps(("m", g))[:, jb * P:(jb + 1) * P],
                                               ksm[:, g, 3, jb:jb + 1], None, ALU.mult)
                    read(ins, ("m", g))

                def add_out(key, g, w):
                    full(dve, key, i)
                    dve.wait_ge(bias_added, 4 * i + 2 * w + g // 2 + 1)
                    read(ve.tensor_tensor(gsl(Xs, g), gsl(Xs, g), ps(key)[:, :], ALU.add), key)

                def added(key):
                    b, n, per = use[key]
                    dve.wait_ge(psum_free[b], n + 1 + i * per)

                layernorm(5, 0, Xs, Xn, 4 * i)
                layernorm(5, 1, Xs, Xn, 4 * i)
                for g in (0, 1):
                    keys_max(g)
                    queries_max(g)
                queries_norm(0)
                keys_max(2)
                queries_max(2)
                context_out(0)
                queries_norm(1)
                mix_out(0)
                keys_max(3)
                queries_max(3)
                context_out(1)
                add_out(("o", 0), 0, 0)
                queries_norm(2)
                mix_out(1)
                context_out(2)
                add_out(("o", 1), 1, 0)
                queries_norm(3)
                mix_out(2)
                context_out(3)
                add_out(("o", 2), 2, 0)
                mix_out(3)
                add_out(("o", 3), 3, 0)
                added(("o", 1))
                layernorm(6, 0, Xs, Xn, 4 * i)
                added(("o", 3))
                layernorm(6, 1, Xs, Xn, 4 * i)
                for g in range(G):
                    add_out(("fdown", g), g, 1)
                for g in (2, 3):
                    added(("fdown", g))
                step.leave(LAYERS)
            for u in range(U):
                step(ve.tensor_tensor(usl(Hs, u), usl(Hs, u), usl(Xs, u), ALU.add))
                step.settle()

            for u in range(U):
                layernorm(13, u, Hs, Xn)
            for u in range(U):
                route_unit(1, u)
            experts(1)

        @block.tensor
        def _(pe):
            te = nc.tensor

            def col(g, j):
                return slice(g * GC + j * P, g * GC + (j + 1) * P)

            def transpose4(key, src, i=0):
                dst = bank_free(key, i)
                for j in range(4):
                    ins = te.transpose(dst[:, j * P:(j + 1) * P], src[:, j * P:(j + 1) * P], ident[:, :])
                made(ins, key)

            def xt(t, k, g, src, i=0, ki=0):
                pe.wait_ge(xn_ready, ln_no(k, g // 2) + ki)
                transpose4(("xt", t, g), gsl(src, g), i)

            def xt_in(t, g, i=0):
                b, n, per = use[("xt", t, g)]
                pe.wait_ge(psum_free[b], n + 1 + i * per if per else n + 1)

            pe.wait_ge(tab_in, 5 * 16)
            pe.wait_ge(tab_lhs_ready, 1)
            for n, (lhs, rhs, rows) in enumerate(((mtT[:, 0:P], tokW, P), (mtT[:, P:250], tokW, 122),
                                                  (ppR[:, :], ppW, 10))):
                dst = bank_free(("table", n))
                made(te.matmul(dst[0:rows, 0:D], lhs, rhs[:, :], start=True, stop=True), ("table", n))
            pe.wait_ge(tables_ready, 1)
            pe.wait_ge(ident_ready, 1)
            for g in range(G):
                pe.wait_ge(onehot_ready, g + 1)
                dst = bank_free(("embed", g))
                for j in range(4):
                    for h in range(2):
                        c = (2 * h + j // 2) * S + (j % 2) * P
                        o = (2 * j + h) * D
                        for n, rows in enumerate((P, 122, 10)):
                            for part in range(3):
                                ins = te.matmul(dst[:, o:o + D], onehot[0:rows, g % 2, n, c:c + P],
                                                tabs[0:rows, n, part, :], start=(n == 0 and part == 0),
                                                stop=(n == 2 and part == 2))
                made(ins, ("embed", g))
            for g in range(G):
                xt(0, 0, g, Xs)
            pe.wait_ge(enc_in, 12 * 16)
            for g in range(G):
                xt_in(0, g)
                for h in range(2):
                    hs = slice(h * D, (h + 1) * D)
                    dst = bank_free(("enc1", g, h))
                    made(te.matmul(dst[:, :], w_enc1[hs, :], XT[hs, g * GC:(g + 1) * GC], start=True, stop=True),
                         ("enc1", g, h))
                for kind in range(2):
                    ks = slice(kind * D, (kind + 1) * D)
                    for h in range(2):
                        key = ("enc2", g, kind, h)
                        dst = bank_free(key)
                        b, n, _ = use[("enc1", g, h)]
                        pe.wait_ge(psum_free[b], n + 1)
                        made(te.matmul(dst[:, :], w_enc2[ks, :], Gk[ks, g % 2, h, :], start=True, stop=True), key)
            for g in range(G):
                dst = bank_free(("v0", g))
                for j in range(4):
                    ins = te.matmul(dst[:, j * P:(j + 1) * P], XT[:, col(g, j)], bd0[:, 0, :], start=True, stop=True)
                made(ins, ("v0", g))
                pe.wait_ge(cs_ready, g + 1)
                for h in range(2):
                    for jb in range(2):
                        key = ("score", g, h, jb)
                        dst = bank_free(key)
                        kc = h * GC + jb * S
                        qc = (2 + h) * GC + jb * S
                        te.matmul(dst[:, 0:S], Ph[:, g, kc:kc + P], Ph[:, g, qc:qc + S], start=True, stop=True)
                        made(te.matmul(dst[:, S:S + P], Ph[:, g, kc + P:kc + S], Ph[:, g, qc + P:qc + S],
                                       start=True, stop=True), key)
                dst = bank_free(("ret", g))
                pe.wait_ge(psum_free[g % 2], use[("v0", g)][1] + 1)
                for h in range(2):
                    for jb in range(2):
                        key = ("score", g, h, jb)
                        b, n, _ = use[key]
                        pe.wait_ge(psum_free[b], n + 1)
                        sc = Sc[:, g % 2, 2 * h + jb, :]
                        o = (4 * jb + h) * D
                        v0 = Vt[:, g, o:o + D]
                        v1 = Vt[:, g, o + 2 * D:o + 3 * D]
                        te.matmul(dst[:, o:o + D], sc[:, 0:P], v0, start=True, stop=True)
                        te.matmul(dst[:, o + 2 * D:o + 3 * D], sc[:, P:S], v0, start=True, stop=False)
                        ins = te.matmul(dst[:, o + 2 * D:o + 3 * D], sc[:, S:S + P], v1, start=False, stop=True)
                made(ins, ("ret", g))
            for g in range(G):
                xt(1, 1, g, Xn)
            for g in range(G):
                xt_in(1, g)
                dst = bank_free(("o0", g))
                for j in range(4):
                    ins = te.matmul(dst[:, j * P:(j + 1) * P], XT[:, col(g, j)], bd0[:, 1, :], start=True, stop=True)
                made(ins, ("o0", g))

            def moe(m):
                for g in range(G):
                    if m == 0:
                        xt(2, 2, g, Xs)
                    else:
                        xt(12, 13, g, Xn)
                for g in range(G):
                    xt_in(2 if m == 0 else 12, g)
                    dst = bank_free(("gate", m, g))
                    for j in range(4):
                        ins = te.matmul(dst[:, j * 2 * E:(j + 1) * 2 * E], XT[:, col(g, j)], bdg[:, m, :],
                                        start=True, stop=True)
                    made(ins, ("gate", m, g))
                if m == 0:
                    for g in range(G):
                        xt(3, 3, g, Xn)

                def up(s, g, i):
                    n = 4 * s + g
                    if g == 0:
                        pe.wait_ge(pack_in[m][s], 16 + 16 * i)
                    if m == 0:
                        pe.wait_ge(xe_ready, 8 * i + n + 1)
                        src = Xe[:, n % 2, :]
                    else:
                        src = gsl(XT, g)
                    for hc in range(2):
                        dst = [bank_free(("up", m, s, g, hc, h), i) for h in range(2)]
                        for h in range(2):
                            hs = slice(h * D, (h + 1) * D)
                            made(te.matmul(dst[h][:, :], pack[hs, s, hc * P:(hc + 1) * P], src[hs, :], start=True,
                                           stop=True), ("up", m, s, g, hc, h))

                def down(s, g, i):
                    key = ("down", m, s, g)
                    dst = bank_free(key, i)
                    for hc in range(2):
                        for h in range(2):
                            b, n, per = use[("up", m, s, g, hc, h)]
                            pe.wait_ge(psum_free[b], n + 1 + i * per)
                    for j in range(4):
                        for h in range(2):
                            o = (2 * j + h) * D
                            for hc in range(2):
                                ins = te.matmul(dst[:, o:o + D], Hd[:, (4 * s + g) % 2, hc, h, j * P:(j + 1) * P],
                                                pack[:, s, HID + hc * D:HID + (hc + 1) * D], start=(hc == 0),
                                                stop=(hc == 1))
                    made(ins, key)

                def pair(i, last):
                    for n in range(8):
                        if n < 7:
                            up((n + 1) // 4, (n + 1) % 4, i)
                        elif not last:
                            up(0, 0, i + 1)
                        down(n // 4, n % 4, i)

                up(0, 0, 0)
                with pe.Fori(0, E // 2 - 1) as i:
                    pair(i, False)
                pair(E // 2 - 1, True)

            moe(0)

            pe.wait_ge(attn_w_in, 32)
            with pe.Fori(0, LAYERS) as i:
                def t_attn(g):
                    xt("attn", 5, g, Xn, i, 4 * i)

                def project(g):
                    if g == 0:
                        pe.wait_ge(attn_w_in, 32 + 32 * i)
                    xt_in("attn", g, i)
                    dst = bank_free(("k", g), i)
                    made(te.matmul(dst[:, :], bd1[:, 1, :], gsl(XT, g), start=True, stop=True), ("k", g))
                    for what, w in (("q", 0), ("v", 2)):
                        dst = bank_free((what, g), i)
                        for j in range(4):
                            ins = te.matmul(dst[:, j * P:(j + 1) * P], XT[:, col(g, j)], bd1[:, w, :],
                                            start=True, stop=True)
                        made(ins, (what, g))

                def sbuf_has(key):
                    b, n, per = use[key]
                    pe.wait_ge(psum_free[b], n + 1 + i * per)

                def k_turn(g):
                    sbuf_has(("k", g))
                    transpose4(("kt", g), Ke[:, g, :], i)

                def q_turn(g):
                    pe.wait_ge(qn_ready, 4 * i + g + 1)
                    transpose4(("qt", g), Qe[:, g, :], i)

                def context(g):
                    sbuf_has(("kt", g))
                    sbuf_has(("v", g))
                    dst = bank_free(("ctx", g), i)
                    for jb in range(2):
                        for jj in range(2):
                            c = slice((2 * jb + jj) * P, (2 * jb + jj + 1) * P)
                            ins = te.matmul(dst[:, jb * P:(jb + 1) * P], Vt[:, g, c], Kt[:, g % 2, c],
                                            start=(jj == 0), stop=(jj == 1))
                    made(ins, ("ctx", g))

                def mix(g):
                    sbuf_has(("ctx", g))
                    dst = bank_free(("m", g), i)
                    for jb in range(2):
                        ins = te.matmul(dst[:, jb * P:(jb + 1) * P], Cm[:, g % 2, jb, :], bd1[:, 3, :], start=True,
                                        stop=True)
                    made(ins, ("m", g))

                def attend(g):
                    sbuf_has(("m", g))
                    sbuf_has(("qt", g))
                    dst = bank_free(("o", g), i)
                    for j in range(4):
                        ins = te.matmul(dst[:, j * P:(j + 1) * P], Qf[:, g % 2, j * P:(j + 1) * P],
                                        Mm[:, g % 2, j // 2, :], start=True, stop=True)
                    made(ins, ("o", g))

                t_attn(0)
                t_attn(1)
                project(0)
                project(1)
                t_attn(2)
                t_attn(3)
                k_turn(0)
                project(2)
                context(0)
                q_turn(0)
                k_turn(1)
                project(3)
                mix(0)
                context(1)
                q_turn(1)
                k_turn(2)
                attend(0)
                mix(1)
                context(2)
                q_turn(2)
                k_turn(3)
                attend(1)
                mix(2)
                context(3)
                q_turn(3)
                attend(2)
                mix(3)
                attend(3)

                def f_up(g):
                    if g == 0:
                        pe.wait_ge(ff_w_in, 48 + 48 * i)
                    xt_in("ffn", g, i)
                    for hc in range(2):
                        dst = [bank_free(("fup", g, hc, h), i) for h in range(2)]
                        for h in range(2):
                            hs = slice(h * D, (h + 1) * D)
                            made(te.matmul(dst[h][:, :], ff[hs, hc * P:(hc + 1) * P],
                                           XT[hs, g * GC:(g + 1) * GC], start=True, stop=True), ("fup", g, hc, h))

                def f_down(g):
                    dst = bank_free(("fdown", g), i)
                    for hc in range(2):
                        for h in range(2):
                            sbuf_has(("fup", g, hc, h))
                    for j in range(4):
                        for h in range(2):
                            o = (2 * j + h) * D
                            for hc in range(2):
                                ins = te.matmul(dst[:, o:o + D], Hd[:, g % 2, hc, h, j * P:(j + 1) * P],
                                                ff[:, HID + hc * D:HID + (hc + 1) * D], start=(hc == 0),
                                                stop=(hc == 1))
                    made(ins, ("fdown", g))

                xt("ffn", 6, 0, Xn, i, 4 * i)
                xt("ffn", 6, 1, Xn, i, 4 * i)
                f_up(0)
                f_up(1)
                f_down(0)
                f_down(1)
                xt("ffn", 6, 2, Xn, i, 4 * i)
                xt("ffn", 6, 3, Xn, i, 4 * i)
                f_up(2)
                f_up(3)
                f_down(2)
                f_down(3)
            moe(1)


VEC_DMAS = 10 + 6
L1_DMAS = 4
L1_STEPS = 80


def kernel(**inputs):
    import numpy as np
    import concourse.bacc as bacc
    from concourse.bass_utils import run_bass_kernel_spmd

    n = {k: np.asarray(v) for k, v in inputs.items()}

    def cat(*xs, axis=-1):
        return np.concatenate(xs, axis=axis)

    def pack(w1, w2, b1, *more):
        e = w1.shape[0]
        cols = [cat(w1, w1, axis=1), w2.reshape(e, 2, P, D).transpose(0, 2, 1, 3).reshape(e, P, 2 * D),
                b1.reshape(e, 2, P).transpose(0, 2, 1)]
        cols += [cat(v, v)[:, :, None] for v in more]
        return cat(*cols)

    t = "L0_attn_"
    l1 = "L1_attn_"
    arrays = {
        "x": n["x"].reshape(-1), "itok": n["itok_BS_0_63"].reshape(-1),
        "move_tableT": n["L0_tok_move_table"].T, "pp_tableT": n["L0_tok_pp_table"].T,
        "tok_WT": n["L0_tok_W"].T, "tok_b": n["L0_tok_b"],
        "enc1": cat(n[t + "Wk1"], n[t + "Wq1"]),
        "enc2": np.stack([cat(n[t + "Wk2"], n[t + "Wk2"]), cat(n[t + "Wq2"], n[t + "Wq2"])]),
        "Wv": n[t + "Wv"], "Wo": n[t + "Wo"],
        "b_enc1": np.stack([n[t + "bk1"], n[t + "bq1"]])[:, :, None],
        "b_enc2": np.stack([n[t + "bk2"], n[t + "bq2"]])[:, :, None],
        "ln0": np.stack([n[t + "ln_w"], n[t + "ln_b"]])[:, :, None],
        "rows0": np.stack([n[t + "bv"], n[t + "bo"]]),
        "Wr": n["L0_ffn_Wr"], "WgT": n["L1_ffn_Wg"].T,
        "rowg": np.stack([n["L0_ffn_br"], n["L1_ffn_bg"]]),
        "rowb2": np.stack([n["L0_ffn_b2"].reshape(-1), n["L1_ffn_b2"].reshape(-1)]),
        "pack0": pack(n["L0_ffn_W1"], n["L0_ffn_W2"], n["L0_ffn_b1"], n["L0_ffn_ln_g"], n["L0_ffn_ln_b"]),
        "pack1": pack(n["L1_ffn_W1"].transpose(0, 2, 1), n["L1_ffn_W2"].transpose(0, 2, 1), n["L1_ffn_b1"]),
        "l1_attn": cat(n[l1 + "Wq"], n[l1 + "Wk"], n[l1 + "Wv"], n[l1 + "Wo"]),
        "l1_W1": n[l1 + "W1"], "l1_W2": n[l1 + "W2"],
        "l1_ln": np.stack([n[l1 + v] for v in ("ln1_g", "ln1_b", "ln2_g", "ln2_b")], -1).transpose(1, 0, 2),
        "l1_b1": n[l1 + "b1"].reshape(LAYERS, 2, P).transpose(2, 0, 1),
        "l1_rows": np.stack([n[l1 + "bo"], n[l1 + "b2"]], 1).reshape(-1),
    }
    nc = bacc.Bacc("TRN2", target_bir_lowering=False, num_devices=1)
    launch, aps = {}, {}
    for name, v in arrays.items():
        v = np.ascontiguousarray(v)
        launch[f"in_{name}"] = v
        aps[name] = nc.dram_tensor(f"in_{name}", v.shape, mybir.dt.from_np(v.dtype), kind="ExternalInput").ap()
    out = nc.dram_tensor("out_0", (B, S, D), F32, kind="ExternalOutput").ap()
    lm_tower(nc, aps, out)
    r = run_bass_kernel_spmd(nc, [launch], core_ids=[0])
    return r.results[0]["out_0"]
```

```python
from contextlib import ExitStack

import concourse.bass as bass
from concourse import mybir

ALU = mybir.AluOpType
ACT = mybir.ActivationFunctionType
F32 = mybir.dt.float32
BF16 = mybir.dt.bfloat16
I32 = mybir.dt.int32
AX_X = mybir.AxisListType.X

P = 128
D = 64
S = 256
B = 16
G = 4
U = 2
GC = 512
UC = 1024
UT = 16
E = 8
HID = 256
LAYERS = 4
HEADS = 8
DH = 8
EPS = 1e-5
PHASES = 64
MAGIC = 0x5F3759DF
ROUND = float(3 * 2 ** 22)
TWO_PI = 6.283185
NEWTON = 3



class PsumPlan:

    def __init__(self):
        self.count = [0] * 8
        self.at = {}
        self.body = None

    def add(self, key, bank):
        if self.body is None:
            self.at[key] = (bank, self.count[bank], 0)
            self.count[bank] += 1
        else:
            self.body.append((key, bank))

    def loop(self):
        self.body = []

    def end(self, trips):
        per = [sum(b == bank for _, b in self.body) for bank in range(8)]
        seen = list(self.count)
        for key, bank in self.body:
            self.at[key] = (bank, seen[bank], per[bank])
            seen[bank] += 1
        self.count = [c + trips * p for c, p in zip(self.count, per)]
        self.body = None


def plan_psum():
    plan = PsumPlan()
    for n in range(3):
        plan.add(("table", n), 2 + n)
    plan.add(("b1", 0), 5)
    for g in range(G):
        plan.add(("embed", g), g % 2)

    def transposes(t, groups=range(G)):
        for g in groups:
            plan.add(("xt", t, g), 6 + g % 2)

    transposes(0)
    for g in range(G):
        for h in range(2):
            plan.add(("enc1", g, h), h)
        for kind in range(2):
            for h in range(2):
                plan.add(("enc2", g, kind, h), 2 + 2 * kind + h)
    for g in range(G):
        plan.add(("v0", g), g % 2)
        for h in range(2):
            for jb in range(2):
                plan.add(("score", g, h, jb), 2 + 2 * h + jb)
        plan.add(("ret", g), 6 + g % 2)
    transposes(1)
    for g in range(G):
        plan.add(("o0", g), g % 2)

    def moe(m):
        transposes(2 if m == 0 else 12)
        for g in range(G):
            plan.add(("gate", m, g), 4 + g % 2)
        for g in range(G):
            for k in range(2):
                plan.add(("xs", m, g, k), 2 * (g % 2) + k)
            plan.add(("ct", m, g), 6 + g % 2)
        plan.loop()
        for s in range(2):
            for g in range(G):
                for hc in range(2):
                    for h in range(2):
                        plan.add(("up", m, s, g, hc, h), 2 * hc + h)
                plan.add(("wb", m, s, g), 6 + g % 2)
                plan.add(("down", m, s, g), 4 + g % 2)
        plan.end(E // 2)
        for g in range(G):
            plan.add(("at", m, g), 6 + g % 2)

    moe(0)
    plan.loop()
    transposes("attn")
    for g in range(G):
        plan.add(("q", g), g % 2)
        plan.add(("k", g), 2 + g % 2)
    for what, g in (("v", 0), ("v", 1), ("v", 2), ("qt", 0), ("v", 3), ("qt", 1), ("qt", 2), ("qt", 3)):
        plan.add((what, g), 4)
    for g in range(G):
        plan.add(("kt", g), 5)
        plan.add(("ctx", g), 6)
        plan.add(("m", g), 6)
        plan.add(("o", g), 7)
    transposes("ffn")
    for g in range(G):
        for hc in range(2):
            for h in range(2):
                plan.add(("fup", g, hc, h), 2 * hc + h)
        plan.add(("fdown", g), 4 + g % 2)
    plan.end(LAYERS)
    moe(1)
    return plan.at


class Chain:

    def __init__(self, eng, sem):
        self.eng, self.sem, self.n, self.i, self.per = eng, sem, 0, None, 0

    def __call__(self, ins):
        ins.then_inc(self.sem, 1)
        self.n += 1
        return ins

    def settle(self):
        self.eng.wait_ge(self.sem, self.n if self.i is None else self.n + self.i * self.per)

    def enter(self, i, per):
        self.i, self.per, self.start = i, per, self.n

    def leave(self, trips):
        assert self.n - self.start == self.per, (self.n - self.start, self.per)
        self.n = self.start + trips * self.per
        self.i = None


def lm_tower(nc, a, out):
    use = plan_psum()
    ctx = ExitStack()
    with ctx:
        def sb(name, shape, dt=F32):
            return ctx.enter_context(nc.sbuf_tensor(name, shape, dt))

        def sem(name):
            return ctx.enter_context(nc.semaphore(name))

        ctx.enter_context(nc.allow_non_contiguous_dma("small vectors and weights, once"))

        bank = [ctx.enter_context(nc.psum_tensor(f"bank{b}", [P, GC], F32)) for b in range(8)]
        Hs = sb("Hs", [P, G * GC])
        Xs = sb("Xs", [P, G * GC])
        Xn = sb("Xn", [P, G * GC])
        Cen = sb("Cen", [P, G * GC])
        Sq = sb("Sq", [P, G * GC])
        XT = sb("XT", [P, G * GC])
        stat = sb("stat", [P, U, 6, UT])
        Ph = sb("Ph", [P, G, 4 * GC])
        tok_i = Ph[:, 0:2, :].rearrange("p a b -> p (a b)").bitcast(I32)
        pp_i = Ph[:, 2:4, :].rearrange("p a b -> p (a b)").bitcast(I32)
        onehot = sb("onehot", [P, 2, 3, UC], BF16)
        ppstep = sb("ppstep", [16, 2, UC])
        Gk = sb("Gk", [P, 2, 2, GC])
        Turn = Sq
        Sc = sb("Sc", [P, 2, 4, 384])
        Vt = sb("Vt", [P, G, GC])
        Hd = sb("Hd", [P, 2, 2, 2, GC])
        Xs2 = Ph[:, 0:2, :].rearrange("p a b -> p (a b)").bitcast(BF16).rearrange("p (k c) -> p k c", k=2)
        X3 = Ph[:, 2:4, :].rearrange("p a b -> p (a b)").bitcast(BF16)[:, 0:G * E * 3 * D].rearrange(
            "p (t n d) -> p t n d", n=3, d=D)
        w1all = Hd[0:D, :, :, :, :].rearrange("p a b c d -> p (a b c d)")[:, 0:E * HID]
        Tmp = sb("Tmp", [P, GC])
        Wb = sb("Wb", [P, 2, GC])
        Qe = Ph[:, 0, :].rearrange("p (n c) -> p n c", n=G)
        Ke = Ph[:, 1, :].rearrange("p (n c) -> p n c", n=G)
        Kt = Ph[:, 2, 0:UC].rearrange("p (n c) -> p n c", n=2)
        Qf = Ph[:, 2, UC:2 * UC].rearrange("p (n c) -> p n c", n=2)
        Cm = sb("Cm", [P, 2, 2, P])
        Mm = sb("Mm", [P, 2, 2, P])
        small = sb("small", [P, G, 3, D])
        ksm = sb("ksm", [P, G, 4, 2])
        route = sb("route", [P, 8, UT * E])
        rt = sb("rt", [P, 8, UT])
        comb = sb("comb", [P, 16, 16])
        combr = sb("combr", [P, 16, 16])
        comb3 = sb("comb3", [P, 16, 3, 16], BF16)
        CT = sb("CT", [P, G * GC], BF16)
        ident = sb("ident", [P, P])
        identb = sb("identb", [P, P], BF16)
        select = sb("select", [P, E, P], BF16)
        selcur = sb("selcur", [P, 2, P], BF16)
        onescol = sb("onescol", [P, 1])
        headmask = sb("headmask", [P, P])
        causal = sb("causal", [P, 384])
        iota_i = sb("iota_i", [P, 1], I32)
        iota_f = sb("iota_f", [P, 4])
        epos_i = sb("epos_i", [P, UT], I32)
        epos = sb("epos", [P, UT])
        prio_i = sb("prio_i", [P, UT * E], I32)
        prio = sb("prio", [P, UT * E])
        turn = sb("turn", [P, 8])
        mtT = sb("mtT", [P, 250])
        tokW = sb("tokW", [P, D])
        ppW = sb("ppW", [32, D])
        ppT = sb("ppT", [32, S])
        ppR = sb("ppR", [32, 10])
        tokb = sb("tokb", [16, D])
        tf = sb("tf", [P, 3, D])
        tabs = sb("tabs", [P, 3, 3, D], BF16)
        w_enc1 = sb("w_enc1", [P, 2, P])
        w_enc2 = sb("w_enc2", [P, 2, P])
        bd0 = sb("bd0", [P, 2, P])
        v_b1 = sb("v_b1", [P, 1])
        v_b2 = sb("v_b2", [P, 2])
        v_ln0 = sb("v_ln0", [P, 2])
        rows0 = sb("rows0", [P, 2, D])
        bdg = sb("bdg", [P, 2, 2 * E])
        rowg = sb("rowg", [P, 2, E])
        b2col = sb("b2col", [P, 2, E])
        b1all = sb("b1all", [P, 2, E, 2])
        b1cur = sb("b1cur", [P, 2, 2])
        blnT = sb("blnT", [D, E])
        PK = 256 + 128 + 1
        pack = sb("pack", [P, 2, PK])
        wf = sb("wf", [P, 2, HID])
        w3 = sb("w3", [P, 2, 3, HID], BF16)
        bd1 = sb("bd1", [P, 4, P])
        ff = sb("ff", [P, 2 * HID + P])
        lvecs = sb("lvecs", [P, LAYERS, 6])
        lvec = sb("lvec", [P, 6])
        lrow = sb("lrow", [P, 2, D])
        rows1 = sb("rows1", [P, LAYERS, 2, D])

        psum_full = [sem(f"psum_full{b}") for b in range(8)]
        psum_free = [sem(f"psum_free{b}") for b in range(8)]
        tok_in = [sem(f"tok_in{g}") for g in range(G)]
        tab_in, enc_in, vec_in, l1_in = sem("tab_in"), sem("enc_in"), sem("vec_in"), sem("l1_in")
        attn_w_in, ff_w_in = sem("attn_w_in"), sem("ff_w_in")
        pack_in = [[sem(f"pack_in{m}{s}") for s in range(2)] for m in range(2)]
        out_done = sem("out_done")
        zeros_ready, consts_ready, ident_ready = sem("zeros_ready"), sem("consts_ready"), sem("ident_ready")
        pool_step, dve_step, act_step = sem("pool_step"), sem("dve_step"), sem("act_step")
        tables_ready, onehot_ready = sem("tables_ready"), sem("onehot_ready")
        tab_lhs_ready = sem("tab_lhs_ready")
        cen_ready, sq_ready, xn_ready = sem("cen_ready"), sem("sq_ready"), sem("xn_ready")
        frac_ready, cs_ready, hx_ready = sem("frac_ready"), sem("cs_ready"), sem("hx_ready")
        gap_ready, tanh_ready = sem("gap_ready"), sem("tanh_ready")
        w3_ready, split_ready, comb_ready = sem("w3_ready"), sem("split_ready"), sem("comb_ready")
        at_zero, b1_in = sem("at_zero"), sem("b1_in")
        acc_done = sem("acc_done")
        bias_added = sem("bias_added")
        negm_ready = sem("negm_ready")
        qe_ready, qn_ready = sem("qe_ready"), sem("qn_ready")

        block = ctx.enter_context(nc.Block())

        def full(eng, key, i=0):
            b, n, per = use[key]
            eng.wait_ge(psum_full[b], n + 1 + i * per if per else n + 1)

        def bank_free(key, i=0):
            b, n, per = use[key]
            if n or per:
                nc.tensor.wait_ge(psum_free[b], n + i * per if per else n)
            return bank[b]

        def made(ins, key):
            ins.then_inc(psum_full[use[key][0]], 1)

        def read(ins, key):
            ins.then_inc(psum_free[use[key][0]], 1)

        def ps(key):
            return bank[use[key][0]]

        def ln_no(k, u):
            return 2 * k + u + 1

        def gsl(t, g):
            return t[:, g * GC:(g + 1) * GC]

        def usl(t, u):
            return t[:, u * UC:(u + 1) * UC].rearrange("p (t d) -> p t d", d=D)

        def tiles(t, g):
            return gsl(t, g).rearrange("p (t d) -> p t d", d=D)

        def row(ap, n=E):
            return ap.unsqueeze(1).broadcast_to([P, n, D])

        def wide(ap, n, d=D):
            return ap.unsqueeze(2).broadcast_to([P, n, d])

        @block.sync
        def _(sp):
            sp.dma_start(mtT[:, :], a["move_tableT"]).then_inc(tab_in, 16)
            sp.dma_start(tokW[:, :], a["tok_WT"][0:P, :]).then_inc(tab_in, 16)
            sp.dma_start(ppW[:, :], a["tok_WT"][P:P + 32, :]).then_inc(tab_in, 16)
            sp.dma_start(ppT[:, :], a["pp_tableT"]).then_inc(tab_in, 16)
            sp.dma_start(tokb[0:10, :], a["tok_b"].partition_broadcast(10)).then_inc(tab_in, 16)
            for g in range(G):
                sl = slice(g * UC, (g + 1) * UC)
                sp.dma_start(tok_i[:, sl], a["x"][sl].partition_broadcast(P)).then_inc(tok_in[g], 16)
                sp.dma_start(pp_i[0:10, sl], a["itok"][sl].partition_broadcast(10)).then_inc(tok_in[g], 16)
            def packs(m):
                for s in range(2):
                    if m == 1:
                        full(sp, ("down", 0, s, G - 1), E // 2 - 1)
                    w = PK if m == 0 else PK - 1
                    sp.dma_start(pack[:, s, 0:w], a[f"pack{m}"][s]).then_inc(pack_in[m][s], 16)
                with sp.Fori(0, E // 2 - 1) as i:
                    for s in range(2):
                        full(sp, ("down", m, s, G - 1), i)
                        src = a[f"pack{m}"][bass.ds(2 * i + 2 + s, 1)].rearrange("e p c -> (e p) c")
                        sp.dma_start(pack[:, s, 0:w], src).then_inc(pack_in[m][s], 16)

            def ff_weights(src_ff, src_w2):
                for h in range(2):
                    sp.dma_start(ff[h * D:(h + 1) * D, h * HID:(h + 1) * HID], src_ff).then_inc(ff_w_in, 16)
                sp.dma_start(ff[:, 2 * HID:2 * HID + P].rearrange("p (c d) -> p c d", c=2),
                             src_w2.rearrange("(c p) d -> p c d", c=2)).then_inc(ff_w_in, 16)

            def attn_weights(src):
                for h in range(2):
                    sp.dma_start(bd1[h * D:(h + 1) * D, :, h * D:(h + 1) * D], src).then_inc(attn_w_in, 16)

            sp.dma_start(w1all, a["w1all"]).then_inc(b1_in, 16)
            sp.dma_start(blnT[:, :], a["blnT"]).then_inc(b1_in, 16)
            sp.wait_ge(zeros_ready, 1)
            packs(0)
            attn_weights(a["l1_attn"][0].rearrange("d (w n) -> d w n", w=4))
            ff_weights(a["l1_W1"][0], a["l1_W2"][0])
            with sp.Fori(0, LAYERS - 1) as i:
                full(sp, ("m", G - 1), i)
                attn_weights(a["l1_attn"][bass.ds(i + 1, 1)].rearrange("l d (w n) -> (l d) w n", w=4))
                full(sp, ("fdown", G - 1), i)
                ff_weights(a["l1_W1"][bass.ds(i + 1, 1)].rearrange("l d n -> (l d) n"),
                           a["l1_W2"][bass.ds(i + 1, 1)].rearrange("l d n -> (l d) n"))
            packs(1)
            for g in range(G):
                b, n, _ = use[("at", 1, g)]
                sp.wait_ge(psum_free[b], n + 1)
                for h in range(2):
                    for jb in range(2):
                        dst = out[4 * g + 2 * h + jb].rearrange("(j p) d -> p j d", p=P)
                        src = gsl(Hs, g).rearrange("p (b j k d) -> p b j k d", b=2, j=2, k=2)[:, jb, :, h, :]
                        sp.dma_start(dst, src).then_inc(out_done, 16)
            sp.wait_ge(out_done, 16 * B)

        @block.gpsimd
        def _(pool):
            step = Chain(pool, pool_step)
            gp = nc.gpsimd
            gp.memset(bd0[:, :, :], 0.0)
            gp.memset(bdg[:, :, :], 0.0)
            gp.memset(w_enc1[:, :, :], 0.0)
            gp.memset(w_enc2[:, :, :], 0.0)
            gp.memset(ff[:, :], 0.0)
            gp.memset(comb3[:, :, :, :], 0.0)
            gp.memset(CT[:, :], 0.0)
            gp.memset(onescol[:, :], 1.0)
            gp.memset(bd1[:, :, :], 0.0).then_inc(zeros_ready, 1)
            step(gp.iota(iota_i[:, :], [[0, 1]], base=0, channel_multiplier=1))
            step(gp.iota(epos_i[:, :], [[0, 4], [P, 2], [0, 2]], base=1, channel_multiplier=1))
            step(gp.iota(prio_i[:, :], [[0, UT], [-1, E]], base=E, channel_multiplier=0))
            step(gp.memset(ident[:, :], 0.0))
            step(gp.memset(select[:, :, :], 0.0))
            step(gp.memset(headmask[:, :], 1.0))
            step(gp.memset(causal[:, :], 1.0))
            step.settle()
            gp.affine_select(out=ident[:, :], in_=ident[:, :], compare_op=ALU.not_equal, fill=1.0, base=0,
                             pattern=[[-1, P]], channel_multiplier=1).then_inc(ident_ready, 1)
            hm = headmask[:, :].rearrange("p (b c) -> p b c", c=DH)
            step(gp.affine_select(out=hm, in_=hm, compare_op=ALU.is_ge, fill=0.0, base=0,
                                  pattern=[[-DH, P // DH], [0, DH]], channel_multiplier=1))
            step.settle()
            step(gp.affine_select(out=hm, in_=hm, compare_op=ALU.is_ge, fill=0.0, base=DH - 1,
                                  pattern=[[DH, P // DH], [0, DH]], channel_multiplier=-1))
            for c in (0, 2):
                tri = causal[:, c * P:(c + 1) * P]
                step(gp.affine_select(out=tri, in_=tri, compare_op=ALU.is_ge, fill=0.0, base=0,
                                      pattern=[[1, P]], channel_multiplier=-1))
            step(gp.tensor_copy(iota_f[:, 0:1], iota_i[:, :]))
            step(gp.tensor_copy(epos[:, :], epos_i[:, :]))
            pool.wait_ge(ident_ready, 1)
            step(gp.tensor_copy(identb[:, :], ident[:, :]))
            gp.tensor_copy(prio[:, :], prio_i[:, :]).then_inc(consts_ready, 1)
            for part in range(3):
                sel = select[:, :, :].rearrange("p e (h d) -> p e h d", h=2)
                step(gp.affine_select(out=sel, in_=sel, compare_op=ALU.not_equal, fill=1.0, base=-16 * part,
                                      pattern=[[-1, E], [-E, 2], [0, D]], channel_multiplier=1))
                step.settle()

            pool.wait_ge(vec_in, VEC_DMAS * 16)
            for u in range(U):
                pool.wait_ge(xn_ready, ln_no(0, u))
                step(gp.tensor_tensor(usl(Hs, u), usl(Hs, u), usl(Xs, u), ALU.add))
                step.settle()
                gp.tensor_tensor(usl(Hs, u), usl(Hs, u), row(rows0[:, 1, :], UT), ALU.add).then_inc(hx_ready, 1)

            def moe_weights(m):
                for g in range(G):
                    full(pool, ("gate", m, g))
                    gp.memset(gsl(XT, g), 0.0).then_inc(at_zero, 1)
                with pool.Fori(0, E // 2) as i:
                    step.enter(i, 2 * 7)
                    for s in range(2):
                        pool.wait_ge(pack_in[m][s], 16 + 16 * i)
                        pool.wait_ge(psum_full[3], use[("up", m, s, G - 1, 1, 1)][1] + 1 - 8 + i * 8)
                        gcol = pack[:, s, 384:385] if m == 0 else onescol[:, :]
                        wide_g = gcol.broadcast_to([P, HID])
                        step(gp.tensor_tensor(wf[:, 0, :], pack[:, s, 0:HID], wide_g, ALU.mult))
                        e = bass.ds(2 * i + s, 1)
                        step(gp.tensor_copy(b1cur[:, s, :], b1all[:, m, e, :].rearrange("p e c -> p (e c)")))
                        step(gp.tensor_copy(selcur[:, s, :], select[:, e, :].rearrange("p e c -> p (e c)")))
                        step(gp.tensor_tensor(w3[:, s, 0, :], pack[:, s, 0:HID], wide_g, ALU.mult))
                        step.settle()
                        step(gp.tensor_tensor(w3[D:P, s, 2, :], pack[D:P, s, 0:HID],
                                              (pack[D:P, s, 384:385] if m == 0 else onescol[D:P, :]).broadcast_to(
                                                  [D, HID]), ALU.mult))
                        step.settle()
                        step(gp.tensor_tensor(wf[:, 1, :], wf[:, 0, :], w3[:, s, 0, :], ALU.subtract))
                        step(gp.tensor_tensor(w3[:, s, 1, :], wf[:, 0, :], w3[:, s, 0, :], ALU.subtract))
                        step.settle()
                        gp.tensor_tensor(w3[0:D, s, 2, :], wf[0:D, 1, :], w3[0:D, s, 1, :],
                                         ALU.subtract).then_inc(w3_ready, 1)
                        pool.wait_ge(w3_ready, E * m + 2 * i + s + 1)
                    step.leave(E // 2)

            moe_weights(0)
            pool.wait_ge(l1_in, L1_DMAS * 16)
            with pool.Fori(0, LAYERS) as i:
                step.enter(i, 1)
                step(gp.tensor_copy(lrow[:, :, :].rearrange("p w d -> p (w d)"),
                                    rows1[:, bass.ds(i, 1), :, :].rearrange("p l w d -> p (l w d)")))
                step.settle()
                step.leave(LAYERS)
                for w in range(2):
                    for u in range(U):
                        pool.wait_ge(cen_ready, ln_no(5 + w, u) + 4 * i)
                        gp.tensor_tensor(usl(Xs, u), usl(Xs, u), row(lrow[:, w, :], UT), ALU.add).then_inc(bias_added, 1)
                pool.wait_ge(bias_added, 4 * i + 4)
            moe_weights(1)

        @block.scalar
        def _(act):
            ac = nc.scalar
            step = Chain(act, act_step)

            act.wait_ge(zeros_ready, 1)
            for h in range(2):
                hs = slice(h * D, (h + 1) * D)
                act.dma_start(w_enc1[hs, h, :], a["enc1"]).then_inc(enc_in, 16)
                act.dma_start(w_enc2[hs, h, :], a["enc2"][h]).then_inc(enc_in, 16)
                act.dma_start(bd0[hs, 0, hs], a["Wv"]).then_inc(enc_in, 16)
                act.dma_start(bd0[hs, 1, hs], a["Wo"]).then_inc(enc_in, 16)
                act.dma_start(bdg[hs, 0, h * E:(h + 1) * E], a["Wr"]).then_inc(enc_in, 16)
                act.dma_start(bdg[hs, 1, h * E:(h + 1) * E], a["WgT"]).then_inc(enc_in, 16)
                for n in range(2):
                    act.dma_start(v_b2[hs, n:n + 1], a["b_enc2"][n]).then_inc(vec_in, 16)
                    act.dma_start(v_ln0[hs, n:n + 1], a["ln0"][n]).then_inc(vec_in, 16)
                act.dma_start(v_b1[hs, :], a["b_enc1"][h]).then_inc(vec_in, 16)
            for n in range(2):
                act.dma_start(rows0[:, n, :], a["rows0"][n].partition_broadcast(P)).then_inc(vec_in, 16)
                act.dma_start(rowg[:, n, :], a["rowg"][n].partition_broadcast(P)).then_inc(vec_in, 16)
                for h in range(2):
                    act.dma_start(b2col[h * D:(h + 1) * D, n, :], a["b2T"][n]).then_inc(vec_in, 16)
            act.dma_start(b1all[:, :, :, :], a["b1all"]).then_inc(vec_in, 16)
            for h in range(2):
                act.dma_start(lvecs[h * D:(h + 1) * D, :, 0:4], a["l1_ln"]).then_inc(l1_in, 16)
            act.dma_start(lvecs[:, :, 4:6], a["l1_b1"]).then_inc(l1_in, 16)
            act.dma_start(rows1[:, :, :, :].rearrange("p l w d -> p (l w d)"),
                          a["l1_rows"].partition_broadcast(P)).then_inc(l1_in, 16)

            def square(k, u, i=0):
                act.wait_ge(cen_ready, ln_no(k, u) + i)
                ac.activation(usl(Sq, u), usl(Cen, u), ACT.Square).then_inc(sq_ready, 1)

            def xt_out(t, g, i=0, scale=1.0, bias=0.0):
                full(act, ("xt", t, g), i)
                src = ps(("xt", t, g))
                if t in (0, 2, 3, 12):
                    read2 = ac.copy(gsl(XT, g), src[:, :])
                else:
                    read2 = ac.activation(gsl(XT, g), src[:, :], ACT.Identity, scale=scale, bias=bias)
                read2.then_inc(psum_free[use[("xt", t, g)][0]], 1)

            for g in range(G):
                full(act, ("embed", g))
                read(ac.copy(gsl(Hs, g), ps(("embed", g))[:, :]), ("embed", g))
            for u in range(U):
                square(0, u)
                for g in (2 * u, 2 * u + 1):
                    xt_out(0, g)
            act.wait_ge(vec_in, VEC_DMAS * 16)
            for g in range(G):
                for h in range(2):
                    full(act, ("enc1", g, h))
                    if g >= 2 and h == 0:
                        full(act, ("enc2", g - 2, 1, 1))
                    read(ac.activation(Gk[:, g % 2, h, :], ps(("enc1", g, h))[:, :], ACT.Gelu,
                                       bias=v_b1[:, 0:1]), ("enc1", g, h))
                for kind in range(2):
                    for h in range(2):
                        key = ("enc2", g, kind, h)
                        full(act, key)
                        n = 2 * kind + h
                        read(ac.activation(Ph[:, g, n * GC:(n + 1) * GC], ps(key)[:, :], ACT.Tanh,
                                           bias=v_b2[:, kind:kind + 1]), key)
            for g in range(G):
                act.wait_ge(frac_ready, g + 1)
                ac.activation(Ph[:, g, :], Ph[:, g, :], ACT.Sin, scale=TWO_PI).then_inc(cs_ready, 1)
                if g >= 1:
                    full(act, ("ret", g - 1))
                    read(ac.copy(gsl(Xn, g - 1), ps(("ret", g - 1))[:, :]), ("ret", g - 1))
            full(act, ("ret", G - 1))
            read(ac.copy(gsl(Xn, G - 1), ps(("ret", G - 1))[:, :]), ("ret", G - 1))
            for u in range(U):
                square(1, u)
                for g in (2 * u, 2 * u + 1):
                    xt_out(1, g, 0, v_ln0[:, 0:1], v_ln0[:, 1:2])

            def moe(m):
                k, t = (2, 2) if m == 0 else (13, 12)
                for u in range(U):
                    square(k, u)
                    for g in (2 * u, 2 * u + 1):
                        xt_out(t, g)
                for u in range(U):
                    if m == 0:
                        square(3, u)
                    act.wait_ge(gap_ready, 2 * m + u + 1)
                    ac.activation(rt[:, 6 + u, :], rt[:, 4 + u, :], ACT.Tanh, scale=0.5).then_inc(tanh_ready, 1)
                for g in range(G):
                    for kk in range(2):
                        key = ("xs", m, g, kk)
                        full(act, key)
                        dst = Xs2[:, kk, g * UC:(g + 1) * UC]
                        read(ac.copy(dst, ps(key)[:, :].bitcast(BF16)), key)
                    key = ("ct", m, g)
                    full(act, key)
                    read(ac.copy(CT[0:48, g * GC:(g + 1) * GC], ps(key)[0:48, :].bitcast(BF16)[:, 0:GC]), key)
                func = ACT.Gelu if m == 0 else ACT.Relu
                with act.Fori(0, E // 2) as i:
                    for s in range(2):
                        act.wait_ge(w3_ready, E * m + s + 1 + 2 * i)
                        for g in range(G):
                            n = 4 * s + g
                            for hc in range(2):
                                for h in range(2):
                                    key = ("up", m, s, g, hc, h)
                                    full(act, key, i)
                                    ins = ac.activation(Hd[:, n % 2, hc, h, :], ps(key)[:, :], func,
                                                        bias=b1cur[:, s, hc:hc + 1])
                                    read(ins, key)
                            b, c, per = use[("down", m, s, g)]
                            act.wait_ge(psum_free[b], c + i * per)
                            key = ("wb", m, s, g)
                            full(act, key, i)
                            read(ac.copy(Wb[:, n % 2, :], ps(key)[:, :]), key)

            moe(0)
            for u in range(U):
                square(4, u)
            act.wait_ge(l1_in, L1_DMAS * 16)
            scale = float(DH) ** -0.25
            with act.Fori(0, LAYERS) as i:
                step.enter(i, 1)
                step(ac.copy(lvec[:, :], lvecs[:, bass.ds(i, 1), :].rearrange("p l o -> p (l o)")))
                step.settle()
                step.leave(LAYERS)

                def vec(n):
                    return lvec[:, n:n + 1]

                def v_out(g):
                    full(act, ("v", g), i)
                    read(ac.copy(Vt[:, g, :], ps(("v", g))[:, :]), ("v", g))

                def kexp(g):
                    act.wait_ge(negm_ready, 4 * i + g + 1)
                    for jb in range(2):
                        c = slice(jb * S, (jb + 1) * S)
                        ins = ac.activation(Ke[:, g, c], ps(("k", g))[:, c], ACT.Exp, scale=scale,
                                            bias=ksm[:, g, 1, jb:jb + 1], accum_out=ksm[:, g, 2, jb:jb + 1])
                    read(ins, ("k", g))

                def qexp(g):
                    b, n, per = use[("q", g)]
                    act.wait_ge(psum_free[b], n + 1 + i * per)
                    ac.activation(Qe[:, g, :], Qe[:, g, :], ACT.Exp, scale=scale).then_inc(qe_ready, 1)

                def kt_out(g):
                    full(act, ("kt", g), i)
                    read(ac.copy(Kt[:, g % 2, :], ps(("kt", g))[:, :]), ("kt", g))

                def qt_out(g):
                    full(act, ("qt", g), i)
                    read(ac.copy(Qf[:, g % 2, :], ps(("qt", g))[:, :]), ("qt", g))

                square(5, 0, 4 * i)
                xt_out("attn", 0, i, vec(0), vec(1))
                xt_out("attn", 1, i, vec(0), vec(1))
                square(5, 1, 4 * i)
                v_out(0)
                v_out(1)
                xt_out("attn", 2, i, vec(0), vec(1))
                xt_out("attn", 3, i, vec(0), vec(1))
                kexp(0)
                qexp(0)
                kt_out(0)
                kexp(1)
                qexp(1)
                v_out(2)
                qt_out(0)
                kt_out(1)
                kexp(2)
                qexp(2)
                v_out(3)
                qt_out(1)
                kt_out(2)
                kexp(3)
                qexp(3)
                qt_out(2)
                kt_out(3)
                qt_out(3)

                def hidden(g):
                    for hc in range(2):
                        for h in range(2):
                            key = ("fup", g, hc, h)
                            full(act, key, i)
                            read(ac.activation(Hd[:, g % 2, hc, h, :], ps(key)[:, :], ACT.Gelu,
                                               bias=vec(4 + hc)), key)

                square(6, 0, 4 * i)
                xt_out("ffn", 0, i, vec(2), vec(3))
                xt_out("ffn", 1, i, vec(2), vec(3))
                square(6, 1, 4 * i)
                hidden(0)
                hidden(1)
                xt_out("ffn", 2, i, vec(2), vec(3))
                xt_out("ffn", 3, i, vec(2), vec(3))
                hidden(2)
                hidden(3)
                b, n, per = use[("fup", G - 1, 1, 1)]
                act.wait_ge(psum_free[b], n + 1 + i * per)
            moe(1)

        @block.vector
        def _(dve):
            step = Chain(dve, dve_step)
            ve = nc.vector

            dve.wait_ge(tab_in, 5 * 16)
            step(ve.tensor_scalar(mtT[:, :], mtT[:, :], 0.0, None, ALU.max))
            step(ve.tensor_copy(ppR[:, 0:9], ppT[:, 0:249:31]))
            ve.tensor_copy(ppR[:, 9:10], ppT[:, 255:256]).then_inc(tab_lhs_ready, 1)
            dve.wait_ge(consts_ready, 1)
            step(ve.tensor_scalar(iota_f[:, 1:2], iota_f[:, 0:1], 128.0, None, ALU.add))
            step(ve.tensor_scalar(iota_f[:, 2:3], iota_f[:, 0:1], -1.0, None, ALU.add))
            step(ve.tensor_scalar(turn[:, 1:2], iota_f[:, 0:1], 64.0, -64.0, ALU.is_ge, ALU.mult))
            step.settle()
            step(ve.tensor_tensor(turn[:, 2:3], iota_f[:, 0:1], turn[:, 1:2], ALU.add))
            step(ve.tensor_scalar(turn[:, 3:4], turn[:, 1:2], 1.0 / 256, 0.25, ALU.mult, ALU.add))
            step.settle()
            step(ve.tensor_scalar(turn[:, 4:5], turn[:, 2:3], 16.0, 0.5, ALU.is_ge, ALU.mult))
            step(ve.tensor_scalar(turn[:, 5:6], turn[:, 2:3], 32.0, None, ALU.is_ge))
            step(ve.tensor_scalar(turn[:, 6:7], turn[:, 2:3], 48.0, 2.0, ALU.is_ge, ALU.mult))
            step.settle()
            step(ve.tensor_tensor(turn[:, 7:8], turn[:, 4:5], turn[:, 5:6], ALU.add))
            step.settle()
            step(ve.scalar_tensor_tensor(turn[:, 0:1], turn[:, 6:7], 0.5, turn[:, 7:8], ALU.add, ALU.add))
            step(ve.tensor_scalar(epos[:, :], epos[:, :], EPS * PHASES, None, ALU.mult))
            for n, (rows, add) in enumerate(((P, None), (122, None), (10, tokb))):
                full(dve, ("table", n))
                src = ps(("table", n))[0:rows, 0:D]
                if add is None:
                    ins = ve.tensor_copy(tf[0:rows, 0, :], src)
                else:
                    ins = ve.tensor_tensor(tf[0:rows, 0, :], src, add[0:rows, :], ALU.add)
                read(ins, ("table", n))
                dve.wait_ge(psum_free[2 + n], 1)
                step(ve.tensor_copy(tabs[0:rows, n, 0, :], tf[0:rows, 0, :]))
                step.settle()
                step(ve.tensor_tensor(tf[0:rows, 1, :], tf[0:rows, 0, :], tabs[0:rows, n, 0, :], ALU.subtract))
                step.settle()
                step(ve.tensor_copy(tabs[0:rows, n, 1, :], tf[0:rows, 1, :]))
                step.settle()
                ins = ve.tensor_tensor(tabs[0:rows, n, 2, :], tf[0:rows, 1, :], tabs[0:rows, n, 1, :], ALU.subtract)
                if n < 2:
                    step(ins)
                    step.settle()
                else:
                    ins.then_inc(tables_ready, 1)

            dve.wait_ge(vec_in, VEC_DMAS * 16)
            full(dve, ("b1", 0))
            read(ve.tensor_tensor(b1all[:, 0, :, :].rearrange("p e c -> p (e c)"), ps(("b1", 0))[:, 0:2 * E],
                                  b1all[:, 0, :, :].rearrange("p e c -> p (e c)"), ALU.add), ("b1", 0))

            def one_hot(g):
                dve.wait_ge(tok_in[g], 32)
                if g >= 2:
                    full(dve, ("embed", g - 2))
                sl = slice(g * UC, (g + 1) * UC)
                step(ve.tensor_scalar(onehot[:, g % 2, 0, :], tok_i[:, sl], iota_f[:, 0:1], None, ALU.is_equal))
                step(ve.tensor_scalar(onehot[0:122, g % 2, 1, :], tok_i[0:122, sl], iota_f[0:122, 1:2], None,
                                      ALU.is_equal))
                step(ve.tensor_scalar(ppstep[0:10, g % 2, :], pp_i[0:10, sl], 1.0, -1.0, ALU.min, ALU.mult))
                step.settle()
                ve.tensor_scalar(onehot[0:10, g % 2, 2, :], ppstep[0:10, g % 2, :], 8.0, iota_f[0:10, 2:3],
                                 ALU.min, ALU.is_equal).then_inc(onehot_ready, 1)

            def layernorm(k, u, src, dst, i=0, eps=EPS):
                st = stat[:, u]
                step(ve.tensor_reduce(st[:, 0, :], usl(src, u), AX_X, ALU.add))
                step.settle()
                step(ve.tensor_scalar(st[:, 1, :], st[:, 0, :], -1.0 / D, None, ALU.mult))
                step.settle()
                ve.tensor_tensor(usl(Cen, u), usl(src, u), wide(st[:, 1, :], UT), ALU.add).then_inc(cen_ready, 1)
                dve.wait_ge(sq_ready, ln_no(k, u) + i)
                step(ve.tensor_reduce(st[:, 2, :], usl(Sq, u), AX_X, ALU.add))
                step.settle()
                if eps is epos:
                    step(ve.scalar_tensor_tensor(st[:, 3, :], st[:, 2, :], 1.0 / D, epos[:, :], ALU.mult, ALU.add))
                else:
                    step(ve.tensor_scalar(st[:, 3, :], st[:, 2, :], 1.0 / D, eps, ALU.mult, ALU.add))
                step.settle()
                step(ve.tensor_scalar(st[:, 5, :].bitcast(I32), st[:, 3, :].bitcast(I32), 1, None,
                                      ALU.logical_shift_right))
                step.settle()
                step(ve.tensor_scalar(st[:, 4, :].bitcast(I32), st[:, 5, :].bitcast(I32), -1.0, float(MAGIC),
                                      ALU.mult, ALU.add))
                step.settle()
                for _ in range(NEWTON):
                    step(ve.tensor_tensor(st[:, 5, :], st[:, 4, :], st[:, 4, :], ALU.mult))
                    step.settle()
                    step(ve.scalar_tensor_tensor(st[:, 5, :], st[:, 5, :], -0.5, st[:, 3, :], ALU.mult, ALU.mult))
                    step.settle()
                    step(ve.scalar_tensor_tensor(st[:, 4, :], st[:, 5, :], 1.5, st[:, 4, :], ALU.add, ALU.mult))
                    step.settle()
                ve.tensor_tensor(usl(dst, u), usl(Cen, u), wide(st[:, 4, :], UT), ALU.mult).then_inc(xn_ready, 1)

            for g in range(G):
                one_hot(g)
            for u in range(U):
                dve.wait_ge(psum_free[0], u + 1)
                dve.wait_ge(psum_free[1], u + 1)
                layernorm(0, u, Hs, Xs)

            step.settle()
            for g in range(G):
                for n in range(4):
                    b, c, _ = use[("enc2", g, n // 2, n % 2)]
                    dve.wait_ge(psum_free[b], c + 1)
                step(ve.tensor_scalar(Ph[:, g, :], Ph[:, g, :], turn[:, 0:1], turn[:, 3:4], ALU.mult, ALU.add))
                step.settle()
                step(ve.tensor_scalar(Turn[:, :], Ph[:, g, :], ROUND, -ROUND, ALU.add, ALU.add))
                step.settle()
                ve.tensor_tensor(Ph[:, g, :], Ph[:, g, :], Turn[:, :], ALU.subtract).then_inc(frac_ready, 1)
                dve.wait_ge(frac_ready, g + 1)
            dve.wait_ge(vec_in, VEC_DMAS * 16)
            for g in range(G):
                full(dve, ("v0", g))
                read(ve.tensor_tensor(Vt[:, g, :].rearrange("p (t d) -> p t d", d=D),
                                      ps(("v0", g))[:, :].rearrange("p (t d) -> p t d", d=D),
                                      row(rows0[:, 0, :]), ALU.add), ("v0", g))
                for h in range(2):
                    for jb in range(2):
                        key = ("score", g, h, jb)
                        full(dve, key)
                        if g >= 2 and h == 0 and jb == 0:
                            full(dve, ("ret", g - 2))
                        read(ve.tensor_tensor(Sc[:, g % 2, 2 * h + jb, :], ps(key)[:, 0:384], causal[:, :],
                                              ALU.mult), key)
            for u in range(U):
                dve.wait_ge(psum_free[6], use[("ret", 2 * u)][1] + 1)
                dve.wait_ge(psum_free[7], use[("ret", 2 * u + 1)][1] + 1)
                layernorm(1, u, Xn, Xn, 0, epos)
            for g in range(G):
                full(dve, ("o0", g))
                dve.wait_ge(hx_ready, g // 2 + 1)
                read(ve.tensor_tensor(gsl(Hs, g), gsl(Hs, g), ps(("o0", g))[:, :], ALU.add), ("o0", g))

            def route_unit(m, u):
                lg, eq, f1, f2, t1, t2 = (route[:, n, :].rearrange("p (t e) -> p t e", e=E) for n in range(6))
                pr = prio[:, :].rearrange("p (t e) -> p t e", e=E)
                for g in (2 * u, 2 * u + 1):
                    full(dve, ("gate", m, g))
                    ins = ve.tensor_tensor(lg[:, (g % 2) * E:(g % 2 + 1) * E, :],
                                           ps(("gate", m, g))[:, 0:8 * E].rearrange("p (t e) -> p t e", e=E),
                                           rowg[:, m, :].unsqueeze(1).broadcast_to([P, E, E]), ALU.add)
                    read(ins, ("gate", m, g))
                    dve.wait_ge(psum_free[4 + g % 2], use[("gate", m, g)][1] + 1)

                def best(scores, top, first):
                    step(ve.tensor_reduce(top, scores, AX_X, ALU.max))
                    step.settle()
                    step(ve.tensor_tensor(eq, scores, wide(top, UT, E), ALU.is_equal))
                    step.settle()
                    step(ve.tensor_tensor(t1, eq, pr, ALU.mult))
                    step.settle()
                    step(ve.tensor_reduce(rt[:, 2, :], t1, AX_X, ALU.max))
                    step.settle()
                    step(ve.tensor_tensor(first, t1, wide(rt[:, 2, :], UT, E), ALU.is_equal))
                    step.settle()

                best(lg, rt[:, 0, :], f1)
                step(ve.scalar_tensor_tensor(route[:, 5, :], route[:, 2, :], -3.0e38, route[:, 0, :],
                                             ALU.mult, ALU.add))
                step.settle()
                best(t2, rt[:, 1, :], f2)
                ve.tensor_tensor(rt[:, 4 + u, :], rt[:, 0, :], rt[:, 1, :], ALU.subtract).then_inc(gap_ready, 1)
                dve.wait_ge(tanh_ready, 2 * m + u + 1)
                step(ve.tensor_scalar(rt[:, 2, :], rt[:, 6 + u, :], 0.5, 0.5, ALU.mult, ALU.add))
                step(ve.tensor_scalar(rt[:, 3, :], rt[:, 6 + u, :], -0.5, 0.5, ALU.mult, ALU.add))
                step.settle()
                step(ve.tensor_tensor(t1, f1, wide(rt[:, 2, :], UT, E), ALU.mult))
                step(ve.tensor_tensor(t2, f2, wide(rt[:, 3, :], UT, E), ALU.mult))
                step.settle()
                cs = slice(8 * u, 8 * u + 8)
                step(ve.tensor_tensor(comb[:, cs, :].rearrange("p a (h e) -> p (a h) e", e=E), t1, t2, ALU.add))
                step.settle()
                step(ve.tensor_copy(comb3[:, cs, 0, :], comb[:, cs, :]))
                step.settle()
                step(ve.tensor_tensor(combr[:, cs, :], comb[:, cs, :], comb3[:, cs, 0, :], ALU.subtract))
                step.settle()
                step(ve.tensor_copy(comb3[:, cs, 1, :], combr[:, cs, :]))
                step.settle()
                ve.tensor_tensor(comb3[:, cs, 2, :], combr[:, cs, :], comb3[:, cs, 1, :],
                                 ALU.subtract).then_inc(comb_ready, 1)
                dve.wait_ge(comb_ready, 2 * m + u + 1)

            def split_unit(m, u):
                dve.wait_ge(xn_ready, ln_no(3 if m == 0 else 13, u))
                x3 = X3[:, u * UT:(u + 1) * UT, :, :]
                step(ve.tensor_copy(x3[:, :, 1, :], usl(Xn, u)))
                step.settle()
                step(ve.tensor_tensor(usl(Sq, u), usl(Xn, u), x3[:, :, 1, :], ALU.subtract))
                step.settle()
                step(ve.tensor_copy(x3[:, :, 0, :], usl(Sq, u)))
                step.settle()
                ve.tensor_tensor(x3[:, :, 2, :], usl(Sq, u), x3[:, :, 0, :], ALU.subtract).then_inc(split_ready, 1)
                dve.wait_ge(split_ready, 2 * m + u + 1)

            def experts(m):
                dve.wait_ge(at_zero, G * (m + 1))
                with dve.Fori(0, E // 2) as i:
                    for n in range(8):
                        s, g = n // 4, n % 4
                        key = ("down", m, s, g)
                        b, c, per = use[("wb", m, s, g)]
                        dve.wait_ge(psum_free[b], c + 1 + i * per)
                        full(dve, key, i)
                        b2 = b2col[:, m, bass.ds(2 * i + s, 1)]
                        read(ve.scalar_tensor_tensor(Tmp[:, :], ps(key)[:, :], b2, Wb[:, n % 2, :], ALU.add,
                                                     ALU.mult), key)
                        b, c, per = use[key]
                        dve.wait_ge(psum_free[b], c + 1 + i * per)
                        ve.tensor_tensor(gsl(XT, g), gsl(XT, g), Tmp[:, :], ALU.add).then_inc(acc_done, 1)
                        dve.wait_ge(acc_done, E * G * m + 8 * i + n + 1)
                for g in range(G):
                    key = ("at", m, g)
                    full(dve, key)
                    read(ve.tensor_tensor(gsl(Hs, g), gsl(Hs, g), ps(key)[:, :], ALU.add), key)

            for u in range(U):
                dve.wait_ge(psum_free[0], use[("o0", 2 * u)][1] + 1)
                dve.wait_ge(psum_free[1], use[("o0", 2 * u + 1)][1] + 1)
                layernorm(2, u, Hs, Xs)
            for u in range(U):
                dve.wait_ge(xn_ready, ln_no(2, u))
                layernorm(3, u, Xs, Xn)
                split_unit(0, u)
                route_unit(0, u)
            experts(0)

            for u in range(U):
                for g in (2 * u, 2 * u + 1):
                    b, c, _ = use[("at", 0, g)]
                    dve.wait_ge(psum_free[b], c + 1)
                layernorm(4, u, Hs, Xs)
            dve.wait_ge(xn_ready, ln_no(4, 1))
            with dve.Fori(0, LAYERS) as i:
                step.enter(i, L1_STEPS)

                def keys_max(g):
                    full(dve, ("k", g), i)
                    step(ve.tensor_reduce(ksm[:, g, 0, :], ps(("k", g))[:, :].rearrange("p (b t) -> p b t", b=2),
                                          AX_X, ALU.max))
                    step.settle()
                    ve.tensor_scalar(ksm[:, g, 1, :], ksm[:, g, 0, :], -(float(DH) ** -0.25), None,
                                     ALU.mult).then_inc(negm_ready, 1)

                def queries_max(g):
                    full(dve, ("q", g), i)
                    q = ps(("q", g))[:, :].rearrange("p (n d) -> p n d", d=DH)
                    step(ve.tensor_reduce(small[:, g, 0, :], q, AX_X, ALU.max))
                    step.settle()
                    ins = ve.tensor_tensor(Qe[:, g, :].rearrange("p (n d) -> p n d", d=DH), q,
                                           wide(small[:, g, 0, :], D, DH), ALU.subtract)
                    read(ins, ("q", g))

                def queries_norm(g):
                    dve.wait_ge(qe_ready, 4 * i + g + 1)
                    q = Qe[:, g, :].rearrange("p (n d) -> p n d", d=DH)
                    step(ve.tensor_reduce(small[:, g, 1, :], q, AX_X, ALU.add))
                    step.settle()
                    step(ve.reciprocal(small[:, g, 2, :], small[:, g, 1, :]))
                    step.settle()
                    ve.tensor_tensor(q, q, wide(small[:, g, 2, :], D, DH), ALU.mult).then_inc(qn_ready, 1)

                def context_out(g):
                    full(dve, ("ctx", g), i)
                    ins = ve.tensor_tensor(Cm[:, g % 2, :, :], ps(("ctx", g))[:, 0:S].rearrange(
                        "p (b n) -> p b n", b=2), headmask[:, :].unsqueeze(1).broadcast_to([P, 2, P]), ALU.mult)
                    read(ins, ("ctx", g))

                def mix_out(g):
                    b, n, per = use[("k", g)]
                    dve.wait_ge(psum_free[b], n + 1 + i * per)
                    step(ve.reciprocal(ksm[:, g, 3, :], ksm[:, g, 2, :]))
                    step.settle()
                    full(dve, ("m", g), i)
                    for jb in range(2):
                        ins = ve.tensor_scalar(Mm[:, g % 2, jb, :], ps(("m", g))[:, jb * P:(jb + 1) * P],
                                               ksm[:, g, 3, jb:jb + 1], None, ALU.mult)
                    read(ins, ("m", g))

                def add_out(key, g, w):
                    full(dve, key, i)
                    dve.wait_ge(bias_added, 4 * i + 2 * w + g // 2 + 1)
                    read(ve.tensor_tensor(gsl(Xs, g), gsl(Xs, g), ps(key)[:, :], ALU.add), key)

                def added(key):
                    b, n, per = use[key]
                    dve.wait_ge(psum_free[b], n + 1 + i * per)

                layernorm(5, 0, Xs, Xn, 4 * i)
                layernorm(5, 1, Xs, Xn, 4 * i)
                for g in (0, 1):
                    keys_max(g)
                    queries_max(g)
                queries_norm(0)
                keys_max(2)
                queries_max(2)
                context_out(0)
                queries_norm(1)
                mix_out(0)
                keys_max(3)
                queries_max(3)
                context_out(1)
                add_out(("o", 0), 0, 0)
                queries_norm(2)
                mix_out(1)
                context_out(2)
                add_out(("o", 1), 1, 0)
                queries_norm(3)
                mix_out(2)
                context_out(3)
                add_out(("o", 2), 2, 0)
                mix_out(3)
                add_out(("o", 3), 3, 0)
                added(("o", 1))
                layernorm(6, 0, Xs, Xn, 4 * i)
                added(("o", 3))
                layernorm(6, 1, Xs, Xn, 4 * i)
                for g in range(G):
                    add_out(("fdown", g), g, 1)
                for g in (2, 3):
                    added(("fdown", g))
                step.leave(LAYERS)
            for u in range(U):
                step(ve.tensor_tensor(usl(Hs, u), usl(Hs, u), usl(Xs, u), ALU.add))
                step.settle()

            for u in range(U):
                layernorm(13, u, Hs, Xn)
            for u in range(U):
                split_unit(1, u)
                route_unit(1, u)
            experts(1)

        @block.tensor
        def _(pe):
            te = nc.tensor

            def col(g, j):
                return slice(g * GC + j * P, g * GC + (j + 1) * P)

            def transpose4(key, src, i=0):
                dst = bank_free(key, i)
                for j in range(4):
                    ins = te.transpose(dst[:, j * P:(j + 1) * P], src[:, j * P:(j + 1) * P], ident[:, :])
                made(ins, key)

            def xt(t, k, g, src, i=0, ki=0):
                pe.wait_ge(xn_ready, ln_no(k, g // 2) + ki)
                transpose4(("xt", t, g), gsl(src, g), i)

            def xt_in(t, g, i=0):
                b, n, per = use[("xt", t, g)]
                pe.wait_ge(psum_free[b], n + 1 + i * per if per else n + 1)

            pe.wait_ge(tab_in, 5 * 16)
            pe.wait_ge(tab_lhs_ready, 1)
            for n, (lhs, rhs, rows) in enumerate(((mtT[:, 0:P], tokW, P), (mtT[:, P:250], tokW, 122),
                                                  (ppR[:, :], ppW, 10))):
                dst = bank_free(("table", n))
                made(te.matmul(dst[0:rows, 0:D], lhs, rhs[:, :], start=True, stop=True), ("table", n))
            pe.wait_ge(b1_in, 32)
            dst = bank_free(("b1", 0))
            for e in range(E):
                for hc in range(2):
                    c = e * HID + hc * P
                    ins = te.matmul(dst[:, 2 * e + hc:2 * e + hc + 1], w1all[:, c:c + P], blnT[:, e:e + 1], start=True,
                                    stop=True)
            made(ins, ("b1", 0))
            pe.wait_ge(tables_ready, 1)
            pe.wait_ge(ident_ready, 1)
            for g in range(G):
                pe.wait_ge(onehot_ready, g + 1)
                dst = bank_free(("embed", g))
                for j in range(4):
                    for h in range(2):
                        c = (2 * h + j // 2) * S + (j % 2) * P
                        o = (2 * j + h) * D
                        for n, rows in enumerate((P, 122, 10)):
                            for part in range(3):
                                ins = te.matmul(dst[:, o:o + D], onehot[0:rows, g % 2, n, c:c + P],
                                                tabs[0:rows, n, part, :], start=(n == 0 and part == 0),
                                                stop=(n == 2 and part == 2))
                made(ins, ("embed", g))
            for g in range(G):
                xt(0, 0, g, Xs)
            pe.wait_ge(enc_in, 12 * 16)
            for g in range(G):
                xt_in(0, g)
                for h in range(2):
                    dst = bank_free(("enc1", g, h))
                    made(te.matmul(dst[:, :], w_enc1[:, h, :], gsl(XT, g), start=True, stop=True), ("enc1", g, h))
                for kind in range(2):
                    for h in range(2):
                        key = ("enc2", g, kind, h)
                        dst = bank_free(key)
                        b, n, _ = use[("enc1", g, h)]
                        pe.wait_ge(psum_free[b], n + 1)
                        made(te.matmul(dst[:, :], w_enc2[:, kind, :], Gk[:, g % 2, h, :], start=True, stop=True), key)
            for g in range(G):
                dst = bank_free(("v0", g))
                for j in range(4):
                    ins = te.matmul(dst[:, j * P:(j + 1) * P], XT[:, col(g, j)], bd0[:, 0, :], start=True, stop=True)
                made(ins, ("v0", g))
                pe.wait_ge(cs_ready, g + 1)
                for h in range(2):
                    for jb in range(2):
                        key = ("score", g, h, jb)
                        dst = bank_free(key)
                        kc = h * GC + jb * S
                        qc = (2 + h) * GC + jb * S
                        te.matmul(dst[:, 0:S], Ph[:, g, kc:kc + P], Ph[:, g, qc:qc + S], start=True, stop=True)
                        made(te.matmul(dst[:, S:S + P], Ph[:, g, kc + P:kc + S], Ph[:, g, qc + P:qc + S],
                                       start=True, stop=True), key)
                dst = bank_free(("ret", g))
                pe.wait_ge(psum_free[g % 2], use[("v0", g)][1] + 1)
                for h in range(2):
                    for jb in range(2):
                        key = ("score", g, h, jb)
                        b, n, _ = use[key]
                        pe.wait_ge(psum_free[b], n + 1)
                        sc = Sc[:, g % 2, 2 * h + jb, :]
                        o = (4 * jb + h) * D
                        v0 = Vt[:, g, o:o + D]
                        v1 = Vt[:, g, o + 2 * D:o + 3 * D]
                        te.matmul(dst[:, o:o + D], sc[:, 0:P], v0, start=True, stop=True)
                        te.matmul(dst[:, o + 2 * D:o + 3 * D], sc[:, P:S], v0, start=True, stop=False)
                        ins = te.matmul(dst[:, o + 2 * D:o + 3 * D], sc[:, S:S + P], v1, start=False, stop=True)
                made(ins, ("ret", g))
            for g in range(G):
                xt(1, 1, g, Xn)
            for g in range(G):
                xt_in(1, g)
                dst = bank_free(("o0", g))
                for j in range(4):
                    ins = te.matmul(dst[:, j * P:(j + 1) * P], XT[:, col(g, j)], bd0[:, 1, :], start=True, stop=True)
                made(ins, ("o0", g))

            def moe(m):
                for g in range(G):
                    if m == 0:
                        xt(2, 2, g, Xs)
                    else:
                        xt(12, 13, g, Xn)
                for g in range(G):
                    xt_in(2 if m == 0 else 12, g)
                    dst = bank_free(("gate", m, g))
                    for j in range(4):
                        ins = te.matmul(dst[:, j * 2 * E:(j + 1) * 2 * E], XT[:, col(g, j)], bdg[:, m, :],
                                        start=True, stop=True)
                    made(ins, ("gate", m, g))
                pe.wait_ge(consts_ready, 1)
                for g in range(G):
                    pe.wait_ge(split_ready, 2 * m + g // 2 + 1)
                    for k in range(2):
                        key = ("xs", m, g, k)
                        dst = bank_free(key)[:, :].bitcast(BF16)
                        for h in range(2):
                            for j in range(4):
                                o = h * GC + j * P
                                src = X3[:, g * 8 + 2 * j + h, k:k + 2, :].rearrange("p n d -> p (n d)")
                                ins = te.transpose(dst[:, o:o + P], src, identb[:, :])
                        made(ins, key)
                    pe.wait_ge(comb_ready, 2 * m + g // 2 + 1)
                    key = ("ct", m, g)
                    dst = bank_free(key)[:, :].bitcast(BF16)
                    for j in range(4):
                        src = comb3[:, 4 * g + j, :, :].rearrange("p n c -> p (n c)")
                        ins = te.transpose(dst[0:48, j * P:(j + 1) * P], src, identb[:, :])
                    made(ins, key)
                for g in range(G):
                    for key in (("xs", m, g, 0), ("xs", m, g, 1), ("ct", m, g)):
                        b, c, _ = use[key]
                        pe.wait_ge(psum_free[b], c + 1)

                def up(s, g, i):
                    if g == 0:
                        pe.wait_ge(w3_ready, E * m + s + 1 + 2 * i)
                    for hc in range(2):
                        hcs = slice(hc * P, (hc + 1) * P)
                        for h in range(2):
                            key = ("up", m, s, g, hc, h)
                            dst = bank_free(key, i)
                            c = slice(g * UC + h * GC, g * UC + (h + 1) * GC)
                            te.matmul(dst[:, :], w3[:, s, 0, hcs], Xs2[:, 0, c], start=True, stop=False)
                            te.matmul(dst[:, :], w3[:, s, 1, hcs], Xs2[:, 0, c], start=False, stop=False)
                            made(te.matmul(dst[:, :], w3[:, s, 2, hcs], Xs2[:, 1, c], start=False, stop=True), key)
                    key = ("wb", m, s, g)
                    dst = bank_free(key, i)
                    made(te.matmul(dst[:, :], selcur[:, s, :], CT[:, g * GC:(g + 1) * GC], start=True, stop=True), key)

                def down(s, g, i):
                    if g == 0:
                        pe.wait_ge(pack_in[m][s], 16 + 16 * i)
                    key = ("down", m, s, g)
                    dst = bank_free(key, i)
                    for hc in range(2):
                        for h in range(2):
                            b, n, per = use[("up", m, s, g, hc, h)]
                            pe.wait_ge(psum_free[b], n + 1 + i * per)
                    for hc in range(2):
                        for h in range(2):
                            ins = te.matmul(dst[h * D:(h + 1) * D, :], pack[:, s, HID + hc * D:HID + (hc + 1) * D],
                                            Hd[:, (4 * s + g) % 2, hc, h, :], start=(hc == 0), stop=(hc == 1))
                    made(ins, key)

                def pair(i, last):
                    for n in range(8):
                        if n < 7:
                            up((n + 1) // 4, (n + 1) % 4, i)
                        elif not last:
                            up(0, 0, i + 1)
                        down(n // 4, n % 4, i)

                up(0, 0, 0)
                with pe.Fori(0, E // 2 - 1) as i:
                    pair(i, False)
                pair(E // 2 - 1, True)
                for g in range(G):
                    pe.wait_ge(acc_done, E * G * m + 28 + g + 1)
                    transpose4(("at", m, g), gsl(XT, g))

            moe(0)

            pe.wait_ge(attn_w_in, 32)
            with pe.Fori(0, LAYERS) as i:
                def t_attn(g):
                    xt("attn", 5, g, Xn, i, 4 * i)

                def project(g):
                    if g == 0:
                        pe.wait_ge(attn_w_in, 32 + 32 * i)
                    xt_in("attn", g, i)
                    dst = bank_free(("k", g), i)
                    made(te.matmul(dst[:, :], bd1[:, 1, :], gsl(XT, g), start=True, stop=True), ("k", g))
                    for what, w in (("q", 0), ("v", 2)):
                        dst = bank_free((what, g), i)
                        for j in range(4):
                            ins = te.matmul(dst[:, j * P:(j + 1) * P], XT[:, col(g, j)], bd1[:, w, :],
                                            start=True, stop=True)
                        made(ins, (what, g))

                def sbuf_has(key):
                    b, n, per = use[key]
                    pe.wait_ge(psum_free[b], n + 1 + i * per)

                def k_turn(g):
                    sbuf_has(("k", g))
                    transpose4(("kt", g), Ke[:, g, :], i)

                def q_turn(g):
                    pe.wait_ge(qn_ready, 4 * i + g + 1)
                    transpose4(("qt", g), Qe[:, g, :], i)

                def context(g):
                    sbuf_has(("kt", g))
                    sbuf_has(("v", g))
                    dst = bank_free(("ctx", g), i)
                    for jb in range(2):
                        for jj in range(2):
                            c = slice((2 * jb + jj) * P, (2 * jb + jj + 1) * P)
                            ins = te.matmul(dst[:, jb * P:(jb + 1) * P], Vt[:, g, c], Kt[:, g % 2, c],
                                            start=(jj == 0), stop=(jj == 1))
                    made(ins, ("ctx", g))

                def mix(g):
                    sbuf_has(("ctx", g))
                    dst = bank_free(("m", g), i)
                    for jb in range(2):
                        ins = te.matmul(dst[:, jb * P:(jb + 1) * P], Cm[:, g % 2, jb, :], bd1[:, 3, :], start=True,
                                        stop=True)
                    made(ins, ("m", g))

                def attend(g):
                    sbuf_has(("m", g))
                    sbuf_has(("qt", g))
                    dst = bank_free(("o", g), i)
                    for j in range(4):
                        ins = te.matmul(dst[:, j * P:(j + 1) * P], Qf[:, g % 2, j * P:(j + 1) * P],
                                        Mm[:, g % 2, j // 2, :], start=True, stop=True)
                    made(ins, ("o", g))

                t_attn(0)
                t_attn(1)
                project(0)
                project(1)
                t_attn(2)
                t_attn(3)
                k_turn(0)
                project(2)
                context(0)
                q_turn(0)
                k_turn(1)
                project(3)
                mix(0)
                context(1)
                q_turn(1)
                k_turn(2)
                attend(0)
                mix(1)
                context(2)
                q_turn(2)
                k_turn(3)
                attend(1)
                mix(2)
                context(3)
                q_turn(3)
                attend(2)
                mix(3)
                attend(3)

                def f_up(g):
                    if g == 0:
                        pe.wait_ge(ff_w_in, 48 + 48 * i)
                    xt_in("ffn", g, i)
                    for hc in range(2):
                        dst = [bank_free(("fup", g, hc, h), i) for h in range(2)]
                        for h in range(2):
                            c = h * HID + hc * P
                            made(te.matmul(dst[h][:, :], ff[:, c:c + P], gsl(XT, g), start=True, stop=True),
                                 ("fup", g, hc, h))

                def f_down(g):
                    dst = bank_free(("fdown", g), i)
                    for hc in range(2):
                        for h in range(2):
                            sbuf_has(("fup", g, hc, h))
                    for j in range(4):
                        for h in range(2):
                            o = (2 * j + h) * D
                            for hc in range(2):
                                ins = te.matmul(dst[:, o:o + D], Hd[:, g % 2, hc, h, j * P:(j + 1) * P],
                                                ff[:, 2 * HID + hc * D:2 * HID + (hc + 1) * D], start=(hc == 0),
                                                stop=(hc == 1))
                    made(ins, ("fdown", g))

                xt("ffn", 6, 0, Xn, i, 4 * i)
                xt("ffn", 6, 1, Xn, i, 4 * i)
                f_up(0)
                f_up(1)
                f_down(0)
                f_down(1)
                xt("ffn", 6, 2, Xn, i, 4 * i)
                xt("ffn", 6, 3, Xn, i, 4 * i)
                f_up(2)
                f_up(3)
                f_down(2)
                f_down(3)
            moe(1)


VEC_DMAS = 10 + 4 + 4 + 1
L1_DMAS = 4
L1_STEPS = 80


def kernel(**inputs):
    import numpy as np
    import concourse.bacc as bacc
    from concourse.bass_utils import run_bass_kernel_spmd

    n = {k: np.asarray(v) for k, v in inputs.items()}

    def cat(*xs, axis=-1):
        return np.concatenate(xs, axis=axis)

    def pack(w1, w2, *more):
        e = w1.shape[0]
        cols = [cat(w1, w1, axis=1), w2.reshape(e, 2, P, D).transpose(0, 2, 1, 3).reshape(e, P, 2 * D)]
        cols += [cat(v, v)[:, :, None] for v in more]
        return cat(*cols)

    t = "L0_attn_"
    l1 = "L1_attn_"
    arrays = {
        "x": n["x"].reshape(-1), "itok": n["itok_BS_0_63"].reshape(-1),
        "move_tableT": n["L0_tok_move_table"].T, "pp_tableT": n["L0_tok_pp_table"].T,
        "tok_WT": n["L0_tok_W"].T, "tok_b": n["L0_tok_b"],
        "enc1": cat(n[t + "Wk1"], n[t + "Wq1"]),
        "enc2": np.stack([cat(n[t + "Wk2"], n[t + "Wk2"]), cat(n[t + "Wq2"], n[t + "Wq2"])]),
        "Wv": n[t + "Wv"], "Wo": n[t + "Wo"],
        "b_enc1": np.stack([n[t + "bk1"], n[t + "bq1"]])[:, :, None],
        "b_enc2": np.stack([n[t + "bk2"], n[t + "bq2"]])[:, :, None],
        "ln0": np.stack([n[t + "ln_w"], n[t + "ln_b"]])[:, :, None],
        "rows0": np.stack([n[t + "bv"], n[t + "bo"]]),
        "Wr": n["L0_ffn_Wr"], "WgT": n["L1_ffn_Wg"].T,
        "rowg": np.stack([n["L0_ffn_br"], n["L1_ffn_bg"]]),
        "b2T": np.stack([n["L0_ffn_b2"].T, n["L1_ffn_b2"].T]),
        "b1all": np.stack([n["L0_ffn_b1"], n["L1_ffn_b1"]]).reshape(2, E, 2, P).transpose(3, 0, 1, 2),
        "blnT": n["L0_ffn_ln_b"].T,
        "w1all": n["L0_ffn_W1"].transpose(1, 0, 2).reshape(D, E * HID),
        "pack0": pack(n["L0_ffn_W1"], n["L0_ffn_W2"], n["L0_ffn_ln_g"]),
        "pack1": pack(n["L1_ffn_W1"].transpose(0, 2, 1), n["L1_ffn_W2"].transpose(0, 2, 1)),
        "l1_attn": cat(n[l1 + "Wq"], n[l1 + "Wk"], n[l1 + "Wv"], n[l1 + "Wo"]),
        "l1_W1": n[l1 + "W1"], "l1_W2": n[l1 + "W2"],
        "l1_ln": np.stack([n[l1 + v] for v in ("ln1_g", "ln1_b", "ln2_g", "ln2_b")], -1).transpose(1, 0, 2),
        "l1_b1": n[l1 + "b1"].reshape(LAYERS, 2, P).transpose(2, 0, 1),
        "l1_rows": np.stack([n[l1 + "bo"], n[l1 + "b2"]], 1).reshape(-1),
    }
    nc = bacc.Bacc("TRN2", target_bir_lowering=False, num_devices=1)
    launch, aps = {}, {}
    for name, v in arrays.items():
        v = np.ascontiguousarray(v)
        launch[f"in_{name}"] = v
        aps[name] = nc.dram_tensor(f"in_{name}", v.shape, mybir.dt.from_np(v.dtype), kind="ExternalInput").ap()
    out = nc.dram_tensor("out_0", (B, S, D), F32, kind="ExternalOutput").ap()
    lm_tower(nc, aps, out)
    r = run_bass_kernel_spmd(nc, [launch], core_ids=[0])
    return r.results[0]["out_0"]
```

```python
from contextlib import ExitStack

import concourse.bass as bass
from concourse import mybir

ALU = mybir.AluOpType
ACT = mybir.ActivationFunctionType
F32 = mybir.dt.float32
BF16 = mybir.dt.bfloat16
I32 = mybir.dt.int32
AX_X = mybir.AxisListType.X

P = 128
D = 64
S = 256
B = 16
G = 4
U = 2
GC = 512
UC = 1024
UT = 16
E = 8
HID = 256
LAYERS = 4
DH = 8
EPS = 1e-5
PHASES = 64
MAGIC = 0x5F1FFFF9
NEWTON_A, NEWTON_B = 0.703952253, 2.38924456
ROUND = float(3 * 2 ** 22)
VEC_DMAS = 3
L1_DMAS = 2
L1_STEPS = 88
TWO_PI = 6.283185



class PsumPlan:

    def __init__(self):
        self.count = [0] * 8
        self.at = {}

    def add(self, key, bank):
        self.at[key] = (bank, self.count[bank])
        self.count[bank] += 1


def plan_psum():
    plan = PsumPlan()
    for n in range(3):
        plan.add(("table", n), 2 + n)
    for g in range(G):
        plan.add(("embed", g), g % 2)

    def turned(t, u):
        for g in (2 * u, 2 * u + 1):
            plan.add(("xt", t, g), 6 + g % 2)

    def enc1(u):
        for g in (2 * u, 2 * u + 1):
            for h in range(2):
                plan.add(("enc1", g, h), 2 * (g % 2) + h)

    def enc2(g):
        for kind in range(2):
            for h in range(2):
                plan.add(("enc2", g, kind, h), 4 + 2 * kind + h)

    turned(0, 0)
    enc1(0)
    enc2(0)
    turned(0, 1)
    enc2(1)
    enc1(1)
    enc2(2)
    enc2(3)
    plan.add(("b1", 0), 0)
    for g in range(G):
        plan.add(("v0", g), g % 2)
        for h in range(2):
            for jb in range(2):
                plan.add(("score", g, h, jb), 2 + 2 * h + jb)
        if 1 <= g < 3:
            plan.add(("ret", g - 1), 6 + (g - 1) % 2)
    for what, g, b in (("ret", 2, 6), ("xt", 0, 0), ("xt", 1, 7), ("o0", 0, 0), ("o0", 1, 7), ("ret", 3, 1),
                       ("xt", 2, 6), ("xt", 3, 7), ("o0", 2, 0), ("o0", 3, 1)):
        plan.add(("xt", 1, g) if what == "xt" else (what, g), b)

    def prepare(m, u, banks):
        keys = [("xm", m, g) for g in (2 * u, 2 * u + 1)] + [("gate", m, u)]
        keys += [("xs", m, g, k) for g in (2 * u, 2 * u + 1) for k in range(2)] + [("ct", m, u)]
        for n, key in enumerate(keys):
            plan.add(key, banks[n % len(banks)])

    def moe(m):
        prepare(m, 0, (5, 6, 7))
        plan.at["before experts", m] = list(plan.count)
        prepare(m, 1, (7,))
        for g in range(G):
            plan.add(("at", m, g), 7 - g // 3)

    moe(0)
    plan.at["before L1"] = list(plan.count)
    moe(1)
    return plan.at


PAIRS = E // 2


class Step:
    def __init__(self, m, u, pair, n):
        self.m, self.n, self.s, self.g = m, n, n // 2, 2 * u + n % 2
        self.ring = n % 2
        self.pair = pair
        self.t = 2 * PAIRS * 4 * m + PAIRS * 4 * u + 4 * pair + n
        self.first = m == 0 and u == 0 and isinstance(pair, int) and 4 * pair + n < 2
        self.very_first = self.first and n == 0
        self.packs = 16 * (PAIRS * u + 1) + 16 * pair
        self.w3 = 2 * PAIRS * (2 * m + u) + 2 * pair + self.s + 1


JOBS = LAYERS * G
BEAT = (("kt", 1, 4, 1), ("qt", 1, 5, 1), ("fdown", 3, 2, 1), ("xa", 0, 3, 1), ("ctx", 1, 0, 1), ("k", 0, 4, 1),
        ("yt", 3, 2, 1), ("q", 0, 5, 1), ("m", 1, 0, 1), ("xf", 2, 3, 1), ("v", 0, 6, 1), ("o", 1, 0, 1),
        ("fup", 2, 7, 1), ("fup", 2, 1, 2), ("fup", 2, 3, 3), ("fup", 2, 2, 4))
PER_JOB = {what: max(n for w, _, _, n in BEAT if w == what) for what, *_ in BEAT}


class Job:
    def __init__(self, m, i=None):
        self.g = m % G
        self.layer = m // G if i is None else i + m // G
        self.n = m if i is None else G * i + m
        self.done = self.n + 1


class Beat:

    def __init__(self, t, i=None):
        self.t, self.i = t, i
        self.jobs = [Job(t - st, i) if i is not None or 0 <= t - st < JOBS else None for st in range(4)]

    def before(self, what, nth=1):
        at = [n for n, (w, _, _, k) in enumerate(BEAT) if w == what and k == nth][0]
        for back in range(1, 3 * len(BEAT)):
            name, stage, bank, k = BEAT[(at - back) % len(BEAT)]
            m = self.t - stage - (back > at) - (back > at + len(BEAT))
            if bank != BEAT[at][2] or (self.i is None and m < 0):
                continue
            n = PER_JOB[name]
            if self.i is not None:
                return name, n * G * self.i + n * m + k
            return name, n * m + k if m < JOBS else n * JOBS
        return None, 0


class Chain:

    def __init__(self, eng, sem):
        self.eng, self.sem, self.n, self.i, self.per = eng, sem, 0, None, 0

    def __call__(self, ins):
        ins.then_inc(self.sem, 1)
        self.n += 1
        return ins

    def settle(self):
        self.eng.wait_ge(self.sem, self.n if self.i is None else self.n + self.i * self.per)

    def enter(self, i, per):
        self.i, self.per, self.start = i, per, self.n

    def leave(self, trips):
        assert self.n - self.start == self.per, (self.n - self.start, self.per)
        self.n = self.start + trips * self.per
        self.i = None


def lm_tower(nc, a, out):
    use = plan_psum()
    ctx = ExitStack()
    with ctx:
        def sb(name, shape, dt=F32):
            return ctx.enter_context(nc.sbuf_tensor(name, shape, dt))

        def sem(name):
            return ctx.enter_context(nc.semaphore(name))

        ctx.enter_context(nc.allow_non_contiguous_dma("small vectors and weights, once"))

        bank = [ctx.enter_context(nc.psum_tensor(f"bank{b}", [P, GC], F32)) for b in range(8)]
        Hs = sb("Hs", [P, G * GC])
        Xs = sb("Xs", [P, G * GC])
        Xn = sb("Xn", [P, G * GC])
        Cen = sb("Cen", [P, G * GC])
        Rest = sb("Rest", [P, G * GC])
        XT = sb("XT", [P, G * GC])
        mom = sb("mom", [P, G * E, 3])
        stat = sb("stat", [P, 4, G * E])
        Ph = sb("Ph", [P, G, 4 * GC])
        tok_i = Ph[:, 0:2, :].rearrange("p a b -> p (a b)").bitcast(I32)
        pp_i = Ph[:, 2:4, :].rearrange("p a b -> p (a b)").bitcast(I32)
        onehot = sb("onehot", [P, 2, 3, UC], BF16)
        ppstep = sb("ppstep", [16, 2, UC])
        Gk = sb("Gk", [P, 2, 2, GC])
        Turn = Rest
        Sc = sb("Sc", [P, 2, 4, 384])
        Vt = sb("Vt", [P, G, GC])
        Hd = sb("Hd", [P, 2, 2, 2, GC])
        Xs2 = Ph[:, 0:2, :].rearrange("p a b -> p (a b)").bitcast(BF16).rearrange("p (k c) -> p k c", k=2)
        X3 = Ph[:, 2:4, :].rearrange("p a b -> p (a b)").bitcast(BF16)[:, 0:G * E * 3 * D].rearrange(
            "p (t n d) -> p t n d", n=3, d=D)
        w1all = Hd[0:D, :, :, :, :].rearrange("p a b c d -> p (a b c d)")[:, 0:E * HID]
        Tmp = sb("Tmp", [P, GC])
        Yt = Tmp
        Wb = sb("Wb", [P, 2, GC])
        Qe = Ph[:, 0, :].rearrange("p (n c) -> p n c", n=G)
        Ke = Ph[:, 1, :].rearrange("p (n c) -> p n c", n=G)
        Kt = Ph[:, 2, 0:UC].rearrange("p (n c) -> p n c", n=2)
        Qf = Ph[:, 2, UC:2 * UC].rearrange("p (n c) -> p n c", n=2)
        Cm = sb("Cm", [P, 2, 2, P])
        Mm = sb("Mm", [P, 2, 2, P])
        small = sb("small", [P, G, 3, D])
        ksm = sb("ksm", [P, G, 4, 2])
        route = sb("route", [P, 8, UT * E])
        rt = sb("rt", [P, 8, UT])
        comb = sb("comb", [P, 16, 16])
        combr = sb("combr", [P, 16, 16])
        comb3 = sb("comb3", [P, 16, 3, 16], BF16)
        CT = sb("CT", [P, G * GC], BF16)
        ident = sb("ident", [P, P])
        identb = sb("identb", [P, P], BF16)
        select = sb("select", [P, E, P], BF16)
        selcur = sb("selcur", [P, 2, P], BF16)
        onescol = sb("onescol", [P, 1])
        headmask = sb("headmask", [P, P])
        causal = sb("causal", [P, 384])
        iota_i = sb("iota_i", [P, 1], I32)
        iota_f = sb("iota_f", [P, 4])
        epos_i = sb("epos_i", [P, UT], I32)
        epos = sb("epos", [P, UT])
        prio_i = sb("prio_i", [P, UT * E], I32)
        prio = sb("prio", [P, UT * E])
        turn = sb("turn", [P, 8])
        mtT = sb("mtT", [P, 250])
        tokW = sb("tokW", [P, D])
        ppW = sb("ppW", [32, D])
        ppT = sb("ppT", [32, S])
        ppR = sb("ppR", [32, 10])
        tokb = sb("tokb", [16, D])
        tf = sb("tf", [P, 3, D])
        tabs = sb("tabs", [P, 3, 3, D], BF16)
        w_enc1 = sb("w_enc1", [P, 2, P])
        w_enc2 = sb("w_enc2", [P, 2, P])
        bd0 = sb("bd0", [P, 2, P])
        vecs0 = sb("vecs0", [P, 5])
        v_b1, v_b2, v_ln0 = vecs0[:, 0:1], vecs0[:, 1:3], vecs0[:, 3:5]
        rows = sb("rows", [P, 2 * D + 2 * E])
        rows0 = rows[:, 0:2 * D].rearrange("p (n d) -> p n d", n=2)
        bdg = sb("bdg", [P, 2, 2 * E])
        rowg = rows[:, 2 * D:2 * D + 2 * E].rearrange("p (n e) -> p n e", n=2)
        b2col = sb("b2col", [P, 2, E])
        b1all = sb("b1all", [P, 2, E, 2])
        b1cur = sb("b1cur", [P, 2, 2])
        blnT = sb("blnT", [D, E])
        w1e = sb("w1e", [P, 2, HID + 1])
        w2e = sb("w2e", [P, 2, P])
        wf = sb("wf", [P, 2, HID])
        w3 = sb("w3", [P, 2, 3, HID], BF16)
        bd1 = sb("bd1", [P, 4, P])
        ff = sb("ff", [P, 2 * HID + P])
        lvecs = sb("lvecs", [P, LAYERS, 6])
        lvec = sb("lvec", [P, 6])
        lrow = sb("lrow", [P, 2, D])
        rows1 = sb("rows1", [P, LAYERS, 2, D])

        psum_full = [sem(f"psum_full{b}") for b in range(8)]
        psum_free = [sem(f"psum_free{b}") for b in range(8)]
        tok_in = [sem(f"tok_in{g}") for g in range(G)]
        tab_in, enc_in, vec_in, l1_in = sem("tab_in"), sem("enc_in"), sem("vec_in"), sem("l1_in")
        qkv_in, wo_in, w1_in, w2_in = sem("qkv_in"), sem("wo_in"), sem("w1_in"), sem("w2_in")
        l1_made = {what: sem(f"{what}_made") for what in PER_JOB}
        l1_read = {what: sem(f"{what}_read") for what in PER_JOB}
        l1_means = [sem(f"l1_means{w}") for w in range(2)]
        centred = [sem(f"centred{w}") for w in range(2)]
        normed = [sem(f"normed{w}") for w in range(2)]
        biased = [sem(f"biased{w}") for w in range(2)]
        w1e_in = [[sem(f"w1e_in{m}{s}") for s in range(2)] for m in range(2)]
        w2e_in = [[sem(f"w2e_in{m}{s}") for s in range(2)] for m in range(2)]
        out_done = sem("out_done")
        zeros_ready, consts_ready, ident_ready = sem("zeros_ready"), sem("consts_ready"), sem("ident_ready")
        pool_step, dve_step, act_step = sem("pool_step"), sem("dve_step"), sem("act_step")
        iota_ready, b1all_in = sem("iota_ready"), sem("b1all_in")
        tables_ready, onehot_ready = sem("tables_ready"), sem("onehot_ready")
        tab_lhs_ready = sem("tab_lhs_ready")
        means_ready, cen_ready, xn_ready = sem("means_ready"), sem("cen_ready"), sem("xn_ready")
        frac_ready, cs_ready, hx_ready = sem("frac_ready"), sem("cs_ready"), sem("hx_ready")
        gap_ready, tanh_ready = sem("gap_ready"), sem("tanh_ready")
        w3_ready, split_ready, comb_ready = sem("w3_ready"), sem("split_ready"), sem("comb_ready")
        at_zero, b1_in = sem("at_zero"), sem("b1_in")
        up_made, up_read = sem("up_made"), sem("up_read")
        wb_made, wb_read = sem("wb_made"), sem("wb_read")
        down_made, down_read, acc_done = sem("down_made"), sem("down_read"), sem("acc_done")
        negm_ready, qe_ready, qn_ready = sem("negm_ready"), sem("qe_ready"), sem("qn_ready")

        block = ctx.enter_context(nc.Block())

        def full(eng, key):
            b, n = use[key]
            eng.wait_ge(psum_full[b], n + 1)

        def taken(eng, key):
            b, n = use[key]
            eng.wait_ge(psum_free[b], n + 1)

        def bank_free(key):
            b, n = use[key]
            if n:
                nc.tensor.wait_ge(psum_free[b], n)
            return bank[b]

        def made(ins, key):
            ins.then_inc(psum_full[use[key][0]], 1)

        def read(ins, key):
            ins.then_inc(psum_free[use[key][0]], 1)

        def ps(key):
            return bank[use[key][0]]

        def l1_bank(what, nth=1):
            return bank[[b for w, _, b, k in BEAT if w == what and k == nth][0]]

        def l1_full(eng, what, job, nth=None):
            n = PER_JOB[what]
            eng.wait_ge(l1_made[what], job.done if n == 1 else n * job.n + (nth or n))

        def l1_taken(eng, what, job):
            n = PER_JOB[what]
            eng.wait_ge(l1_read[what], n * job.n + n)

        ln_order = [(0, 0), (0, 1), (1, 0), (2, 0), (1, 1), (3, 0), (2, 1), (3, 1), (4, 0), (4, 1), (5, 0), (5, 1)]

        def ln_count(k, u):
            return ln_order.index((k, u)) + 1

        def gslice(g):
            return slice(g * GC, (g + 1) * GC)

        def gsl(t, g):
            return t[:, gslice(g)]

        def usl(t, u):
            return t[:, u * UC:(u + 1) * UC].rearrange("p (t d) -> p t d", d=D)

        def tiles(t, g):
            return gsl(t, g).rearrange("p (t d) -> p t d", d=D)

        def row(ap, n=E):
            return ap.unsqueeze(1).broadcast_to([P, n, D])

        def wide(ap, n, d=D):
            return ap.unsqueeze(2).broadcast_to([P, n, d])

        @block.sync
        def _(sp):
            sp.dma_start(mtT[:, :], a["move_tableT"]).then_inc(tab_in, 16)
            sp.dma_start(tokW[:, :], a["tok_WT"][0:P, :]).then_inc(tab_in, 16)
            sp.dma_start(ppW[:, :], a["tok_WT"][P:P + 32, :]).then_inc(tab_in, 16)
            sp.dma_start(ppT[:, :], a["pp_tableT"]).then_inc(tab_in, 16)
            sp.dma_start(tokb[0:10, :], a["tok_b"].partition_broadcast(10)).then_inc(tab_in, 16)
            for g in range(G):
                sl = slice(g * UC, (g + 1) * UC)
                sp.dma_start(tok_i[:, sl], a["x"][sl].partition_broadcast(P)).then_inc(tok_in[g], 16)
                sp.dma_start(pp_i[0:10, sl], a["itok"][sl].partition_broadcast(10)).then_inc(tok_in[g], 16)

            def experts(m, first):
                w = HID + (m == 0)

                def load(s, expert, before=None):
                    if before is not None:
                        sp.wait_ge(w3_ready, 2 * before + s + 1)
                    src = a[f"w1e{m}"][expert].rearrange("e p c -> (e p) c")
                    sp.dma_start(w1e[:, s, 0:w], src).then_inc(w1e_in[m][s], 16)
                    if before is not None:
                        sp.wait_ge(down_made, 4 * before + 2 * s + 2)
                    src = a[f"w2e{m}"][expert].rearrange("e p c -> (e p) c")
                    sp.dma_start(w2e[:, s, :], src).then_inc(w2e_in[m][s], 16)

                if first:
                    for s in range(2):
                        load(s, slice(s, s + 1), None if m == 0 else 2 * PAIRS - 1)
                    return
                with sp.Fori(0, PAIRS - 1) as i:
                    for s in range(2):
                        load(s, bass.ds(2 * i + 2 + s, 1), i + 2 * PAIRS * m)
                with sp.Fori(0, PAIRS) as i:
                    for s in range(2):
                        load(s, bass.ds(2 * i + s, 1), i + 2 * PAIRS * m + PAIRS - 1)

            def qkv_weights(src):
                for h in range(2):
                    hs = slice(h * D, (h + 1) * D)
                    sp.dma_start(bd1[hs, 0:3, hs], src.rearrange("d (w n) -> d w n", w=3)).then_inc(qkv_in, 16)

            def wo_weights(src):
                for h in range(2):
                    hs = slice(h * D, (h + 1) * D)
                    sp.dma_start(bd1[hs, 3, hs], src).then_inc(wo_in, 16)

            def w1_weights(src):
                for h in range(2):
                    sp.dma_start(ff[h * D:(h + 1) * D, h * HID:(h + 1) * HID], src).then_inc(w1_in, 16)

            def w2_weights(src):
                sp.dma_start(ff[:, 2 * HID:2 * HID + P].rearrange("p (c d) -> p c d", c=2),
                             src.rearrange("(c p) d -> p c d", c=2)).then_inc(w2_in, 16)

            sp.dma_start(w1all, a["w1all"]).then_inc(b1_in, 16)
            sp.dma_start(blnT[:, :], a["blnT"]).then_inc(b1_in, 16)
            sp.wait_ge(zeros_ready, 1)
            experts(0, True)
            experts(0, False)
            experts(1, True)
            qkv_weights(a["l1_attn"][0][:, 0:3 * D])
            wo_weights(a["l1_attn"][0][:, 3 * D:4 * D])
            w1_weights(a["l1_W1"][0])
            w2_weights(a["l1_W2"][0])
            with sp.Fori(0, LAYERS - 1) as i:
                sp.wait_ge(l1_made["v"], G * i + G)
                nxt = a["l1_attn"][bass.ds(i + 1, 1)].rearrange("l d c -> (l d) c")
                qkv_weights(nxt[:, 0:3 * D])
                sp.wait_ge(l1_made["m"], G * i + G)
                wo_weights(nxt[:, 3 * D:4 * D])
                sp.wait_ge(l1_made["fup"], 4 * G * i + 4 * G)
                w1_weights(a["l1_W1"][bass.ds(i + 1, 1)].rearrange("l d n -> (l d) n"))
                sp.wait_ge(l1_made["fdown"], G * i + G)
                w2_weights(a["l1_W2"][bass.ds(i + 1, 1)].rearrange("l d n -> (l d) n"))
            experts(1, False)
            for g in range(G):
                taken(sp, ("at", 1, g))
                for h in range(2):
                    for jb in range(2):
                        dst = out[4 * g + 2 * h + jb].rearrange("(j p) d -> p j d", p=P)
                        src = gsl(Hs, g).rearrange("p (b j k d) -> p b j k d", b=2, j=2, k=2)[:, jb, :, h, :]
                        sp.dma_start(dst, src).then_inc(out_done, 16)
            sp.wait_ge(out_done, 16 * B)

        @block.gpsimd
        def _(pool):
            step = Chain(pool, pool_step)
            gp = nc.gpsimd
            step(gp.iota(iota_i[:, :], [[0, 1]], base=0, channel_multiplier=1))
            step(gp.iota(epos_i[:, :], [[0, 4], [P, 2], [0, 2]], base=1, channel_multiplier=1))
            step(gp.iota(prio_i[:, :], [[0, UT], [-1, E]], base=E, channel_multiplier=0))
            step.settle()
            step(gp.tensor_copy(epos[:, :], epos_i[:, :]))
            step(gp.tensor_copy(prio[:, :], prio_i[:, :]))
            gp.tensor_copy(iota_f[:, 0:1], iota_i[:, :]).then_inc(iota_ready, 1)
            gp.memset(bd0[:, :, :], 0.0)
            gp.memset(bdg[:, :, :], 0.0)
            gp.memset(w_enc1[:, :, :], 0.0)
            gp.memset(w_enc2[:, :, :], 0.0)
            gp.memset(ff[:, :], 0.0)
            gp.memset(onescol[:, :], 1.0)
            gp.memset(bd1[:, :, :], 0.0).then_inc(zeros_ready, 1)
            step(gp.memset(ident[:, :], 0.0))
            step(gp.memset(select[:, :, :], 0.0))
            step(gp.memset(headmask[:, :], 1.0))
            step(gp.memset(causal[:, :], 1.0))
            step.settle()
            gp.affine_select(out=ident[:, :], in_=ident[:, :], compare_op=ALU.not_equal, fill=1.0, base=0,
                             pattern=[[-1, P]], channel_multiplier=1).then_inc(ident_ready, 1)
            hm = headmask[:, :].rearrange("p (b c) -> p b c", c=DH)
            step(gp.affine_select(out=hm, in_=hm, compare_op=ALU.is_ge, fill=0.0, base=0,
                                  pattern=[[-DH, P // DH], [0, DH]], channel_multiplier=1))
            step.settle()
            step(gp.affine_select(out=hm, in_=hm, compare_op=ALU.is_ge, fill=0.0, base=DH - 1,
                                  pattern=[[DH, P // DH], [0, DH]], channel_multiplier=-1))
            for c in (0, 2):
                tri = causal[:, c * P:(c + 1) * P]
                step(gp.affine_select(out=tri, in_=tri, compare_op=ALU.is_ge, fill=0.0, base=0,
                                      pattern=[[1, P]], channel_multiplier=-1))
            gp.memset(comb3[:, :, :, :], 0.0)
            gp.memset(CT[:, :], 0.0)
            pool.wait_ge(ident_ready, 1)
            gp.tensor_copy(identb[:, :], ident[:, :]).then_inc(consts_ready, 1)
            for part in range(3):
                sel = select[:, :, :].rearrange("p e (h d) -> p e h d", h=2)
                step(gp.affine_select(out=sel, in_=sel, compare_op=ALU.not_equal, fill=1.0, base=-16 * part,
                                      pattern=[[-1, E], [-E, 2], [0, D]], channel_multiplier=1))
                step.settle()

            def centre(k, u, src):
                pool.wait_ge(means_ready, ln_count(k, u))
                gp.tensor_tensor(usl(Cen, u), usl(src, u), wide(mom[:, u * UT:(u + 1) * UT, 1], UT),
                                 ALU.subtract).then_inc(cen_ready, 1)

            centre(0, 0, Hs)
            centre(0, 1, Hs)
            pool.wait_ge(vec_in, VEC_DMAS * 16)
            for u in range(U):
                pool.wait_ge(xn_ready, ln_count(0, u))
                step(gp.tensor_tensor(usl(Hs, u), usl(Hs, u), usl(Xs, u), ALU.add))
                step.settle()
                gp.tensor_tensor(usl(Hs, u), usl(Hs, u), row(rows0[:, 1, :], UT), ALU.add).then_inc(hx_ready, 1)

            def weights(m, s, pair, expert, used):
                pool.wait_ge(w1e_in[m][s], 16 + 16 * pair)
                if used:
                    pool.wait_ge(up_read, 16 * (2 * PAIRS * m + pair - 1) + 8 * s + 8)
                    pool.wait_ge(wb_made, 4 * (2 * PAIRS * m + pair - 1) + 2 * s + 2)
                gcol = w1e[:, s, HID:HID + 1] if m == 0 else onescol[:, :]
                wide_g = gcol.broadcast_to([P, HID])
                step(gp.tensor_tensor(wf[:, 0, :], w1e[:, s, 0:HID], wide_g, ALU.mult))
                e = bass.ds(expert, 1)
                step(gp.tensor_copy(b1cur[:, s, :], b1all[:, m, e, :].rearrange("p e c -> p (e c)")))
                step(gp.tensor_copy(selcur[:, s, :], select[:, e, :].rearrange("p e c -> p (e c)")))
                step(gp.tensor_tensor(w3[:, s, 0, :], w1e[:, s, 0:HID], wide_g, ALU.mult))
                step.settle()
                step(gp.tensor_tensor(w3[D:P, s, 2, :], w1e[D:P, s, 0:HID],
                                      (w1e[D:P, s, HID:HID + 1] if m == 0 else onescol[D:P, :]).broadcast_to(
                                          [D, HID]), ALU.mult))
                step.settle()
                step(gp.tensor_tensor(wf[:, 1, :], wf[:, 0, :], w3[:, s, 0, :], ALU.subtract))
                step(gp.tensor_tensor(w3[:, s, 1, :], wf[:, 0, :], w3[:, s, 0, :], ALU.subtract))
                step.settle()
                gp.tensor_tensor(w3[0:D, s, 2, :], wf[0:D, 1, :], w3[0:D, s, 1, :],
                                 ALU.subtract).then_inc(w3_ready, 1)
                pool.wait_ge(w3_ready, 4 * PAIRS * m + 2 * pair + s + 1)

            def moe_weights(m):
                def zero_sums(u):
                    for g in (2 * u, 2 * u + 1):
                        full(pool, ("gate", m, u))
                        gp.memset(gsl(XT, g), 0.0).then_inc(at_zero, 1)

                if m == 1:
                    centre(5, 0, Hs)
                else:
                    taken(pool, ("b1", 0))
                    for s in range(2):
                        weights(m, s, 0, s, False)
                    centre(1, 0, Xn)
                    centre(2, 0, Hs)
                    centre(1, 1, Xn)
                    centre(3, 0, Xs)
                    centre(2, 1, Hs)
                zero_sums(0)
                if m == 0:
                    centre(3, 1, Xs)
                else:
                    centre(5, 1, Hs)
                with pool.Fori(0, PAIRS - 1) as i:
                    step.enter(i, 2 * 7)
                    for s in range(2):
                        weights(m, s, i + 1, 2 * i + 2 + s, True)
                    step.leave(PAIRS - 1)
                zero_sums(1)
                with pool.Fori(0, PAIRS) as i:
                    step.enter(i, 2 * 7)
                    for s in range(2):
                        weights(m, s, i + PAIRS, 2 * i + s, True)
                    step.leave(PAIRS)

            moe_weights(0)
            pool.wait_ge(l1_in, L1_DMAS * 16)

            def new_row(w, layer):
                step(gp.tensor_copy(lrow[:, w, :],
                                    rows1[:, bass.ds(layer, 1), w, :].rearrange("p l d -> p (l d)")))

            def centre_and_add(w, n, g, row_used=None):
                pool.wait_ge(l1_means[w], n + 1)
                gp.tensor_tensor(tiles(Cen, g), tiles(Xs, g), wide(mom[:, g * E:(g + 1) * E, 1], E),
                                 ALU.subtract).then_inc(centred[w], 1)
                step.settle()
                pool.wait_ge(centred[w], n + 1)
                if row_used is not None:
                    pool.wait_ge(biased[1 - w], row_used)
                gp.tensor_tensor(tiles(Xs, g), tiles(Xs, g), row(lrow[:, w, :], E), ALU.add).then_inc(biased[w], 1)

            new_row(0, 0)
            new_row(1, 0)
            for u in range(U):
                if u == 1:
                    centre(4, 1, Hs)
                for g in (2 * u, 2 * u + 1):
                    centre_and_add(0, g, g)
            centre_and_add(1, 0, 0, G)
            weights(1, 0, 0, 0, True)
            centre_and_add(1, 1, 1)
            weights(1, 1, 0, 1, True)
            with pool.Fori(0, LAYERS - 1) as i:
                step.enter(i, 2)
                for k in range(4):
                    attn, feed = Job(k + G, i), Job(k + 2, i)
                    if k == 0:
                        new_row(0, i + 1)
                    centre_and_add(0, attn.n, attn.g, feed.n if k == 2 else None)
                    if k == 2:
                        new_row(1, i + 1)
                    centre_and_add(1, feed.n, feed.g, attn.done if k == 3 else None)
                step.leave(LAYERS - 1)
            for n in (JOBS - 2, JOBS - 1):
                centre_and_add(1, n, n % G)
            moe_weights(1)

        @block.scalar
        def _(act):
            ac = nc.scalar
            step = Chain(act, act_step)

            act.dma_start(b1all[:, :, :, :], a["b1all"]).then_inc(b1all_in, 16)
            act.wait_ge(zeros_ready, 1)
            for h in range(2):
                hs = slice(h * D, (h + 1) * D)
                act.dma_start(w_enc1[hs, h, :], a["enc1"]).then_inc(enc_in, 16)
                act.dma_start(w_enc2[hs, h, :], a["enc2"][h]).then_inc(enc_in, 16)
                act.dma_start(bd0[hs, :, hs], a["Wvo"]).then_inc(enc_in, 16)
                act.dma_start(bdg[hs, :, h * E:(h + 1) * E], a["gates"]).then_inc(enc_in, 16)
            act.dma_start(vecs0[:, :], a["vecs0"]).then_inc(vec_in, 16)
            act.dma_start(rows[:, :], a["rows"].partition_broadcast(P)).then_inc(vec_in, 16)
            act.dma_start(b2col[:, :, :], a["b2T"]).then_inc(vec_in, 16)
            act.dma_start(lvecs[:, :, :], a["l1_vecs"]).then_inc(l1_in, 16)
            act.dma_start(rows1[:, :, :, :].rearrange("p l w d -> p (l w d)"),
                          a["l1_rows"].partition_broadcast(P)).then_inc(l1_in, 16)

            def xt_out(t, g):
                key = ("xt", t, g)
                full(act, key)
                if t == 0:
                    read(ac.copy(gsl(XT, g), ps(key)[:, :]), key)
                else:
                    read(ac.activation(gsl(XT, g), ps(key)[:, :], ACT.Identity, scale=v_ln0[:, 0:1],
                                       bias=v_ln0[:, 1:2]), key)

            for g in range(G):
                full(act, ("embed", g))
                read(ac.copy(gsl(Hs, g), ps(("embed", g))[:, :]), ("embed", g))

            def gelus(u):
                for g in (2 * u, 2 * u + 1):
                    for h in range(2):
                        full(act, ("enc1", g, h))
                        if g >= 2 and h == 0:
                            full(act, ("enc2", g - 2, 1, 1))
                        read(ac.activation(Gk[:, g % 2, h, :], ps(("enc1", g, h))[:, :], ACT.Gelu,
                                           bias=v_b1[:, 0:1]), ("enc1", g, h))

            def tanhs(g):
                for kind in range(2):
                    for h in range(2):
                        key = ("enc2", g, kind, h)
                        full(act, key)
                        n = 2 * kind + h
                        read(ac.activation(Ph[:, g, n * GC:(n + 1) * GC], ps(key)[:, :], ACT.Tanh,
                                           bias=v_b2[:, kind:kind + 1]), key)

            xt_out(0, 0)
            xt_out(0, 1)
            act.wait_ge(vec_in, VEC_DMAS * 16)
            gelus(0)
            tanhs(0)
            xt_out(0, 2)
            xt_out(0, 3)
            tanhs(1)
            gelus(1)
            tanhs(2)
            tanhs(3)

            def retrieved(g):
                full(act, ("ret", g))
                read(ac.copy(gsl(Xn, g), ps(("ret", g))[:, :]), ("ret", g))

            for g in range(G):
                act.wait_ge(frac_ready, g + 1)
                ac.activation(Ph[:, g, :], Ph[:, g, :], ACT.Sin, scale=TWO_PI).then_inc(cs_ready, 1)
                if g >= 2:
                    retrieved(g - 2)
            retrieved(2)
            xt_out(1, 0)
            xt_out(1, 1)
            retrieved(3)
            xt_out(1, 2)
            xt_out(1, 3)

            def turned_out(m, g):
                key = ("xm", m, g)
                full(act, key)
                read(ac.copy(gsl(XT, g), ps(key)[:, :]), key)

            def tanh_gap(m, u):
                act.wait_ge(gap_ready, 2 * m + u + 1)
                ac.activation(rt[:, 6 + u, :], rt[:, 4 + u, :], ACT.Tanh, scale=0.5).then_inc(tanh_ready, 1)

            def parts_out(m, g, k):
                key = ("xs", m, g, k)
                full(act, key)
                read(ac.copy(Xs2[:, k, g * UC:(g + 1) * UC], ps(key)[:, :].bitcast(BF16)), key)

            def weights_out(m, u):
                key = ("ct", m, u)
                full(act, key)
                read(ac.copy(CT[0:48, u * UC:(u + 1) * UC], ps(key)[0:48, :].bitcast(BF16)), key)

            def prepare(m, u):
                for g in (2 * u, 2 * u + 1):
                    turned_out(m, g)
                for g in (2 * u, 2 * u + 1):
                    for k in range(2):
                        parts_out(m, g, k)
                tanh_gap(m, u)
                weights_out(m, u)

            def experts(m):
                func = ACT.Gelu if m == 0 else ACT.Relu

                def hidden(st):
                    if st.n % 2 == 0:
                        act.wait_ge(w3_ready, st.w3)
                    for k in range(4):
                        act.wait_ge(up_made, 4 * st.t + k + 1)
                        ac.activation(Hd[:, st.ring, k // 2, k % 2, :], bank[k][:, :], func,
                                      bias=b1cur[:, st.s, k // 2:k // 2 + 1]).then_inc(up_read, 1)
                    if not st.first:
                        act.wait_ge(down_read, st.t - 1)
                    act.wait_ge(wb_made, st.t + 1)
                    ac.copy(Wb[:, st.ring, :], bank[6][:, :]).then_inc(wb_read, 1)

                beside = {1: (turned_out, m, 2), 2: (turned_out, m, 3), 4: (parts_out, m, 2, 0),
                          5: (parts_out, m, 2, 1), 6: (parts_out, m, 3, 0), 7: (parts_out, m, 3, 1)}
                for n in range(8):
                    hidden(Step(m, 0, n // 4, n % 4))
                    if n in beside:
                        what, *args = beside[n]
                        what(*args)
                    if n == 6:
                        tanh_gap(m, 1)
                weights_out(m, 1)
                for u, first in ((0, 2), (1, 0)):
                    with act.Fori(0, PAIRS - first) as i:
                        for n in range(4):
                            hidden(Step(m, u, i + first, n))

            prepare(0, 0)
            experts(0)
            act.wait_ge(l1_in, L1_DMAS * 16)
            scale = float(DH) ** -0.25

            def vec(n):
                return lvec[:, n:n + 1]

            def new_vecs(lo, hi, layer):
                step(ac.copy(lvec[:, lo:hi], lvecs[:, bass.ds(layer, 1), lo:hi].rearrange("p l o -> p (l o)")))
                step.settle()

            def beat(bt):
                proj, att, up, down = bt.jobs

                def copy_out(what, job, dst):
                    l1_full(act, what, job)
                    ac.copy(dst, l1_bank(what)[:, :]).then_inc(l1_read[what], 1)

                def xt_out_g(what, job, n):
                    l1_full(act, what, job)
                    ac.activation(gsl(XT, job.g), l1_bank(what)[:, :], ACT.Identity, scale=vec(n),
                                  bias=vec(n + 1)).then_inc(l1_read[what], 1)

                def hidden(job):
                    for nth in range(1, 5):
                        l1_full(act, "fup", job, nth)
                        hc, h = (nth - 1) // 2, (nth - 1) % 2
                        ac.activation(Hd[:, job.g % 2, hc, h, :], l1_bank("fup", nth)[:, :], ACT.Gelu,
                                      bias=vec(4 + hc)).then_inc(l1_read["fup"], 1)

                def kexp(job):
                    g = job.g
                    act.wait_ge(negm_ready, job.done)
                    for jb in range(2):
                        c = slice(jb * S, (jb + 1) * S)
                        ins = ac.activation(Ke[:, g, c], l1_bank("k")[:, c], ACT.Exp, scale=scale,
                                            bias=ksm[:, g, 1, jb:jb + 1], accum_out=ksm[:, g, 2, jb:jb + 1])
                    ins.then_inc(l1_read["k"], 1)

                def qexp(job):
                    l1_taken(act, "q", job)
                    ac.activation(Qe[:, job.g, :], Qe[:, job.g, :], ACT.Exp, scale=scale).then_inc(qe_ready, 1)

                if att:
                    copy_out("kt", att, Kt[:, att.g % 2, :])
                    copy_out("qt", att, Qf[:, att.g % 2, :])
                if down:
                    copy_out("fdown", down, Yt[:, :])
                if proj:
                    if proj.g == 0 and bt.t > 0:
                        act.wait_ge(l1_read["xa"], proj.n)
                        new_vecs(0, 2, proj.layer)
                    xt_out_g("xa", proj, 0)
                    kexp(proj)
                if up:
                    if up.g == 0 and bt.t > 2:
                        act.wait_ge(l1_read["fup"], 4 * up.n)
                        new_vecs(2, 6, up.layer)
                    xt_out_g("xf", up, 2)
                if proj:
                    copy_out("v", proj, Vt[:, proj.g, :])
                    qexp(proj)
                if up:
                    hidden(up)

            new_vecs(0, 2, 0)
            new_vecs(2, 6, 0)
            for t in range(3):
                beat(Beat(t))
            with act.Fori(0, LAYERS - 1) as i:
                step.enter(i, 2)
                for k in range(4):
                    beat(Beat(3 + k, i))
                step.leave(LAYERS - 1)
            for t in range(JOBS - 1, JOBS + 3):
                beat(Beat(t))
                if t == JOBS + 1:
                    for g in (0, 1):
                        turned_out(1, g)
                    for k in range(2):
                        parts_out(1, 0, k)
            tanh_gap(1, 0)
            for k in range(2):
                parts_out(1, 1, k)
            weights_out(1, 0)
            experts(1)

        @block.vector
        def _(dve):
            step = Chain(dve, dve_step)
            ve = nc.vector

            dve.wait_ge(tab_in, 5 * 16)
            step(ve.tensor_scalar(mtT[:, :], mtT[:, :], 0.0, None, ALU.max))
            step(ve.tensor_copy(ppR[:, 0:9], ppT[:, 0:249:31]))
            ve.tensor_copy(ppR[:, 9:10], ppT[:, 255:256]).then_inc(tab_lhs_ready, 1)
            dve.wait_ge(iota_ready, 1)
            step(ve.tensor_scalar(iota_f[:, 1:2], iota_f[:, 0:1], 128.0, None, ALU.add))
            step(ve.tensor_scalar(iota_f[:, 2:3], iota_f[:, 0:1], -1.0, None, ALU.add))
            for n, (rows, add) in enumerate(((P, None), (122, None), (10, tokb))):
                full(dve, ("table", n))
                src = ps(("table", n))[0:rows, 0:D]
                if add is None:
                    ins = ve.tensor_copy(tf[0:rows, 0, :], src)
                else:
                    ins = ve.tensor_tensor(tf[0:rows, 0, :], src, add[0:rows, :], ALU.add)
                read(ins, ("table", n))
                dve.wait_ge(psum_free[2 + n], 1)
                step(ve.tensor_copy(tabs[0:rows, n, 0, :], tf[0:rows, 0, :]))
                step.settle()
                step(ve.tensor_tensor(tf[0:rows, 1, :], tf[0:rows, 0, :], tabs[0:rows, n, 0, :], ALU.subtract))
                step.settle()
                step(ve.tensor_copy(tabs[0:rows, n, 1, :], tf[0:rows, 1, :]))
                step.settle()
                ins = ve.tensor_tensor(tabs[0:rows, n, 2, :], tf[0:rows, 1, :], tabs[0:rows, n, 1, :], ALU.subtract)
                if n < 2:
                    step(ins)
                    step.settle()
                else:
                    ins.then_inc(tables_ready, 1)

            def one_hot(g):
                dve.wait_ge(tok_in[g], 32)
                if g >= 2:
                    full(dve, ("embed", g - 2))
                sl = slice(g * UC, (g + 1) * UC)
                step(ve.tensor_scalar(onehot[:, g % 2, 0, :], tok_i[:, sl], iota_f[:, 0:1], None, ALU.is_equal))
                step(ve.tensor_scalar(onehot[0:122, g % 2, 1, :], tok_i[0:122, sl], iota_f[0:122, 1:2], None,
                                      ALU.is_equal))
                step(ve.tensor_scalar(ppstep[0:10, g % 2, :], pp_i[0:10, sl], 1.0, -1.0, ALU.min, ALU.mult))
                step.settle()
                ve.tensor_scalar(onehot[0:10, g % 2, 2, :], ppstep[0:10, g % 2, :], 8.0, iota_f[0:10, 2:3],
                                 ALU.min, ALU.is_equal).then_inc(onehot_ready, 1)

            def moments(src, tile0, n, ready):
                for t in range(tile0, tile0 + n, 2):
                    pair = src[:, t * D:(t + 2) * D].rearrange("p (t d) -> p d t", t=2)
                    ins = ve.bn_stats(mom[:, t:t + 2, :].rearrange("p t s -> p (t s)"), pair)
                    if t + 2 < tile0 + n:
                        step(ins)
                ins.then_inc(ready, 1)

            def unit(t, u):
                return t[:, u * UT:(u + 1) * UT]

            def one(t, g):
                return t[:, g * E:(g + 1) * E]

            def pairs(t, odd):
                return t.rearrange("p (h g e) -> p h g e", h=2, g=2)[:, :, odd, :]

            def inv_sqrt(part, at, eps):
                v, y, z, w = (part(stat[:, k, :], at) for k in range(4))
                var = part(mom[:, :, 2], at)
                if eps is epos:
                    step(ve.scalar_tensor_tensor(v, var, 1.0 / D, epos[:, :], ALU.mult, ALU.add))
                else:
                    step(ve.tensor_scalar(v, var, 1.0 / D, eps, ALU.mult, ALU.add))
                step.settle()
                step(ve.tensor_scalar(z.bitcast(I32), v.bitcast(I32), 1, None, ALU.logical_shift_right))
                step.settle()
                step(ve.tensor_scalar(y.bitcast(I32), z.bitcast(I32), -1.0, float(MAGIC), ALU.mult, ALU.add))
                step.settle()
                step(ve.tensor_tensor(z, y, y, ALU.mult))
                step.settle()
                step(ve.tensor_tensor(z, z, v, ALU.mult))
                step.settle()
                step(ve.scalar_tensor_tensor(z, z, -NEWTON_B, y, ALU.add, ALU.mult))
                step.settle()
                step(ve.scalar_tensor_tensor(w, z, NEWTON_A * NEWTON_A, z, ALU.mult, ALU.mult))
                step(ve.tensor_scalar(y, z, -NEWTON_A * 0.375, None, ALU.mult))
                step.settle()
                step(ve.tensor_tensor(w, w, v, ALU.mult))
                step.settle()
                step(ve.scalar_tensor_tensor(w, w, -10.0 / 3, w, ALU.add, ALU.mult))
                step.settle()
                step(ve.scalar_tensor_tensor(z, w, 5.0, y, ALU.add, ALU.mult))
                step.settle()
                return z

            def layernorm(k, u, src, dst, eps=EPS, own=False):
                moments(src, u * UT, UT, means_ready)
                step.settle()
                dve.wait_ge(means_ready, ln_count(k, u))
                if own:
                    ve.tensor_tensor(usl(Cen, u), usl(src, u), wide(mom[:, u * UT:(u + 1) * UT, 1], UT),
                                     ALU.subtract).then_inc(cen_ready, 1)
                r = inv_sqrt(unit, u, eps)
                dve.wait_ge(cen_ready, ln_count(k, u))
                ve.tensor_tensor(usl(dst, u), usl(Cen, u), wide(r, UT), ALU.mult).then_inc(xn_ready, 1)

            def measure(g, w, n):
                moments(Xs, g * E, E, l1_means[w])
                step.settle()
                dve.wait_ge(l1_means[w], n + 1)

            def first_norms(u):
                dve.wait_ge(xn_ready, ln_count(4, u))
                for g in (2 * u, 2 * u + 1):
                    measure(g, 0, g)
                r = inv_sqrt(unit, u, EPS)
                for g in (2 * u, 2 * u + 1):
                    dve.wait_ge(centred[0], g + 1)
                    ve.tensor_tensor(tiles(Xn, g), tiles(Cen, g), wide(r[:, (g % 2) * E:(g % 2 + 1) * E], E),
                                     ALU.mult).then_inc(normed[0], 1)

            one_hot(0)
            one_hot(1)
            step(ve.tensor_scalar(turn[:, 1:2], iota_f[:, 0:1], 64.0, -64.0, ALU.is_ge, ALU.mult))
            step.settle()
            step(ve.tensor_tensor(turn[:, 2:3], iota_f[:, 0:1], turn[:, 1:2], ALU.add))
            step(ve.tensor_scalar(turn[:, 3:4], turn[:, 1:2], 1.0 / 256, 0.25, ALU.mult, ALU.add))
            step.settle()
            step(ve.tensor_scalar(turn[:, 4:5], turn[:, 2:3], 16.0, 0.5, ALU.is_ge, ALU.mult))
            step(ve.tensor_scalar(turn[:, 5:6], turn[:, 2:3], 32.0, None, ALU.is_ge))
            step(ve.tensor_scalar(turn[:, 6:7], turn[:, 2:3], 48.0, 2.0, ALU.is_ge, ALU.mult))
            step.settle()
            step(ve.tensor_tensor(turn[:, 7:8], turn[:, 4:5], turn[:, 5:6], ALU.add))
            step.settle()
            step(ve.scalar_tensor_tensor(turn[:, 0:1], turn[:, 6:7], 0.5, turn[:, 7:8], ALU.add, ALU.add))
            step(ve.tensor_scalar(epos[:, :], epos[:, :], EPS * PHASES, None, ALU.mult))
            one_hot(2)
            one_hot(3)
            for u in range(U):
                dve.wait_ge(psum_free[0], u + 1)
                dve.wait_ge(psum_free[1], u + 1)
                layernorm(0, u, Hs, Xs)

            step.settle()
            for g in range(G):
                for n in range(4):
                    taken(dve, ("enc2", g, n // 2, n % 2))
                step(ve.tensor_scalar(Ph[:, g, :], Ph[:, g, :], turn[:, 0:1], turn[:, 3:4], ALU.mult, ALU.add))
                step.settle()
                step(ve.tensor_scalar(Turn[:, :], Ph[:, g, :], ROUND, -ROUND, ALU.add, ALU.add))
                step.settle()
                ve.tensor_tensor(Ph[:, g, :], Ph[:, g, :], Turn[:, :], ALU.subtract).then_inc(frac_ready, 1)
                dve.wait_ge(frac_ready, g + 1)
            dve.wait_ge(vec_in, VEC_DMAS * 16)
            dve.wait_ge(consts_ready, 1)
            dve.wait_ge(b1all_in, 16)
            full(dve, ("b1", 0))
            b1 = b1all[:, 0, :, :].rearrange("p e c -> p (e c)")
            read(ve.tensor_tensor(b1, ps(("b1", 0))[:, 0:2 * E], b1, ALU.add), ("b1", 0))

            def mask_scores(g):
                full(dve, ("v0", g))
                read(ve.tensor_tensor(Vt[:, g, :].rearrange("p (t d) -> p t d", d=D),
                                      ps(("v0", g))[:, :].rearrange("p (t d) -> p t d", d=D),
                                      row(rows0[:, 0, :]), ALU.add), ("v0", g))
                for h in range(2):
                    for jb in range(2):
                        key = ("score", g, h, jb)
                        full(dve, key)
                        if g >= 2 and h == 0 and jb == 0:
                            full(dve, ("ret", g - 2))
                        read(ve.tensor_tensor(Sc[:, g % 2, 2 * h + jb, :], ps(key)[:, 0:384], causal[:, :],
                                              ALU.mult), key)

            def norm_retrieved(u):
                for g in (2 * u, 2 * u + 1):
                    taken(dve, ("ret", g))
                layernorm(1, u, Xn, Xn, epos)

            def attended(u):
                for g in (2 * u, 2 * u + 1):
                    full(dve, ("o0", g))
                    dve.wait_ge(hx_ready, g // 2 + 1)
                    read(ve.tensor_tensor(gsl(Hs, g), gsl(Hs, g), ps(("o0", g))[:, :], ALU.add), ("o0", g))

            for g in range(3):
                mask_scores(g)
            norm_retrieved(0)
            mask_scores(3)
            attended(0)

            lg, eq, f1, f2, t1, t2 = (route[:, n, :].rearrange("p (t e) -> p t e", e=E) for n in range(6))
            pr = prio[:, :].rearrange("p (t e) -> p t e", e=E)

            def best(scores, top, first):
                step(ve.tensor_reduce(top, scores, AX_X, ALU.max))
                step.settle()
                step(ve.tensor_tensor(eq, scores, wide(top, UT, E), ALU.is_equal))
                step.settle()
                step(ve.tensor_tensor(t1, eq, pr, ALU.mult))
                step.settle()
                step(ve.tensor_reduce(rt[:, 2, :], t1, AX_X, ALU.max))
                step.settle()
                step(ve.tensor_tensor(first, t1, wide(rt[:, 2, :], UT, E), ALU.is_equal))
                step.settle()

            def route_scores(m, u):
                key = ("gate", m, u)
                full(dve, key)
                ins = ve.tensor_tensor(lg, ps(key)[:, 0:UT * E].rearrange("p (t e) -> p t e", e=E),
                                       rowg[:, m, :].unsqueeze(1).broadcast_to([P, UT, E]), ALU.add)
                read(ins, key)
                taken(dve, key)

            def route_best():
                best(lg, rt[:, 0, :], f1)

            def route_second(u):
                step(ve.scalar_tensor_tensor(route[:, 5, :], route[:, 2, :], -3.0e38, route[:, 0, :],
                                             ALU.mult, ALU.add))
                step.settle()
                best(t2, rt[:, 1, :], f2)
                ve.tensor_tensor(rt[:, 4 + u, :], rt[:, 0, :], rt[:, 1, :], ALU.subtract).then_inc(gap_ready, 1)

            def route_weights(m, u):
                dve.wait_ge(tanh_ready, 2 * m + u + 1)
                step(ve.tensor_scalar(rt[:, 2, :], rt[:, 6 + u, :], 0.5, 0.5, ALU.mult, ALU.add))
                step(ve.tensor_scalar(rt[:, 3, :], rt[:, 6 + u, :], -0.5, 0.5, ALU.mult, ALU.add))
                step.settle()
                step(ve.tensor_tensor(t1, f1, wide(rt[:, 2, :], UT, E), ALU.mult))
                step(ve.tensor_tensor(t2, f2, wide(rt[:, 3, :], UT, E), ALU.mult))
                step.settle()
                cs = slice(8 * u, 8 * u + 8)
                step(ve.tensor_tensor(comb[:, cs, :].rearrange("p a (h e) -> p (a h) e", e=E), t1, t2, ALU.add))
                step.settle()
                step(ve.tensor_copy(comb3[:, cs, 0, :], comb[:, cs, :]))
                step.settle()
                step(ve.tensor_tensor(combr[:, cs, :], comb[:, cs, :], comb3[:, cs, 0, :], ALU.subtract))
                step.settle()
                step(ve.tensor_copy(comb3[:, cs, 1, :], combr[:, cs, :]))
                step.settle()
                ve.tensor_tensor(comb3[:, cs, 2, :], combr[:, cs, :], comb3[:, cs, 1, :],
                                 ALU.subtract).then_inc(comb_ready, 1)
                dve.wait_ge(comb_ready, 2 * m + u + 1)

            def split_unit(m, u):
                dve.wait_ge(xn_ready, ln_count(3 if m == 0 else 5, u))
                x3 = X3[:, u * UT:(u + 1) * UT, :, :]
                step(ve.tensor_copy(x3[:, :, 1, :], usl(Xn, u)))
                step.settle()
                step(ve.tensor_tensor(usl(Rest, u), usl(Xn, u), x3[:, :, 1, :], ALU.subtract))
                step.settle()
                step(ve.tensor_copy(x3[:, :, 0, :], usl(Rest, u)))
                step.settle()
                ve.tensor_tensor(x3[:, :, 2, :], usl(Rest, u), x3[:, :, 0, :], ALU.subtract).then_inc(split_ready, 1)
                dve.wait_ge(split_ready, 2 * m + u + 1)

            def weigh(st):
                dve.wait_ge(wb_read, st.t + 1)
                dve.wait_ge(down_made, st.t + 1)
                b2 = b2col[:, st.m, bass.ds(2 * st.pair + st.s, 1)]
                ve.scalar_tensor_tensor(Tmp[:, :], bank[4 + st.ring][:, :], b2, Wb[:, st.ring, :], ALU.add,
                                        ALU.mult).then_inc(down_read, 1)
                dve.wait_ge(down_read, st.t + 1)
                ve.tensor_tensor(gsl(XT, st.g), gsl(XT, st.g), Tmp[:, :], ALU.add).then_inc(acc_done, 1)
                dve.wait_ge(acc_done, st.t + 1)

            def mixed(m, g):
                key = ("at", m, g)
                full(dve, key)
                read(ve.tensor_tensor(gsl(Hs, g), gsl(Hs, g), ps(key)[:, :], ALU.add), key)

            def mixed_in(m, u):
                for g in (2 * u, 2 * u + 1):
                    taken(dve, ("at", m, g))

            def attended_in(u):
                for g in (2 * u, 2 * u + 1):
                    taken(dve, ("o0", g))

            attended_in(0)
            layernorm(2, 0, Hs, Xs)
            norm_retrieved(1)
            dve.wait_ge(xn_ready, ln_count(2, 0))
            layernorm(3, 0, Xs, Xn)
            split_unit(0, 0)
            route_scores(0, 0)
            route_best()
            route_second(0)
            route_weights(0, 0)
            attended(1)
            attended_in(1)
            layernorm(2, 1, Hs, Xs)
            dve.wait_ge(at_zero, 2)
            for n in range(8):
                weigh(Step(0, 0, n // 4, n % 4))
                if n == 0:
                    dve.wait_ge(xn_ready, ln_count(2, 1))
                    layernorm(3, 1, Xs, Xn)
                if n == 2:
                    route_scores(0, 1)
                    split_unit(0, 1)
                if n == 3:
                    route_best()
                if n == 4:
                    route_second(1)
                if n == 6:
                    route_weights(0, 1)
            with dve.Fori(0, PAIRS - 2) as i:
                for n in range(4):
                    weigh(Step(0, 0, i + 2, n))
            dve.wait_ge(at_zero, 4)
            for n in range(4):
                weigh(Step(0, 1, 0, n))
                if n in (1, 2):
                    mixed(0, n - 1)
            mixed_in(0, 0)
            layernorm(4, 0, Hs, Xs, own=True)
            with dve.Fori(0, PAIRS - 2) as i:
                for n in range(4):
                    weigh(Step(0, 1, i + 1, n))
            for n in range(4):
                weigh(Step(0, 1, PAIRS - 1, n))
                if n == 0:
                    first_norms(0)
            for g in (2, 3):
                mixed(0, g)

            mixed_in(0, 1)
            layernorm(4, 1, Hs, Xs)

            def beat(bt):
                proj, att, up, down = bt.jobs

                def keys_max(job):
                    g = job.g
                    l1_full(dve, "k", job)
                    step(ve.tensor_reduce(ksm[:, g, 0, :], l1_bank("k")[:, :].rearrange("p (b t) -> p b t", b=2),
                                          AX_X, ALU.max))
                    step.settle()
                    ve.tensor_scalar(ksm[:, g, 1, :], ksm[:, g, 0, :], -(float(DH) ** -0.25), None,
                                     ALU.mult).then_inc(negm_ready, 1)

                def queries_max(job):
                    g = job.g
                    l1_full(dve, "q", job)
                    q = l1_bank("q")[:, :].rearrange("p (n d) -> p n d", d=DH)
                    step(ve.tensor_reduce(small[:, g, 0, :], q, AX_X, ALU.max))
                    step.settle()
                    ve.tensor_tensor(Qe[:, g, :].rearrange("p (n d) -> p n d", d=DH), q,
                                     wide(small[:, g, 0, :], D, DH), ALU.subtract).then_inc(l1_read["q"], 1)

                def queries_norm(job):
                    g = job.g
                    dve.wait_ge(qe_ready, job.done)
                    q = Qe[:, g, :].rearrange("p (n d) -> p n d", d=DH)
                    step(ve.tensor_reduce(small[:, g, 1, :], q, AX_X, ALU.add))
                    step.settle()
                    step(ve.reciprocal(small[:, g, 2, :], small[:, g, 1, :]))
                    step.settle()
                    ve.tensor_tensor(q, q, wide(small[:, g, 2, :], D, DH), ALU.mult).then_inc(qn_ready, 1)

                def context_out(job):
                    l1_full(dve, "ctx", job)
                    ve.tensor_tensor(Cm[:, job.g % 2, :, :], l1_bank("ctx")[:, 0:S].rearrange(
                        "p (b n) -> p b n", b=2), headmask[:, :].unsqueeze(1).broadcast_to([P, 2, P]),
                                     ALU.mult).then_inc(l1_read["ctx"], 1)

                def mix_out(job):
                    g = job.g
                    l1_taken(dve, "k", job)
                    step(ve.reciprocal(ksm[:, g, 3, :], ksm[:, g, 2, :]))
                    step.settle()
                    l1_full(dve, "m", job)
                    for jb in range(2):
                        ins = ve.tensor_scalar(Mm[:, g % 2, jb, :], l1_bank("m")[:, jb * P:(jb + 1) * P],
                                               ksm[:, g, 3, jb:jb + 1], None, ALU.mult)
                    ins.then_inc(l1_read["m"], 1)

                def add_out(what, job, w):
                    l1_full(dve, what, job)
                    dve.wait_ge(biased[w], job.done)
                    ve.tensor_tensor(gsl(Xs, job.g), gsl(Xs, job.g), l1_bank(what)[:, :],
                                     ALU.add).then_inc(l1_read[what], 1)
                    l1_taken(dve, what, job)

                more = down and (bt.i is not None)
                if att:
                    context_out(att)
                if proj:
                    keys_max(proj)
                if down:
                    add_out("yt", down, 1)
                if att:
                    mix_out(att)
                if proj:
                    queries_max(proj)
                if more:
                    measure(down.g, 0, G + down.n)
                if att:
                    add_out("o", att, 0)
                if proj:
                    queries_norm(proj)
                if att:
                    measure(att.g, 1, att.n)
                if att:
                    if more:
                        r = inv_sqrt(pairs, att.g % 2, EPS)
                        dve.wait_ge(centred[0], G + down.done)
                        ve.tensor_tensor(tiles(Xn, down.g), tiles(Cen, down.g), wide(r[:, down.g // 2, :], E),
                                         ALU.mult).then_inc(normed[0], 1)
                        r = r[:, att.g // 2, :]
                    else:
                        r = inv_sqrt(one, att.g, EPS)
                    dve.wait_ge(centred[1], att.done)
                    ve.tensor_tensor(tiles(Xn, att.g), tiles(Cen, att.g), wide(r, E), ALU.mult).then_inc(normed[1], 1)

            def finished(g):
                step(ve.tensor_tensor(gsl(Hs, g), gsl(Hs, g), gsl(Xs, g), ALU.add))

            beat(Beat(0))
            first_norms(1)
            beat(Beat(1))
            beat(Beat(2))
            with dve.Fori(0, LAYERS - 1) as i:
                step.enter(i, L1_STEPS)
                for k in range(4):
                    beat(Beat(3 + k, i))
                step.leave(LAYERS - 1)
            for t in range(JOBS - 1, JOBS + 3):
                beat(Beat(t))
                finished(t - JOBS + 1)
                if t == JOBS:
                    step.settle()
                    layernorm(5, 0, Hs, Xn)
                if t == JOBS + 1:
                    split_unit(1, 0)
                    route_scores(1, 0)
                    route_best()
                    route_second(0)
            step.settle()
            route_weights(1, 0)
            layernorm(5, 1, Hs, Xn)

            dve.wait_ge(at_zero, 6)
            for n in range(8):
                weigh(Step(1, 0, n // 4, n % 4))
                if n == 2:
                    route_scores(1, 1)
                    split_unit(1, 1)
                if n == 3:
                    route_best()
                if n == 4:
                    route_second(1)
                if n == 6:
                    route_weights(1, 1)
            with dve.Fori(0, PAIRS - 2) as i:
                for n in range(4):
                    weigh(Step(1, 0, i + 2, n))
            dve.wait_ge(at_zero, 8)
            for n in range(4):
                weigh(Step(1, 1, 0, n))
                if n in (1, 2):
                    mixed(1, n - 1)
            with dve.Fori(0, PAIRS - 1) as i:
                for n in range(4):
                    weigh(Step(1, 1, i + 1, n))
            for g in (2, 3):
                mixed(1, g)

        @block.tensor
        def _(pe):
            te = nc.tensor

            def col(g, j):
                return slice(g * GC + j * P, g * GC + (j + 1) * P)

            def transpose4(key, src):
                dst = bank_free(key)
                for j in range(4):
                    ins = te.transpose(dst[:, j * P:(j + 1) * P], src[:, j * P:(j + 1) * P], ident[:, :])
                made(ins, key)

            def xt(t, g, src):
                pe.wait_ge(xn_ready, ln_count(t, g // 2))
                transpose4(("xt", t, g), gsl(src, g))

            pe.wait_ge(tab_in, 5 * 16)
            pe.wait_ge(tab_lhs_ready, 1)
            for n, (lhs, rhs, rows) in enumerate(((mtT[:, 0:P], tokW, P), (mtT[:, P:250], tokW, 122),
                                                  (ppR[:, :], ppW, 10))):
                dst = bank_free(("table", n))
                made(te.matmul(dst[0:rows, 0:D], lhs, rhs[:, :], start=True, stop=True), ("table", n))

            def bias_through_w1():
                pe.wait_ge(b1_in, 32)
                dst = bank_free(("b1", 0))
                for e in range(E):
                    for hc in range(2):
                        c = e * HID + hc * P
                        ins = te.matmul(dst[:, 2 * e + hc:2 * e + hc + 1], w1all[:, c:c + P], blnT[:, e:e + 1],
                                        start=True, stop=True)
                made(ins, ("b1", 0))

            pe.wait_ge(tables_ready, 1)
            pe.wait_ge(ident_ready, 1)
            for g in range(G):
                pe.wait_ge(onehot_ready, g + 1)
                dst = bank_free(("embed", g))
                for j in range(4):
                    for h in range(2):
                        c = (2 * h + j // 2) * S + (j % 2) * P
                        o = (2 * j + h) * D
                        for n, rows in enumerate((P, 122, 10)):
                            for part in range(3):
                                ins = te.matmul(dst[:, o:o + D], onehot[0:rows, g % 2, n, c:c + P],
                                                tabs[0:rows, n, part, :], start=(n == 0 and part == 0),
                                                stop=(n == 2 and part == 2))
                made(ins, ("embed", g))

            def encode1(g):
                taken(pe, ("xt", 0, g))
                for h in range(2):
                    dst = bank_free(("enc1", g, h))
                    made(te.matmul(dst[:, :], w_enc1[:, h, :], gsl(XT, g), start=True, stop=True), ("enc1", g, h))

            def encode2(g):
                for kind in range(2):
                    for h in range(2):
                        key = ("enc2", g, kind, h)
                        dst = bank_free(key)
                        taken(pe, ("enc1", g, h))
                        made(te.matmul(dst[:, :], w_enc2[:, kind, :], Gk[:, g % 2, h, :], start=True, stop=True), key)

            xt(0, 0, Xs)
            xt(0, 1, Xs)
            pe.wait_ge(enc_in, 8 * 16)
            encode1(0)
            encode1(1)
            encode2(0)
            xt(0, 2, Xs)
            xt(0, 3, Xs)
            encode2(1)
            encode1(2)
            encode1(3)
            encode2(2)
            encode2(3)
            bias_through_w1()

            def scores(g):
                dst = bank_free(("v0", g))
                for j in range(4):
                    ins = te.matmul(dst[:, j * P:(j + 1) * P], XT[:, col(g, j)], bd0[:, 0, :], start=True, stop=True)
                made(ins, ("v0", g))
                pe.wait_ge(cs_ready, g + 1)
                for h in range(2):
                    for jb in range(2):
                        key = ("score", g, h, jb)
                        dst = bank_free(key)
                        kc = h * GC + jb * S
                        qc = (2 + h) * GC + jb * S
                        te.matmul(dst[:, 0:S], Ph[:, g, kc:kc + P], Ph[:, g, qc:qc + S], start=True, stop=True)
                        made(te.matmul(dst[:, S:S + P], Ph[:, g, kc + P:kc + S], Ph[:, g, qc + P:qc + S],
                                       start=True, stop=True), key)

            def retrieve(g):
                dst = bank_free(("ret", g))
                taken(pe, ("v0", g))
                for h in range(2):
                    for jb in range(2):
                        taken(pe, ("score", g, h, jb))
                        sc = Sc[:, g % 2, 2 * h + jb, :]
                        o = (4 * jb + h) * D
                        v0 = Vt[:, g, o:o + D]
                        v1 = Vt[:, g, o + 2 * D:o + 3 * D]
                        te.matmul(dst[:, o:o + D], sc[:, 0:P], v0, start=True, stop=True)
                        te.matmul(dst[:, o + 2 * D:o + 3 * D], sc[:, P:S], v0, start=True, stop=False)
                        ins = te.matmul(dst[:, o + 2 * D:o + 3 * D], sc[:, S:S + P], v1, start=False, stop=True)
                made(ins, ("ret", g))

            for g in range(G):
                scores(g)
                if 1 <= g < 3:
                    retrieve(g - 1)
            retrieve(2)
            for u in range(U):
                for g in (2 * u, 2 * u + 1):
                    xt(1, g, Xn)
                for g in (2 * u, 2 * u + 1):
                    taken(pe, ("xt", 1, g))
                    dst = bank_free(("o0", g))
                    for j in range(4):
                        ins = te.matmul(dst[:, j * P:(j + 1) * P], XT[:, col(g, j)], bd0[:, 1, :], start=True,
                                        stop=True)
                    made(ins, ("o0", g))
                if u == 0:
                    retrieve(3)

            def turn_stream(m, g):
                pe.wait_ge(xn_ready, ln_count(2 if m == 0 else 5, g // 2))
                transpose4(("xm", m, g), gsl(Xs if m == 0 else Xn, g))

            def gate(m, u):
                key = ("gate", m, u)
                dst = bank_free(key)
                for g in (2 * u, 2 * u + 1):
                    taken(pe, ("xm", m, g))
                    for j in range(4):
                        o = ((g % 2) * 4 + j) * 2 * E
                        ins = te.matmul(dst[:, o:o + 2 * E], XT[:, col(g, j)], bdg[:, m, :], start=True, stop=True)
                made(ins, key)

            def turn_parts(m, g, k):
                pe.wait_ge(split_ready, 2 * m + g // 2 + 1)
                key = ("xs", m, g, k)
                dst = bank_free(key)[:, :].bitcast(BF16)
                for h in range(2):
                    for j in range(4):
                        o = h * GC + j * P
                        src = X3[:, g * 8 + 2 * j + h, k:k + 2, :].rearrange("p n d -> p (n d)")
                        ins = te.transpose(dst[:, o:o + P], src, identb[:, :])
                made(ins, key)

            def turn_weights(m, u):
                pe.wait_ge(comb_ready, 2 * m + u + 1)
                key = ("ct", m, u)
                dst = bank_free(key)[:, :].bitcast(BF16)
                for j in range(8):
                    src = comb3[:, 8 * u + j, :, :].rearrange("p n c -> p (n c)")
                    ins = te.transpose(dst[0:48, j * P:(j + 1) * P], src, identb[:, :])
                made(ins, key)

            def prepare(m, u):
                for g in (2 * u, 2 * u + 1):
                    turn_stream(m, g)
                gate(m, u)
                for g in (2 * u, 2 * u + 1):
                    for k in range(2):
                        turn_parts(m, g, k)
                turn_weights(m, u)

            def operands_in(m, u):
                keys = [("xs", m, g, k) for g in (2 * u, 2 * u + 1) for k in range(2)] + [("ct", m, u)]
                last = {}
                for key in keys:
                    b, n = use[key]
                    last[b] = n + 1
                for b, c in last.items():
                    pe.wait_ge(psum_free[b], c)

            def experts(m):
                def up(st):
                    if st.n % 2 == 0:
                        pe.wait_ge(w3_ready, st.w3)
                    for k in range(4):
                        hcs = slice(k // 2 * P, (k // 2 + 1) * P)
                        c = slice(st.g * UC + (k % 2) * GC, st.g * UC + (k % 2 + 1) * GC)
                        dst = bank[k]
                        if not st.very_first:
                            pe.wait_ge(up_read, 4 * st.t + k - 3)
                        te.matmul(dst[:, :], w3[:, st.s, 0, hcs], Xs2[:, 0, c], start=True, stop=False)
                        te.matmul(dst[:, :], w3[:, st.s, 1, hcs], Xs2[:, 0, c], start=False, stop=False)
                        te.matmul(dst[:, :], w3[:, st.s, 2, hcs], Xs2[:, 1, c], start=False,
                                  stop=True).then_inc(up_made, 1)
                    if not st.very_first:
                        pe.wait_ge(wb_read, st.t)
                    te.matmul(bank[6][:, :], selcur[:, st.s, :], CT[:, gslice(st.g)], start=True,
                              stop=True).then_inc(wb_made, 1)

                def down(st):
                    if st.n % 2 == 0:
                        pe.wait_ge(w2e_in[m][st.s], st.packs)
                    if not st.first:
                        pe.wait_ge(down_read, st.t - 1)
                    pe.wait_ge(up_read, 4 * st.t + 4)
                    for hc in range(2):
                        for h in range(2):
                            ins = te.matmul(bank[4 + st.ring][h * D:(h + 1) * D, :],
                                            w2e[:, st.s, hc * D:(hc + 1) * D],
                                            Hd[:, st.ring, hc, h, :], start=(hc == 0), stop=(hc == 1))
                    ins.then_inc(down_made, 1)

                def turn_back(g):
                    last = Step(m, g // 2, PAIRS - 1, 2 + g % 2)
                    pe.wait_ge(acc_done, last.t + 1)
                    transpose4(("at", m, g), gsl(XT, g))

                for b in range(7):
                    pe.wait_ge(psum_free[b], use["before experts", m][b])
                operands_in(m, 0)
                beside = {0: (turn_stream, m, 2), 1: (turn_stream, m, 3), 2: (gate, m, 1), 3: (turn_parts, m, 2, 0),
                          4: (turn_parts, m, 2, 1), 5: (turn_parts, m, 3, 0), 6: (turn_parts, m, 3, 1),
                          7: (turn_weights, m, 1)}
                up(Step(m, 0, 0, 0))
                for n in range(8):
                    if n < 7:
                        up(Step(m, 0, (n + 1) // 4, (n + 1) % 4))
                    down(Step(m, 0, n // 4, n % 4))
                    what, *args = beside[n]
                    what(*args)
                with pe.Fori(0, PAIRS - 2) as i:
                    up(Step(m, 0, i + 2, 0))
                    for n in range(4):
                        if n < 3:
                            up(Step(m, 0, i + 2, n + 1))
                        down(Step(m, 0, i + 2, n))
                operands_in(m, 1)
                up(Step(m, 1, 0, 0))
                for n in range(4):
                    up(Step(m, 1, (n + 1) // 4, (n + 1) % 4))
                    down(Step(m, 1, 0, n))
                    if n in (1, 2):
                        turn_back(n - 1)
                with pe.Fori(0, PAIRS - 2) as i:
                    for n in range(4):
                        up(Step(m, 1, i + 1 + (n + 1) // 4, (n + 1) % 4))
                        down(Step(m, 1, i + 1, n))
                for n in range(4):
                    if n < 3:
                        up(Step(m, 1, PAIRS - 1, n + 1))
                    down(Step(m, 1, PAIRS - 1, n))
                pe.wait_ge(wb_read, 8 * PAIRS * (m + 1))
                for g in (2, 3):
                    turn_back(g)
                pe.wait_ge(down_read, 8 * PAIRS * (m + 1))

            pe.wait_ge(consts_ready, 1)
            prepare(0, 0)
            experts(0)

            for b in range(8):
                pe.wait_ge(psum_free[b], use["before L1"][b])

            def beat(bt):
                proj, att, up, down = bt.jobs

                def l1_free(what, nth=1):
                    name, count = bt.before(what, nth)
                    if name is not None:
                        pe.wait_ge(l1_read[name], count)
                    return l1_bank(what, nth)

                def turn(what, src):
                    dst = l1_free(what)
                    for j in range(4):
                        ins = te.transpose(dst[:, j * P:(j + 1) * P], src[:, j * P:(j + 1) * P], ident[:, :])
                    ins.then_inc(l1_made[what], 1)

                if att:
                    l1_taken(pe, "k", att)
                    turn("kt", Ke[:, att.g, :])
                    pe.wait_ge(qn_ready, att.done)
                    turn("qt", Qe[:, att.g, :])
                if down:
                    if down.g == 0:
                        pe.wait_ge(w2_in, 16 + 16 * down.layer)
                    dst = l1_free("fdown")
                    l1_taken(pe, "fup", down)
                    for hc in range(2):
                        for h in range(2):
                            ins = te.matmul(dst[h * D:(h + 1) * D, :], ff[:, 2 * HID + hc * D:2 * HID + (hc + 1) * D],
                                            Hd[:, down.g % 2, hc, h, :], start=(hc == 0), stop=(hc == 1))
                    ins.then_inc(l1_made["fdown"], 1)
                if proj:
                    pe.wait_ge(normed[0], proj.done)
                    turn("xa", gsl(Xn, proj.g))
                if att:
                    l1_taken(pe, "kt", att)
                    l1_taken(pe, "v", att)
                    dst = l1_free("ctx")
                    for jb in range(2):
                        for jj in range(2):
                            c = slice((2 * jb + jj) * P, (2 * jb + jj + 1) * P)
                            ins = te.matmul(dst[:, jb * P:(jb + 1) * P], Vt[:, att.g, c], Kt[:, att.g % 2, c],
                                            start=(jj == 0), stop=(jj == 1))
                    ins.then_inc(l1_made["ctx"], 1)

                def project(what, w):
                    dst = l1_free(what)
                    for j in range(4):
                        ins = te.matmul(dst[:, j * P:(j + 1) * P], XT[:, col(proj.g, j)], bd1[:, w, :],
                                        start=True, stop=True)
                    ins.then_inc(l1_made[what], 1)

                if proj:
                    if proj.g == 0:
                        pe.wait_ge(qkv_in, 32 + 32 * proj.layer)
                    l1_taken(pe, "xa", proj)
                    dst = l1_free("k")
                    te.matmul(dst[:, :], bd1[:, 1, :], gsl(XT, proj.g), start=True,
                              stop=True).then_inc(l1_made["k"], 1)
                if down:
                    l1_taken(pe, "fdown", down)
                    turn("yt", Yt)
                if proj:
                    project("q", 0)
                if att:
                    if att.g == 0:
                        pe.wait_ge(wo_in, 32 + 32 * att.layer)
                    l1_taken(pe, "ctx", att)
                    dst = l1_free("m")
                    for jb in range(2):
                        ins = te.matmul(dst[:, jb * P:(jb + 1) * P], Cm[:, att.g % 2, jb, :], bd1[:, 3, :],
                                        start=True, stop=True)
                    ins.then_inc(l1_made["m"], 1)
                if up:
                    pe.wait_ge(normed[1], up.done)
                    turn("xf", gsl(Xn, up.g))
                if proj:
                    project("v", 2)
                if att:
                    l1_taken(pe, "m", att)
                    l1_taken(pe, "qt", att)
                    dst = l1_free("o")
                    for j in range(4):
                        ins = te.matmul(dst[:, j * P:(j + 1) * P], Qf[:, att.g % 2, j * P:(j + 1) * P],
                                        Mm[:, att.g % 2, j // 2, :], start=True, stop=True)
                    ins.then_inc(l1_made["o"], 1)
                if up:
                    if up.g == 0:
                        pe.wait_ge(w1_in, 32 + 32 * up.layer)
                    l1_taken(pe, "xf", up)
                    for nth in range(1, 5):
                        dst = l1_free("fup", nth)
                        hc, h = (nth - 1) // 2, (nth - 1) % 2
                        c = h * HID + hc * P
                        te.matmul(dst[:, :], ff[:, c:c + P], gsl(XT, up.g), start=True,
                                  stop=True).then_inc(l1_made["fup"], 1)

            for t in range(3):
                beat(Beat(t))
            with pe.Fori(0, LAYERS - 1) as i:
                for k in range(4):
                    beat(Beat(3 + k, i))
            for t in range(JOBS - 1, JOBS + 3):
                beat(Beat(t))
                if t == JOBS + 1:
                    pe.wait_ge(l1_read["q"], JOBS)
                    pe.wait_ge(l1_read["v"], JOBS)
                    pe.wait_ge(l1_read["fup"], 4 * JOBS - 3)
                    for g in (0, 1):
                        turn_stream(1, g)
                    gate(1, 0)
                    for k in range(2):
                        turn_parts(1, 0, k)
            for what, n in PER_JOB.items():
                pe.wait_ge(l1_read[what], n * JOBS)
            for k in range(2):
                turn_parts(1, 1, k)
            turn_weights(1, 0)
            experts(1)


def kernel(**inputs):
    import numpy as np
    import concourse.bacc as bacc
    from concourse.bass_utils import run_bass_kernel_spmd

    n = {k: np.asarray(v) for k, v in inputs.items()}

    def cat(*xs, axis=-1):
        return np.concatenate(xs, axis=axis)

    def twice(w1, *more):
        return cat(cat(w1, w1, axis=1), *(cat(v, v)[:, :, None] for v in more))

    def blocks(w2):
        e = w2.shape[0]
        return w2.reshape(e, 2, P, D).transpose(0, 2, 1, 3).reshape(e, P, 2 * D)

    t = "L0_attn_"
    l1 = "L1_attn_"
    arrays = {
        "x": n["x"].reshape(-1), "itok": n["itok_BS_0_63"].reshape(-1),
        "move_tableT": n["L0_tok_move_table"].T, "pp_tableT": n["L0_tok_pp_table"].T,
        "tok_WT": n["L0_tok_W"].T, "tok_b": n["L0_tok_b"],
        "enc1": cat(n[t + "Wk1"], n[t + "Wq1"]),
        "enc2": np.stack([cat(n[t + "Wk2"], n[t + "Wk2"]), cat(n[t + "Wq2"], n[t + "Wq2"])]),
        "Wvo": np.stack([n[t + "Wv"], n[t + "Wo"]], 1),
        "vecs0": np.stack([cat(n[t + "bk1"], n[t + "bq1"])] + [cat(n[t + v], n[t + v]) for v in (
            "bk2", "bq2", "ln_w", "ln_b")], -1),
        "rows": cat(n[t + "bv"], n[t + "bo"], n["L0_ffn_br"], n["L1_ffn_bg"]),
        "gates": np.stack([n["L0_ffn_Wr"], n["L1_ffn_Wg"].T], 1),
        "b2T": cat(*[np.stack([n["L0_ffn_b2"].T, n["L1_ffn_b2"].T], 1)] * 2, axis=0),
        "b1all": np.stack([n["L0_ffn_b1"], n["L1_ffn_b1"]]).reshape(2, E, 2, P).transpose(3, 0, 1, 2),
        "blnT": n["L0_ffn_ln_b"].T,
        "w1all": n["L0_ffn_W1"].transpose(1, 0, 2).reshape(D, E * HID),
        "w1e0": twice(n["L0_ffn_W1"], n["L0_ffn_ln_g"]), "w2e0": blocks(n["L0_ffn_W2"]),
        "w1e1": twice(n["L1_ffn_W1"].transpose(0, 2, 1)), "w2e1": blocks(n["L1_ffn_W2"].transpose(0, 2, 1)),
        "l1_attn": cat(n[l1 + "Wq"], n[l1 + "Wk"], n[l1 + "Wv"], n[l1 + "Wo"]),
        "l1_W1": n[l1 + "W1"], "l1_W2": n[l1 + "W2"],
        "l1_vecs": cat(
            cat(*[np.stack([n[l1 + v] for v in ("ln1_g", "ln1_b", "ln2_g", "ln2_b")], -1)] * 2, axis=1),
            n[l1 + "b1"].reshape(LAYERS, 2, P).transpose(0, 2, 1)).transpose(1, 0, 2),
        "l1_rows": np.stack([n[l1 + "bo"], n[l1 + "b2"]], 1).reshape(-1),
    }
    nc = bacc.Bacc("TRN2", target_bir_lowering=False, num_devices=1)
    launch, aps = {}, {}
    for name, v in arrays.items():
        v = np.ascontiguousarray(v)
        launch[f"in_{name}"] = v
        aps[name] = nc.dram_tensor(f"in_{name}", v.shape, mybir.dt.from_np(v.dtype), kind="ExternalInput").ap()
    out = nc.dram_tensor("out_0", (B, S, D), F32, kind="ExternalOutput").ap()
    lm_tower(nc, aps, out)
    r = run_bass_kernel_spmd(nc, [launch], core_ids=[0])
    return r.results[0]["out_0"]
```
